# Optimizing a Trainium2 kernel written in Bass

```python
import numpy as np
import jax
import jax.numpy as jnp

def _softmax(x, axis=-1):
    return jax.nn.softmax(x, axis=axis)

def _gelu(x):
    return jax.nn.gelu(x, approximate=True)

def _silu(x):
    return jax.nn.silu(x)

def _sigmoid(x):
    return jax.nn.sigmoid(x)

def _layernorm(x, axis=-1, eps=1e-05):
    m = jnp.mean(x, axis=axis, keepdims=True)
    v = jnp.var(x, axis=axis, keepdims=True)
    return (x - m) / jnp.sqrt(v + eps)

def _scatter_add(tgt, idx, src, axis=0):
    return tgt.at[idx].add(src)

def _segment_sum(src, seg, n):
    return jax.ops.segment_sum(src, seg, n)
kernel_name = 'mk_recurrent_d2_jaxref_r8_67088a'

def setup_inputs(seed: int=0):
    np.random.seed(seed)
    _w = jnp.asarray

    def _L0_attn_setup():
        import jax, jax.numpy as jnp
        import numpy as np
        B, T, C, H = (2, 256, 128, 16)
        HD = C // H
        key = jax.random.key(seed)
        ks = jax.random.split(key, 10)
        s = 0.02
        x = jax.random.normal(ks[0], (B, T, C), dtype=jnp.float32)
        Wq = jax.random.normal(ks[1], (C, C), dtype=jnp.float32) * s
        bq = jnp.zeros((C,), dtype=jnp.float32)
        Wk = jax.random.normal(ks[2], (C, C), dtype=jnp.float32) * s
        bk = jnp.zeros((C,), dtype=jnp.float32)
        Wv = jax.random.normal(ks[3], (C, C), dtype=jnp.float32) * s
        bv = jnp.zeros((C,), dtype=jnp.float32)
        Wp = jax.random.normal(ks[4], (C, C), dtype=jnp.float32) * s
        bp = jnp.zeros((C,), dtype=jnp.float32)
        resolve_level = jnp.float32(0.7)
        return {'x': x, 'Wq': Wq, 'bq': bq, 'Wk': Wk, 'bk': bk, 'Wv': Wv, 'bv': bv, 'Wp': Wp, 'bp': bp, 'resolve_level': resolve_level}
    _L0_attn_in = _L0_attn_setup()

    def _L0_ffn_setup():
        import jax, jax.numpy as jnp
        import numpy as np
        DIM = 128
        HIDDEN = 384
        SCALE = 1.0 / 127.0

        def _dequant(w_int, dtype):
            return w_int.astype(dtype) * jnp.asarray(SCALE, dtype)
        key = jax.random.key(seed)
        k_x, k_g, k_u, k_d = jax.random.split(key, 4)
        x = jax.random.normal(k_x, (4, 256, DIM), dtype=jnp.float32)
        w_gate = jax.random.randint(k_g, (HIDDEN, DIM), -127, 128, dtype=jnp.int32)
        w_up = jax.random.randint(k_u, (HIDDEN, DIM), -127, 128, dtype=jnp.int32)
        w_down = jax.random.randint(k_d, (DIM, HIDDEN), -127, 128, dtype=jnp.int32)
        return {'x': x, 'w_gate': w_gate, 'w_up': w_up, 'w_down': w_down}
    _L0_ffn_in = _L0_ffn_setup()

    def _L1_attn_setup():
        import jax, jax.numpy as jnp
        import numpy as np
        TRUNC_LEN = 1024

        def _get_k(ab, h_0, l):
            D = h_0.shape[0]
            num_a = ab.shape[0] - D
            N = ab.shape[1]
            L = TRUNC_LEN
            ab_p = jnp.pad(ab, ((0, 0), (1, L - N - 1 + L % 2)))
            ab_p = ab_p.at[:num_a, 0].set(1.0)
            AB = jnp.fft.rfft(ab_p, axis=-1)
            A = AB[:num_a]
            Bn = AB[num_a:]
            R = D // num_a
            A_rep = jnp.repeat(A, R, axis=0)
            K = Bn / A_rep + h_0[:, None].astype(Bn.dtype)
            k = jnp.fft.irfft(K, n=L + L % 2, axis=-1)[:, :l]
            return k
        key = jax.random.key(seed)
        k1, k2, k3 = jax.random.split(key, 3)
        B, L, D, N = (4, TRUNC_LEN, 128, 64)
        u = jax.random.normal(k1, (B, L, D), dtype=jnp.float32)
        ab = jax.random.normal(k2, (2 * D, N), dtype=jnp.float32) * 0.01
        h_0 = jax.random.normal(k3, (D,), dtype=jnp.float32)
        return {'u': u, 'ab': ab, 'h_0': h_0}
    _L1_attn_in = _L1_attn_setup()

    def _L1_ffn_setup():
        import jax, jax.numpy as jnp
        import numpy as np
        TOP_K = 2
        key = jax.random.key(seed)
        ks = jax.random.split(key, 6)
        B, T, H, E, F = (2, 256, 128, 8, 512)
        s = 0.02
        return {'hidden_states': jax.random.normal(ks[0], (B, T, H), dtype=jnp.float32), 'router_w': jax.random.normal(ks[1], (E, H), dtype=jnp.float32) * s, 'w1': jax.random.normal(ks[2], (E, F, H), dtype=jnp.float32) * s, 'b1': jax.random.normal(ks[3], (E, F), dtype=jnp.float32) * s, 'w2': jax.random.normal(ks[4], (E, H, F), dtype=jnp.float32) * s, 'b2': jax.random.normal(ks[5], (E, H), dtype=jnp.float32) * s}
    _L1_ffn_in = _L1_ffn_setup()
    _d = {'L0_attn_x': _L0_attn_in['x'], 'L0_attn_Wq': _L0_attn_in['Wq'], 'L0_attn_bq': _L0_attn_in['bq'], 'L0_attn_Wk': _L0_attn_in['Wk'], 'L0_attn_bk': _L0_attn_in['bk'], 'L0_attn_Wv': _L0_attn_in['Wv'], 'L0_attn_bv': _L0_attn_in['bv'], 'L0_attn_Wp': _L0_attn_in['Wp'], 'L0_attn_bp': _L0_attn_in['bp'], 'L0_attn_resolve_level': _L0_attn_in['resolve_level'], 'L0_ffn_w_gate': _L0_ffn_in['w_gate'], 'L0_ffn_w_up': _L0_ffn_in['w_up'], 'L0_ffn_w_down': _L0_ffn_in['w_down'], 'L1_attn_ab': _L1_attn_in['ab'], 'L1_attn_h_0': _L1_attn_in['h_0'], 'L1_ffn_router_w': _L1_ffn_in['router_w'], 'L1_ffn_w1': _L1_ffn_in['w1'], 'L1_ffn_b1': _L1_ffn_in['b1'], 'L1_ffn_w2': _L1_ffn_in['w2'], 'L1_ffn_b2': _L1_ffn_in['b2']}
    _x0 = _d['L0_attn_x']
    _d['L0_attn_x'] = jax.random.normal(jax.random.fold_in(jax.random.key(seed), 1), (16, 512, 128), dtype=_x0.dtype)
    del _x0
    return _d

def reference(L0_attn_x, L0_attn_Wq, L0_attn_bq, L0_attn_Wk, L0_attn_bk, L0_attn_Wv, L0_attn_bv, L0_attn_Wp, L0_attn_bp, L0_attn_resolve_level, L0_ffn_w_gate, L0_ffn_w_up, L0_ffn_w_down, L1_attn_ab, L1_attn_h_0, L1_ffn_router_w, L1_ffn_w1, L1_ffn_b1, L1_ffn_w2, L1_ffn_b2):

    def _L0_attn_ref(x, Wq, bq, Wk, bk, Wv, bv, Wp, bp, resolve_level):
        import jax, jax.numpy as jnp
        import numpy as np
        B, T, C, H = (2, 256, 128, 16)
        HD = C // H
        Bx, Tx, Cx = x.shape

        def heads(W, b):
            y = jnp.einsum('btc,dc->btd', x, W) + b
            return y.reshape(Bx, Tx, H, HD).transpose(0, 2, 1, 3)
        q = heads(Wq, bq)
        k = heads(Wk, bk)
        v = heads(Wv, bv)
        scale = 1.0 / jnp.sqrt(jnp.float32(HD))
        attn = jnp.einsum('bhqd,bhkd->bhqk', q, k) * scale
        attn = attn * (0.5 + 0.5 * resolve_level)
        attn = jax.nn.softmax(attn, axis=-1)
        y = jnp.einsum('bhqk,bhkd->bhqd', attn, v)
        y = y.transpose(0, 2, 1, 3).reshape(Bx, Tx, Cx)
        return jnp.einsum('btc,dc->btd', y, Wp) + bp

    def _L0_ffn_ref(x, w_gate, w_up, w_down):
        import jax, jax.numpy as jnp
        import numpy as np
        DIM = 128
        HIDDEN = 384
        SCALE = 1.0 / 127.0

        def _dequant(w_int, dtype):
            return w_int.astype(dtype) * jnp.asarray(SCALE, dtype)
        wg = _dequant(w_gate, x.dtype)
        wu = _dequant(w_up, x.dtype)
        wd = _dequant(w_down, x.dtype)
        gate = jnp.einsum('bsd,hd->bsh', x, wg)
        up = jnp.einsum('bsd,hd->bsh', x, wu)
        h = jax.nn.silu(gate) * up
        return jnp.einsum('bsh,dh->bsd', h, wd)

    def _L1_attn_ref(u, ab, h_0):
        import jax, jax.numpy as jnp
        import numpy as np
        TRUNC_LEN = 1024

        def _get_k(ab, h_0, l):
            D = h_0.shape[0]
            num_a = ab.shape[0] - D
            N = ab.shape[1]
            L = TRUNC_LEN
            ab_p = jnp.pad(ab, ((0, 0), (1, L - N - 1 + L % 2)))
            ab_p = ab_p.at[:num_a, 0].set(1.0)
            AB = jnp.fft.rfft(ab_p, axis=-1)
            A = AB[:num_a]
            Bn = AB[num_a:]
            R = D // num_a
            A_rep = jnp.repeat(A, R, axis=0)
            K = Bn / A_rep + h_0[:, None].astype(Bn.dtype)
            k = jnp.fft.irfft(K, n=L + L % 2, axis=-1)[:, :l]
            return k
        B, l, D = u.shape
        k = _get_k(ab, h_0, l)
        n = 2 * l - l % 2
        Kf = jnp.fft.rfft(k.T, n=n, axis=0)
        Uf = jnp.fft.rfft(u, n=n, axis=1)
        Y = Kf[None, :, :] * Uf
        y = jnp.fft.irfft(Y, n=n, axis=1)[:, :l]
        return y.astype(u.dtype)

    def _L1_ffn_ref(hidden_states, router_w, w1, b1, w2, b2):
        import jax, jax.numpy as jnp
        import numpy as np
        TOP_K = 2
        x = hidden_states
        router_logits = jnp.einsum('bth,eh->bte', x, router_w)
        topk_values, topk_indices = jax.lax.top_k(router_logits, TOP_K)
        topk_weights = jax.nn.softmax(topk_values.astype(jnp.float32), axis=-1).astype(x.dtype)
        h1 = jnp.einsum('bth,efh->btef', x, w1) + b1
        h1 = jax.nn.gelu(h1, approximate=False)
        expert_outputs = jnp.einsum('btef,ehf->bteh', h1, w2) + b2
        gather_idx = topk_indices[..., None]
        topk_expert_outputs = jnp.take_along_axis(expert_outputs, gather_idx, axis=2)
        mixed_output = jnp.sum(topk_expert_outputs * topk_weights[..., None], axis=2)
        return mixed_output
    x = L0_attn_x
    xn = _layernorm(x, axis=-1)
    s = _L0_attn_ref(xn, L0_attn_Wq, L0_attn_bq, L0_attn_Wk, L0_attn_bk, L0_attn_Wv, L0_attn_bv, L0_attn_Wp, L0_attn_bp, L0_attn_resolve_level)
    g = _silu(_L0_ffn_ref(xn, L0_ffn_w_gate, L0_ffn_w_up, L0_ffn_w_down))
    x = x + s * g
    xn = _layernorm(x, axis=-1)
    s = _L1_attn_ref(xn, L1_attn_ab, L1_attn_h_0)
    g = _silu(_L1_ffn_ref(xn, L1_ffn_router_w, L1_ffn_w1, L1_ffn_b1, L1_ffn_w2, L1_ffn_b2))
    x = x + s * g
    return x

_drawn_inputs = setup_inputs


def setup_inputs(seed=0):
    import zlib

    import numpy as np

    out = dict(_drawn_inputs(seed))
    spreads = {'L0_attn_bq': (0.0, 0.8),
     'L0_attn_bk': (0.0, 2.0),
     'L0_attn_bv': (0.0, 0.1),
     'L0_attn_bp': (0.0, 0.1)}
    factors = {'L0_attn_Wq': 8.0,
     'L0_attn_Wk': 8.0,
     'L1_attn_ab': 8.0,
     'L1_attn_h_0': 8.0,
     'L1_ffn_router_w': 8.0,
     'L1_ffn_w1': 8.0,
     'L1_ffn_b1': 8.0,
     'L1_ffn_w2': 8.0,
     'L1_ffn_b2': 21.505}
    for name, (base, spread) in spreads.items():
        noise = np.random.default_rng([zlib.crc32(name.encode()), seed]).standard_normal(out[name].shape)
        drawn = base * np.exp(spread * noise) if base else spread * noise
        out[name] = jnp.asarray(drawn.astype(out[name].dtype))
    for name, factor in factors.items():
        out[name] = (out[name] * factor).astype(out[name].dtype)
    return out
```

```python
import numpy as np
import concourse.bass as bass
from concourse import mybir
from contextlib import ExitStack

FP32 = mybir.dt.float32
FP32R = mybir.dt.float32r
INT32 = mybir.dt.int32
ALU = mybir.AluOpType
ACT = mybir.ActivationFunctionType
AX = mybir.AxisListType

B, T, C = 16, 512, 128
TT = T // 128
EPS = 1e-5

H, HD = 16, 8
HG = 4
NG = H // HG
GR = HG * HD
PARTS = 3
MROW = PARTS * GR
KROWS = MROW + 2 * HG
VW = 32
FFN = 384
FC = FFN // 128
STEPS = NG * TT
AHEAD = 6


class Resident:

    def __init__(self, nc, ctx):
        self.x = ctx.enter_context(nc.sbuf_tensor("x_all", [128, B * TT, C], FP32))
        self.xn = ctx.enter_context(nc.sbuf_tensor("xn_all", [128, B * TT, C], FP32))
        self.ident = ctx.enter_context(nc.sbuf_tensor("ident", [128, 128], FP32))


def head_mask():
    m = np.zeros((128, HG), np.float32)
    for i in range(HG):
        for part in range(PARTS):
            m[GR * part + HD * i:GR * part + HD * (i + 1), i] = 1
        m[MROW + i, i] = m[MROW + HG + i, i] = 1
    return m


def apart(eng, passed):
    eng.sem_inc(passed, 1)


def value_frame():
    f = np.zeros((128, H, VW), np.float32)
    f[:, :, HD:2 * HD] = 1
    return f


def layer0(nc, res, dram):
    with ExitStack() as ctx:
        def sb(name, shape, dt=FP32):
            return ctx.enter_context(nc.sbuf_tensor(name, shape, dt))

        def sem(name):
            return ctx.enter_context(nc.semaphore(name))

        wq, wk, wv, wp = (sb(n, [C, C]) for n in ("wq", "wk", "wv", "wp"))
        bq, bk, bv, level, qscale = (sb(n, [C, 1]) for n in ("bq", "bk", "bv", "level", "qscale"))
        bv_wide = sb("bv_wide", [C, 128])
        bp_row = sb("bp_row", [128, C])
        wg_int, wu_int = sb("wg_int", [C, FFN], INT32), sb("wu_int", [C, FFN], INT32)
        wd_int = sb("wd_int", [128, FC, C], INT32)
        wg, wu, wd = sb("wg", [C, FFN]), sb("wu", [C, FFN]), sb("wd", [128, FC, C])
        mask = sb("mask", [128, HG])

        stats, moments = sb("stats", [128, TT, 6]), sb("moments", [128, TT, 2])
        var_eps, rstd, minus_half = sb("var_eps", [128, TT]), sb("rstd", [128, TT]), sb("minus_half", [128, TT])
        xn = sb("xn", [128, TT, C])
        xnT = sb("xnT", [C, T])

        q_hi = [sb(f"q_hi{p}", [128, T], FP32R) for p in range(2)]
        q_lo = [sb(f"q_lo{p}", [128, T], FP32R) for p in range(2)]
        k_hi = [sb(f"k_hi{p}", [128, T], FP32R) for p in range(2)]
        k_lo = [sb(f"k_lo{p}", [128, T], FP32R) for p in range(2)]
        q_op = [sb(f"q_op{g}", [128, T], FP32R) for g in range(NG)]
        k_op = [sb(f"k_op{p}", [128, T]) for p in range(2)]
        k_head = [[sb(f"k_head{g}_{i}", [128, T], FP32R) for i in range(HG)] for g in range(NG)]
        v_aug = [sb(f"v_aug{p}", [128, TT, H, VW]) for p in range(2)]
        row_max = [sb(f"row_max{p}", [128, TT, HG]) for p in range(2)]
        max_hi = sb("max_hi", [128, TT, HG], FP32R)
        max_parts = sb("max_parts", [128, TT, 2 * HG])
        probs = [sb(f"probs{p}", [128, HG, T]) for p in range(2)]

        y_raw, y_rows, den, yT = (sb(n, [128, T]) for n in ("y_raw", "y_rows", "den", "yT"))
        tanh_g, silu_g = sb("tanh_g", [128, T]), sb("silu_g", [128, T])
        hT = sb("hT", [128, FC, T])
        tanh_z = sb("tanh_z", [128, TT, C])
        gate = [sb(f"gate{p}", [128, TT, C]) for p in range(2)]
        s_out = sb("s_out", [128, TT, C])

        def ps(name, shape):
            return ctx.enter_context(nc.psum_tensor(name, shape, FP32))

        ps_exp = [ps(f"ps_exp{j}", [128, 2, T]) for j in range(2)]
        ps_max = [ps(f"ps_max{j}", [128, T]) for j in range(2)]
        ps_y = ps("ps_y", [128, T])
        ps_side = ps("ps_side", [128, T])
        side_by_token = ps_side[:, :].rearrange("p (t c) -> p t c", t=TT)

        x_loaded, loaded, weights_ready, consts_ready = sem("x_loaded"), sem("loaded"), sem("weights_ready"), sem("consts_ready")
        scale_ready, norm_step, var_ready, rstd_ready = sem("scale_ready"), sem("norm_step"), sem("var_ready"), sem("rstd_ready")
        stats_passed, k_passed = sem("stats_passed"), sem("k_passed")
        xn_ready, xn_out_ready = sem("xn_ready"), sem("xn_out_ready")
        side_ready, side_free = sem("side_ready"), sem("side_free")
        hi_ready, tanh_ready = sem("hi_ready"), sem("tanh_ready")
        q_loaded = [sem(f"q_loaded{g}") for g in range(NG)]
        k_loaded = [sem(f"k_loaded{p}") for p in range(2)]
        k_masked = sem("k_masked")
        max_scores, max_done, max_hi_ready, max_parts_ready = sem("max_scores"), sem("max_done"), sem("max_hi_ready"), sem("max_parts_ready")
        exp_scores, exp_done, pv_done = sem("exp_scores"), sem("exp_done"), sem("pv_done")
        y_evacuated, y_moved, den_inverted, yT_ready = sem("y_evacuated"), sem("y_moved"), sem("den_inverted"), sem("yT_ready")
        gated, x1_ready = sem("gated"), sem("x1_ready")

        def wait(eng, s, v):
            if not isinstance(v, int) or v > 0:
                eng.wait_ge(s, v)

        def norm_in(b):
            if isinstance(b, int):
                return 2 if b == 0 else 2 * b + 1 if b + 2 < B else None
            return 2 * b + 1

        def norm_out(b):
            if isinstance(b, int) and b + 2 >= B:
                return B - 1 + b
            return 2 * b + 2

        def is_last(b):
            return isinstance(b, int) and b == B - 1

        def pairs(b, s, j):
            return 2 * STEPS * b + 2 * s + j + 1

        def max_tiles(b, s, t):
            return TT * (STEPS * b + s + AHEAD) + t + 1

        SIDE = ["xnT", "q", "max", "k", "v", "g0", "max", "u0", "proj", "g1", "max", "u1", "g2", "u2", "max", "down"]
        HEAD_SIDE = ["bias", "xnT", "q", "k", "v", "g0", "u0", "g1", "u1", "g2", "u2", "down", "max"]

        def has_side(b, s):
            if isinstance(b, int) and b == 0 and SIDE[s] == "proj":
                return False
            return not is_last(b) or SIDE[s] == "proj" or (SIDE[s] == "max" and s != STEPS - 2)

        def side(b, s):
            if isinstance(b, int) and b == 0:
                return len(HEAD_SIDE) + sum(has_side(0, t) for t in range(s))
            first = len(HEAD_SIDE) + STEPS * b - 1
            return first + (sum(has_side(b, t) for t in range(s)) if is_last(b) else s)

        def max_head(b, s):
            n = s + AHEAD
            return n >= STEPS, n % STEPS // HG, n % HG

        def has_max(b, s):
            return not (is_last(b) and max_head(b, s)[0])

        def bodies(one):
            one(0, 0)
            with one.engine.Fori(0, (B - 4) // 2) as n:
                one(2 * n + 1, 1)
                one(2 * n + 2, 0)
            for b in range(B - 3, B):
                one(b, b % 2)

        def tiles(b):
            return slice(TT * b, TT * b + TT) if isinstance(b, int) else bass.ds(TT * b, TT)

        def tile(b, t):
            return slice(TT * b + t, TT * b + t + 1) if isinstance(b, int) else bass.ds(TT * b + t, 1)

        LOADS = 16 * (8 + 1 + 3 + 2 + 2 * TT)
        block = ctx.enter_context(nc.Block())

        @block.sync
        def _(sp):
            x_src = dram["x"].rearrange("b (t p) c -> p (b t) c", p=128)
            sp.dma_start(res.x[:, 0:2 * TT, :], x_src[:, 0:2 * TT, :]).then_inc(x_loaded, 16)
            for dst, src in ((wq, "wqT"), (wk, "wkT"), (wv, "wvT"), (wp, "wpT"), (wg_int, "wgT"), (wu_int, "wuT"),
                             (mask, "mask"), (res.ident, "ident")):
                sp.dma_start(dst[:, :], dram[src]).then_inc(loaded, 16)
            sp.dma_start(wd_int[:, :, :], dram["wdT"].rearrange("(f p) c -> p f c", p=128)).then_inc(loaded, 16)
            for dst, src in ((bq, "bq"), (bk, "bk"), (bv, "bv")):
                sp.dma_start(dst[:, :], dram[src].rearrange("(c a) -> c a", a=1)).then_inc(loaded, 16)
            sp.dma_start(bp_row[:, :], dram["bp"].rearrange("(a c) -> a c", a=1).broadcast_to([128, C])).then_inc(loaded, 16)
            sp.dma_start(level[:, :], dram["level"].rearrange("(a c) -> a c", a=1).broadcast_to([128, 1])).then_inc(loaded, 16)
            for p in range(2):
                for t in range(TT):
                    sp.dma_start(v_aug[p][:, t, :, :], dram["value_frame"]).then_inc(loaded, 16)
            sp.wait_ge(x_loaded, 16)
            sp.dma_start(res.x[:, 2 * TT:, :], x_src[:, 2 * TT:, :]).then_inc(x_loaded, 16)

            def load_operands(b, par, g):
                rows = slice(GR * g, GR * g + GR)
                for part, src in enumerate((q_hi, q_lo, q_hi)):
                    sp.dma_start(q_op[g][GR * part:GR * part + GR, :].bitcast(FP32), src[par][rows, :].bitcast(FP32)).then_inc(q_loaded[g], 16)
                wait(sp, k_masked, HG * (NG * b + g - 1))
                for part, src in enumerate((k_hi, k_hi, k_lo)):
                    sp.dma_start(k_op[g % 2][GR * part:GR * part + GR, :], src[par][rows, :].bitcast(FP32)).then_inc(k_loaded[g % 2], 16)

            def move_y(b, g):
                sp.wait_ge(y_evacuated, NG * b + g + 1)
                if g == 0:
                    wait(sp, yT_ready, b)
                for i in range(HG):
                    rows = slice(GR * g + HD * i, GR * g + HD * i + HD)
                    sp.dma_start(y_rows[rows, :], y_raw[VW * i:VW * i + HD, :]).then_inc(y_moved, 16)
                    sp.dma_start(den[rows, :], y_raw[VW * i + HD:VW * i + 2 * HD, :]).then_inc(y_moved, 16)

            sp.wait_ge(consts_ready, 1)
            sp.wait_ge(side_free, HEAD_SIDE.index("k") + 1)
            for g in range(NG):
                load_operands(0, 0, g)

            def one(b, par):
                for g in range(NG):
                    if not is_last(b):
                        sp.wait_ge(exp_scores, pairs(b, TT * g + TT - 1, 1))
                        if g == 0:
                            sp.wait_ge(side_free, side(b, SIDE.index("k")) + 1)
                        load_operands(b + 1, 1 - par, g)
                    move_y(b, g)

            one.engine = sp
            bodies(one)

        @block.gpsimd
        def _(pool):
            for p in range(2):
                pool.memset(k_op[p][:, :], -1.0)
            pool.memset(minus_half[:, :], -0.5).then_inc(consts_ready, 1)

            def mask_heads(b, g):
                pool.wait_ge(k_loaded[g % 2], PARTS * 16 * (NG // 2 * b + g // 2 + 1))
                apart(pool, k_passed)
                for i in range(HG):
                    pool.tensor_scalar(k_head[g][i][0:KROWS, :], k_op[g % 2][0:KROWS, :], mask[0:KROWS, i:i + 1], 1.0,
                                       ALU.mult, ALU.mult).then_inc(k_masked, 1)

            def norm_rstd(n):
                pool.wait_ge(var_ready, n + 1)
                pool.tensor_tensor(rstd[:, :], var_eps[:, :], minus_half[:, :], ALU.pow).then_inc(rstd_ready, 1)

            def gate_out(b, par, projected):
                pool.wait_ge(side_free, projected)
                pool.tensor_tensor(s_out[:, :, :], s_out[:, :, :], gate[par][:, :, :], ALU.mult).then_inc(gated, 1)
                pool.wait_ge(gated, b + 1)
                pool.tensor_tensor(res.x[:, tiles(b), :], s_out[:, :, :], res.x[:, tiles(b), :], ALU.add).then_inc(x1_ready, 1)

            pool.wait_ge(consts_ready, 1)
            norm_rstd(0)
            norm_rstd(1)
            pool.wait_ge(loaded, LOADS)
            for g in range(NG):
                mask_heads(0, g)

            def one(b, par):
                first = isinstance(b, int) and b == 0
                if norm_in(b) is not None:
                    norm_rstd(norm_in(b))
                if not is_last(b):
                    mask_heads(b + 1, 0)
                if not first:
                    gate_out(b - 1, 1 - par, side(b, SIDE.index("proj")) + 1)
                    norm_rstd(norm_out(b))
                if not is_last(b):
                    for g in range(1, NG):
                        mask_heads(b + 1, g)

            one.engine = pool
            bodies(one)
            gate_out(B - 1, (B - 1) % 2, side(B - 1, STEPS) + 1)
            norm_rstd(2 * B - 1)

        @block.vector
        def _(dve):
            def norm_stats(n, b):
                for t in range(TT):
                    last = dve.bn_stats(stats[:, t, :], res.x[:, tile(b, t), :])
                last.then_inc(norm_step, 1)
                dve.wait_ge(norm_step, 2 * n + 1)
                apart(dve, stats_passed)
                for t in range(TT):
                    last = dve.bn_aggr(moments[:, t, :], stats[:, t, :])
                last.then_inc(norm_step, 1)
                dve.wait_ge(norm_step, 2 * n + 2)
                dve.tensor_scalar(var_eps[:, :], moments[:, :, 1], EPS, None, ALU.add).then_inc(var_ready, 1)

            def norm_apply(n, b, dst, ready):
                dve.wait_ge(rstd_ready, n + 1)
                for t in range(TT):
                    last = dve.tensor_scalar(dst(t), res.x[:, tile(b, t), :], moments[:, t, 0:1], rstd[:, t:t + 1],
                                             ALU.subtract, ALU.mult)
                last.then_inc(ready, 1)

            def norm_input(n, b):
                norm_apply(n, b, lambda t: xn[:, t:t + 1, :], xn_ready)

            def norm_output(n, b):
                norm_apply(n, b, lambda t: res.xn[:, tile(b, t), :], xn_out_ready)

            def maximum(t, bank, count, group, i):
                dve.wait_ge(max_scores, count)
                dve.tensor_reduce(row_max[group % 2][:, t, i:i + 1], ps_max[bank][:, :], AX.X, ALU.max).then_inc(max_done, 1)

            def maxima_parts(n, group, tiles_done, rows_made):
                dve.wait_ge(max_done, tiles_done)
                wait(dve, side_ready, rows_made)
                dve.tensor_copy(max_hi[:, :, :], row_max[group % 2][:, :, :]).then_inc(max_hi_ready, 1)
                dve.wait_ge(max_hi_ready, n + 1)
                dve.tensor_copy(max_parts[:, :, 0:HG], max_hi[:, :, :].bitcast(FP32))
                dve.tensor_tensor(max_parts[:, :, HG:], row_max[group % 2][:, :, :], max_hi[:, :, :].bitcast(FP32),
                                  ALU.subtract).then_inc(max_parts_ready, 1)

            def from_side(what, b, par, n):
                if what in ("q", "k"):
                    lo, hi, bias = (q_lo, q_hi, bq) if what == "q" else (k_lo, k_hi, bk)
                    dve.wait_ge(hi_ready, 2 * b + (1 if what == "q" else 2))
                    dve.scalar_tensor_tensor(lo[par][:, :], ps_side[:, :], bias[:, 0:1], hi[par][:, :].bitcast(FP32),
                                             ALU.add, ALU.subtract).then_inc(side_free, 1)
                elif what[0] == "g":
                    dve.wait_ge(tanh_ready, 4 * b + int(what[1]) + 1)
                    dve.scalar_tensor_tensor(silu_g[:, :], tanh_g[:, :], 1.0, ps_side[:, :], ALU.add, ALU.mult).then_inc(side_free, 1)
                elif what[0] == "u":
                    dve.wait_ge(side_ready, n + 1)
                    dve.wait_ge(side_free, n)
                    dve.tensor_tensor(hT[:, int(what[1]), :], silu_g[:, :], ps_side[:, :], ALU.mult).then_inc(side_free, 1)
                elif what == "down":
                    dve.wait_ge(tanh_ready, 4 * b + 4)
                    dve.scalar_tensor_tensor(gate[par][:, :, :], tanh_z[:, :, :], 1.0, side_by_token, ALU.add, ALU.mult).then_inc(side_free, 1)
                elif what == "proj":
                    dve.wait_ge(side_ready, n + 1)
                    dve.tensor_tensor(s_out[:, :, :], side_by_token, bp_row[:, None, :].broadcast_to([128, TT, C]), ALU.add)\
                       .then_inc(side_free, 1)

            def normalise_y(b):
                dve.wait_ge(y_moved, 2 * H * 16 * (b + 1))
                dve.reciprocal(den[:, :], den[:, :]).then_inc(den_inverted, 1)
                dve.wait_ge(den_inverted, b + 1)
                dve.tensor_tensor(yT[:, :], y_rows[:, :], den[:, :], ALU.mult).then_inc(yT_ready, 1)

            dve.wait_ge(x_loaded, 16)
            norm_stats(0, 0)
            norm_input(0, 0)
            dve.wait_ge(loaded, LOADS)
            s8 = float(np.float32(1.0) / np.sqrt(np.float32(HD)))
            unit = float(np.float32(1.0 / 127.0))
            dve.tensor_scalar(qscale[:, :], level[:, :], 0.5 * s8, 0.5 * s8, ALU.mult, ALU.add).then_inc(scale_ready, 1)
            dve.wait_ge(scale_ready, 1)
            dve.tensor_scalar(wq[:, :], wq[:, :], qscale[:, 0:1], None, ALU.mult)
            dve.tensor_scalar(bq[:, :], bq[:, :], qscale[:, 0:1], None, ALU.mult)
            dve.tensor_scalar(wg[:, :], wg_int[:, :], unit, None, ALU.mult)
            dve.tensor_scalar(wu[:, :], wu_int[:, :], unit, None, ALU.mult)
            dve.tensor_scalar(wd[:, :, :], wd_int[:, :, :], unit, 0.5, ALU.mult, ALU.mult)
            dve.tensor_scalar(wp[:, :], wp[:, :], 0.5, None, ALU.mult)
            dve.tensor_scalar(bp_row[:, :], bp_row[:, :], 0.5, None, ALU.mult)
            dve.tensor_copy(bv_wide[:, :], bv[:, 0:1].broadcast_to([C, 128])).then_inc(weights_ready, 1)
            dve.wait_ge(weights_ready, 1)
            dve.wait_ge(side_ready, 1)
            dve.tensor_tensor(bp_row[:, :], ps_side[:, 0:C], bp_row[:, :], ALU.add).then_inc(side_free, 1)
            dve.wait_ge(side_free, 1)
            from_side("q", 0, 0, 2)
            from_side("k", 0, 0, 3)
            norm_stats(1, 1)
            dve.wait_ge(side_ready, 2)
            norm_input(1, 1)
            for n in range(AHEAD):
                for t in range(TT):
                    maximum(t, t % 2, TT * n + t + 1, n // HG, n % HG)
                from_side(HEAD_SIDE[5 + n], 0, 0, 5 + n)
            from_side("down", 0, 0, 11)
            maxima_parts(0, 0, TT * HG, 0)

            def one(b, par):
                first = isinstance(b, int) and b == 0
                for s in range(STEPS):
                    def tile_max(t):
                        if has_max(b, s):
                            _, group, i = max_head(b, s)
                            maximum(t, t % 2, max_tiles(b, s, t), group, i)

                    tile_max(0)
                    if s == 0 and not first:
                        from_side("down", b, par, side(b, 0) - 1)
                    elif s > 0 and has_side(b, s - 1) and SIDE[s - 1] != "down":
                        prev = SIDE[s - 1]
                        if prev == "proj":
                            from_side(prev, b - 1, 1 - par, side(b, s - 1))
                        else:
                            from_side(prev, b + 1, 1 - par, side(b, s - 1))
                    tile_max(1)
                    if s % HG == 2 and has_side(b, s):
                        g = s // HG
                        before = side(b, s - HG) + 1 if g else side(b, 0) - (0 if first else 1)
                        maxima_parts(NG * b + g + 1, g + 1, TT * (STEPS * b + TT * (g + 1) + HG), before)
                    if s == 1 and norm_in(b) is not None:
                        norm_stats(norm_in(b), b + 2)
                    if s == 3 and norm_in(b) is not None:
                        norm_input(norm_in(b), b + 2)
                    if s == 4 and not first:
                        normalise_y(b - 1)
                    tile_max(2)
                    if s == 11 and not first:
                        dve.wait_ge(x1_ready, b)
                        norm_stats(norm_out(b), b - 1)
                    if s == 13 and not first:
                        norm_output(norm_out(b), b - 1)
                    tile_max(3)

            dve.wait_ge(x_loaded, 32)
            one.engine = dve
            bodies(one)
            normalise_y(B - 1)
            from_side("proj", B - 1, (B - 1) % 2, side(B - 1, STEPS))
            dve.wait_ge(x1_ready, B)
            norm_stats(2 * B - 1, B - 1)
            norm_output(2 * B - 1, B - 1)
            dve.wait_ge(xn_out_ready, B)

        @block.scalar
        def _(act):
            def from_side(what, b, par, n, group=None):
                if what in ("bias", "proj") or what[0] == "u":
                    return
                act.wait_ge(side_ready, n + 1)
                if what == "xnT":
                    act.activation(xnT[:, :], ps_side[:, :], ACT.Copy).then_inc(side_free, 1)
                elif what in ("q", "k"):
                    hi, bias = (q_hi, bq) if what == "q" else (k_hi, bk)
                    wait(act, q_loaded[NG - 1], PARTS * 16 * (b - 1))
                    wait(act, k_loaded[1], PARTS * 16 * NG // 2 * (b - 1))
                    act.activation(hi[par][:, :], ps_side[:, :], ACT.Identity, bias=bias[:, 0:1]).then_inc(hi_ready, 1)
                elif what == "v":
                    act.activation(v_aug[par][:, :, :, 0:HD], ps_side[:, :].rearrange("p (t h d) -> p t h d", t=TT, h=H),
                                   ACT.Copy).then_inc(side_free, 1)
                elif what[0] == "g":
                    act.activation(tanh_g[:, :], ps_side[:, :], ACT.Tanh, scale=0.5).then_inc(tanh_ready, 1)
                elif what == "down":
                    act.activation(tanh_z[:, :, :], side_by_token, ACT.Tanh, scale=0.5).then_inc(tanh_ready, 1)
                elif what == "max":
                    act.activation(q_op[group][MROW:KROWS, :], ps_side[MROW:KROWS, :], ACT.Copy).then_inc(side_free, 1)

            act.wait_ge(weights_ready, 1)
            for n, what in enumerate(HEAD_SIDE):
                from_side(what, 0, 0, n, 0)

            def exponentials(b, s, j):
                act.wait_ge(exp_scores, pairs(b, s, j))
                wait(act, pv_done, STEPS * b + s - 1)
                act.activation(probs[s % 2][:, 2 * j:2 * j + 2, :], ps_exp[j][:, :, :], ACT.Exp).then_inc(exp_done, 1)

            def evacuate_y(b, g):
                act.wait_ge(pv_done, STEPS * b + TT * g + TT)
                wait(act, y_moved, 2 * HG * 16 * (NG * b + g))
                act.activation(y_raw[:, :], ps_y[:, :], ACT.Copy).then_inc(y_evacuated, 1)

            def one(b, par):
                first = isinstance(b, int) and b == 0
                for s in range(STEPS):
                    exponentials(b, s, 0)
                    if s == 0 and not first:
                        from_side("down", b, par, side(b, 0) - 1)
                    elif s > 0 and has_side(b, s - 1) and SIDE[s - 1] != "down":
                        from_side(SIDE[s - 1], b + 1, 1 - par, side(b, s - 1), (s // HG + 1) % NG)
                    exponentials(b, s, 1)
                    if s % TT == 0:
                        if s:
                            evacuate_y(b, s // TT - 1)
                        elif not first:
                            evacuate_y(b - 1, NG - 1)

            one.engine = act
            bodies(one)
            evacuate_y(B - 1, NG - 1)

        @block.tensor
        def _(pe):
            def wide(out, lhsT, rhs):
                return pe.matmul(out, lhsT, rhs, start=True, stop=True)

            def to_side(what, b, par, n, group=0):
                wait(pe, side_free, n)
                if what == "bias":
                    pe.wait_ge(weights_ready, 1)
                    last = wide(ps_side[:, 0:C], bv_wide[:, :], wp[:, :])
                elif what == "xnT":
                    pe.wait_ge(xn_ready, b + 1)
                    for t in range(TT):
                        last = pe.transpose(side_by_token[:, t, :], xn[:, t, :], res.ident[:, :])
                elif what in ("q", "k"):
                    last = wide(ps_side[:, :], (wq if what == "q" else wk)[:, :], xnT[:, :])
                elif what == "v":
                    for t in range(TT):
                        last = wide(side_by_token[:, t, :], xnT[:, 128 * t:128 * t + 128], wv[:, :])
                elif what[0] in "gu":
                    f = int(what[1])
                    last = wide(ps_side[:, :], (wg if what[0] == "g" else wu)[:, 128 * f:128 * f + 128], xnT[:, :])
                elif what == "down":
                    for t in range(TT):
                        for f in range(FC):
                            last = pe.matmul(side_by_token[:, t, :], hT[:, f, 128 * t:128 * t + 128], wd[:, f, :],
                                             start=(f == 0), stop=(f == FC - 1))
                elif what == "proj":
                    pe.wait_ge(yT_ready, b + 1)
                    for t in range(TT):
                        last = wide(side_by_token[:, t, :], yT[:, 128 * t:128 * t + 128], wp[:, :])
                elif what == "max":
                    pe.wait_ge(max_parts_ready, group + 1)
                    for t in range(TT):
                        last = wide(ps_side[MROW:KROWS, 128 * t:128 * t + 128], max_parts[:, t, :], res.ident[:, :])
                last.then_inc(side_ready, 1)

            def score_for_max(group, i, t, count):
                wait(pe, max_done, count - 2)
                wide(ps_max[t % 2][:, :], q_op[group][0:MROW, 128 * t:128 * t + 128], k_head[group][i][0:MROW, :])\
                    .then_inc(max_scores, 1)

            def operands(b, group, i):
                pe.wait_ge(q_loaded[group], PARTS * 16 * (b + 1))
                pe.wait_ge(k_masked, HG * (NG * b + group) + i + 1)

            def score_for_exp(b, s, j):
                g, t = s // TT, s % TT
                wait(pe, exp_done, pairs(b, s, j) - 2)
                for i in (2 * j, 2 * j + 1):
                    last = wide(ps_exp[j][:, i % 2, :], k_head[g][i][0:KROWS, 128 * t:128 * t + 128], q_op[g][0:KROWS, :])
                last.then_inc(exp_scores, 1)

            def weigh_values(b, par, s):
                g, t = s // TT, s % TT
                if t == 0:
                    wait(pe, y_evacuated, NG * b + g)
                for i in range(HG):
                    if i % 2 == 0:
                        pe.wait_ge(exp_done, pairs(b, s, i // 2))
                    last = pe.matmul(ps_y[VW * i:VW * i + VW, :], v_aug[par][:, t, HG * g + i, :], probs[s % 2][:, i, :],
                                     start=(t == 0), stop=(t == TT - 1))
                last.then_inc(pv_done, 1)

            pe.wait_ge(loaded, LOADS)
            for n in range(5):
                to_side(HEAD_SIDE[n], 0, 0, n)
            for n in range(AHEAD):
                operands(0, n // HG, n % HG)
                for t in range(TT):
                    score_for_max(n // HG, n % HG, t, TT * n + t + 1)
                to_side(HEAD_SIDE[5 + n], 0, 0, 5 + n)
            to_side("down", 0, 0, 11)
            to_side("max", 0, 0, 12)

            def one(b, par):
                first = isinstance(b, int) and b == 0
                for s in range(STEPS):
                    def tile_max(t):
                        if has_max(b, s):
                            following, group, i = max_head(b, s)
                            if t == 0:
                                operands(b + 1 if following else b, group, i)
                            score_for_max(group, i, t, max_tiles(b, s, t))

                    if s % TT == 0:
                        at = side(b, s - 2) if s else side(b, 0) - (1 if first else 2)
                        pe.wait_ge(side_free, at + 1)
                    score_for_exp(b, s, 0)
                    tile_max(0)
                    if s:
                        weigh_values(b, par, s - 1)
                    elif not first:
                        weigh_values(b - 1, 1 - par, STEPS - 1)
                    tile_max(1)
                    score_for_exp(b, s, 1)
                    tile_max(2)
                    if has_side(b, s):
                        what = SIDE[s]
                        if what == "proj":
                            to_side(what, b - 1, 1 - par, side(b, s))
                        elif what == "max":
                            to_side(what, b, par, side(b, s), NG * b + s // HG + 1)
                        else:
                            to_side(what, b + 1, 1 - par, side(b, s))
                    tile_max(3)

            one.engine = pe
            bodies(one)
            weigh_values(B - 1, (B - 1) % 2, STEPS - 1)
            to_side("proj", B - 1, (B - 1) % 2, side(B - 1, STEPS))



L = 1024
TAPS = 64
FT = L // 2 // 128
E, F = 8, 512
FE = F // 128
KPAD = 128
CG = 4


def transform_tables():
    f = np.arange(L // 2 + 1)
    j = np.arange(1, TAPS + 1)[:, None]
    fwd = np.stack([np.cos(2 * np.pi * j * f / L), -np.sin(2 * np.pi * j * f / L)], 1)
    t = T - 1 - np.arange(T)
    w = np.where(np.arange(L // 2) == 0, 1.0, 2.0)[:, None] / L
    ang = 2 * np.pi * ((np.arange(L // 2)[:, None] * t) % L) / L
    inv = np.stack([w * np.cos(ang), -w * np.sin(ang)], 0).reshape(2, FT, 128, T).transpose(2, 0, 1, 3)
    nyq = ((-1.0) ** t / L)[None, :]
    return fwd.astype(np.float32), np.ascontiguousarray(inv).astype(np.float32), nyq.astype(np.float32)


def make_filters(nc, dram):
    with ExitStack() as ctx:
        def sb(name, shape, dt=FP32):
            return ctx.enter_context(nc.sbuf_tensor(name, shape, dt))

        def sem(name):
            return ctx.enter_context(nc.semaphore(name))

        taps = sb("taps", [TAPS, 2 * C])
        fwd = sb("fwd", [TAPS, 2, L // 2 + 1])
        inv = sb("inv", [128, 2, FT, T])
        nyq_row = sb("nyq_row", [1, T])
        h0 = sb("h0", [C, 1])
        spec = sb("spec", [128, FT, 2, 2, C])
        nyq = sb("nyq", [1, 2, C])
        norm = sb("norm", [128, FT, C]); prod = [sb(f"prod{n}", [128, FT, C]) for n in range(4)]
        ratio = sb("ratio", [128, 2, FT, C]); nyq_ratio = sb("nyq_ratio", [1, C])
        k_pad = sb("k_pad", [C, KPAD + T])
        ps_spec = ctx.enter_context(nc.psum_tensor("ps_spec", [128, FT, 2, 2 * C], FP32))
        ps_nyq = ctx.enter_context(nc.psum_tensor("ps_nyq", [1, 512], FP32))
        ps_k = ctx.enter_context(nc.psum_tensor("ps_k", [C, T], FP32))
        loaded, transformed, copied, step, divided = (sem(n) for n in ("f_loaded", "transformed", "spec_copied", "div_step", "divided"))
        inverted, k_ready, k_stored = sem("inverted"), sem("k_ready"), sem("k_stored")
        block = ctx.enter_context(nc.Block())

        @block.sync
        def _(sp):
            sp.dma_start(taps[:, :], dram["abT"]).then_inc(loaded, 16)
            sp.dma_start(fwd[:, :, :], dram["fwd"]).then_inc(loaded, 16)
            sp.dma_start(nyq_row[:, :], dram["nyq"]).then_inc(loaded, 16)
            sp.dma_start(h0[:, :], dram["h0"].rearrange("(c a) -> c a", a=1)).then_inc(loaded, 16)
            sp.dma_start(inv[:, :, :, :], dram["inv"]).then_inc(loaded, 16)
            sp.wait_ge(k_ready, 1)
            sp.dma_start(dram["k_pad"], k_pad[:, :]).then_inc(k_stored, 16)
            sp.wait_ge(k_stored, 16)

        @block.tensor
        def _(pe):
            pe.wait_ge(loaded, 80)
            for f in range(FT):
                for part in range(2):
                    pe.matmul(ps_spec[:, f, part, :], fwd[:, part, 128 * f:128 * f + 128], taps[:, :], start=True, stop=True)
            pe.matmul(ps_nyq[0:1, 0:2 * C], fwd[:, 0, L // 2:L // 2 + 1], taps[:, :], start=True, stop=True).then_inc(transformed, 1)
            pe.wait_ge(divided, 1)
            for f in range(FT):
                for part in range(2):
                    pe.matmul(ps_k[:, :], ratio[:, part, f, :], inv[:, part, f, :], start=(f == 0 and part == 0), stop=False)
            pe.matmul(ps_k[:, :], nyq_ratio[0:1, :], nyq_row[0:1, :], start=False, stop=True).then_inc(inverted, 1)

        @block.scalar
        def _(act):
            act.wait_ge(transformed, 1)
            act.activation(spec[:, :, :, :, :].rearrange("p f r s c -> p (f r s c)"),
                           ps_spec[:, :, :, :].rearrange("p f r s -> p (f r s)"), ACT.Copy)
            act.activation(nyq[:, :, :].rearrange("p s c -> p (s c)"), ps_nyq[0:1, 0:2 * C], ACT.Copy).then_inc(copied, 1)

        @block.vector
        def _(dve):
            n = [0]

            def done(ins):
                ins.then_inc(step, 1)
                n[0] += 1
                dve.wait_ge(step, n[0])

            ar, br, ai, bi = spec[:, :, 0, 0, :], spec[:, :, 0, 1, :], spec[:, :, 1, 0, :], spec[:, :, 1, 1, :]
            p = [x[:, :, :] for x in prod]
            dve.memset(k_pad[:, T:], 0.0)
            dve.wait_ge(copied, 1)
            dve.tensor_scalar(nyq[:, 0, :], nyq[:, 0, :], 1.0, None, ALU.add)
            done(dve.tensor_scalar(ar, ar, 1.0, None, ALU.add))
            dve.reciprocal(nyq[:, 0, :], nyq[:, 0, :])
            dve.tensor_tensor(p[0], ar, ar, ALU.mult)
            done(dve.tensor_tensor(p[1], ai, ai, ALU.mult))
            dve.tensor_tensor(nyq_ratio[:, :], nyq[:, 0, :], nyq[:, 1, :], ALU.mult)
            done(dve.tensor_tensor(norm[:, :, :], p[0], p[1], ALU.add))
            dve.tensor_tensor(p[0], br, ar, ALU.mult)
            dve.tensor_tensor(p[1], bi, ai, ALU.mult)
            dve.tensor_tensor(p[2], bi, ar, ALU.mult)
            dve.tensor_tensor(p[3], br, ai, ALU.mult)
            done(dve.reciprocal(norm[:, :, :], norm[:, :, :]))
            dve.tensor_tensor(p[0], p[0], p[1], ALU.add)
            done(dve.tensor_tensor(p[2], p[2], p[3], ALU.subtract))
            dve.tensor_tensor(ratio[:, 0, :, :], p[0], norm[:, :, :], ALU.mult)
            dve.tensor_tensor(ratio[:, 1, :, :], p[2], norm[:, :, :], ALU.mult).then_inc(divided, 1)
            dve.wait_ge(inverted, 1)
            dve.tensor_tensor(k_pad[:, T - 1:T], ps_k[:, T - 1:T], h0[:, :], ALU.add)
            dve.tensor_copy(k_pad[:, 0:T - 1], ps_k[:, 0:T - 1]).then_inc(k_ready, 1)


def convolve(nc, res, dram, s_all):
    with ExitStack() as ctx:
        def sb(name, shape, dt=FP32):
            return ctx.enter_context(nc.sbuf_tensor(name, shape, dt))

        def sem(name):
            return ctx.enter_context(nc.semaphore(name))

        NQ = C // CG
        toep = [sb(f"toep{p}", [128, CG, T]) for p in range(2)]
        inputs = [sb(f"conv_in{p}", [128, TT, CG, B]) for p in range(2)]
        by_time = [sb(f"by_time{p}", [128, T]) for p in range(2)]
        ps_t = [ctx.enter_context(nc.psum_tensor(f"ps_t{p}", [128, T], FP32)) for p in range(2)]
        ps_b = [ctx.enter_context(nc.psum_tensor(f"ps_b{p}", [128, TT, CG, 32], FP32)) for p in range(2)]
        toep_loaded = [sem(f"toep_loaded{p}") for p in range(2)]
        cleared, picked, convolved, copied, turned, spread = (sem(n) for n in ("cleared", "picked", "convolved", "by_time_copied", "turned", "spread"))
        block = ctx.enter_context(nc.Block())

        def at(q):
            return slice(CG * q, CG * q + CG) if isinstance(q, int) else bass.ds(CG * q, CG)

        def bodies(eng, one):
            one(0, 0)
            one(1, 1)
            with eng.Fori(1, NQ // 2) as n:
                one(2 * n, 0)
                one(2 * n + 1, 1)

        def wait(eng, s, v):
            if not isinstance(v, int) or v > 0:
                eng.wait_ge(s, v)

        @block.sync
        def _(sp):
            def one(q, p):
                wait(sp, convolved, q - 1)
                src = bass.AP(dram["k_pad"].tensor, CG * (KPAD + T) * q, [[1, 128], [KPAD + T, CG], [1, T]])
                sp.dma_start(toep[p][:, :, :], src).then_inc(toep_loaded[p], 16)

            bodies(sp, one)

        @block.vector
        def _(dve):
            xn = res.xn[:, :, :].rearrange("p (b t) c -> p t b c", b=B)
            s_out = s_all[:, :, :].rearrange("p (b t) c -> p t b c", b=B)
            for p in range(2):
                last = dve.memset(ps_t[p][:, :], 0.0)
            last.then_inc(cleared, 1)

            def pick(q, p):
                wait(dve, convolved, q - 1)
                for t in range(TT):
                    last = dve.tensor_copy(inputs[p][:, t, :, :].rearrange("p c b -> p b c"), xn[:, t, :, at(q)])
                last.then_inc(picked, 1)

            def out(q, p):
                dve.wait_ge(turned, q + 1)
                for t in range(TT):
                    last = dve.tensor_copy(s_out[:, t, :, at(q)], ps_b[p][:, t, :, 0:B].rearrange("p c b -> p b c"))
                last.then_inc(spread, 1)

            pick(0, 0)
            pick(1, 1)
            with dve.Fori(1, NQ // 2) as n:
                for p in range(2):
                    pick(2 * n + p, p)
                    out(2 * n + p - 2, p)
            for q in (NQ - 2, NQ - 1):
                out(q, q % 2)

        @block.scalar
        def _(act):
            def one(q, p):
                act.wait_ge(convolved, q + 1)
                wait(act, turned, q - 1)
                act.activation(by_time[p][:, :], ps_t[p][:, ::-1], ACT.Copy).then_inc(copied, 1)

            bodies(act, one)

        @block.tensor
        def _(pe):
            def product(q, p):
                pe.wait_ge(picked, q + 1)
                pe.wait_ge(toep_loaded[p], 16 * (q // 2 + 1) if isinstance(q, int) else 8 * (q - p) + 16)
                wait(pe, copied, q - 1)
                for t in range(TT):
                    for i in range(CG):
                        last = pe.matmul(ps_t[p][32 * i:32 * i + B, 0:T - 128 * t], inputs[p][:, t, i, :], toep[p][:, i, 128 * t:],
                                         start=(t == 0), stop=(t == TT - 1))
                last.then_inc(convolved, 1)

            def turn(q, p):
                pe.wait_ge(copied, q + 1)
                wait(pe, spread, q - 1)
                for t in range(TT):
                    last = pe.transpose(ps_b[p][:, t, :, :].rearrange("p c b -> p (c b)"), by_time[p][:, 128 * t:128 * t + 128], res.ident[:, :])
                last.then_inc(turned, 1)

            pe.wait_ge(cleared, 1)
            product(0, 0)
            product(1, 1)
            turn(0, 0)
            with pe.Fori(1, NQ // 2) as n:
                product(2 * n, 0)
                turn(2 * n - 1, 1)
                product(2 * n + 1, 1)
                turn(2 * n, 0)
            turn(NQ - 1, 1)


def experts(nc, res, dram, s_all):
    with ExitStack() as ctx:
        def sb(name, shape, dt=FP32):
            return ctx.enter_context(nc.sbuf_tensor(name, shape, dt))

        def sem(name):
            return ctx.enter_context(nc.semaphore(name))

        NT = B * TT
        xnT = sb("xnT_all", [C, B * T])
        w1 = sb("w1", [C, E, F]); w2 = sb("w2", [128, E, FE, C])
        b1 = sb("b1", [128, E, FE]); b2 = sb("b2", [128, E, C]); rw = sb("rw", [C, E])
        numbers = sb("numbers", [128, E])
        xn_now = [sb(f"xn_now{p}", [128, TT, C]) for p in range(2)]; xnT_now = [sb(f"xnT_now{p}", [128, T]) for p in range(2)]
        top = sb("top", [128, NT, 2]); top_now = sb("top_now", [128, TT, 8]); top_at_now = sb("top_at_now", [128, TT, 8], mybir.dt.uint32); chosen = sb("chosen", [128, NT, 2])
        logits = sb("logits", [128, TT, E])
        gap, w_first, w_second = sb("gap", [128, NT]), sb("w_first", [128, NT]), sb("w_second", [128, NT])
        weight, second = sb("weight", [128, NT, E]), sb("second", [128, NT, E])
        hidden = [sb(f"hidden{p}", [128, FE, T]) for p in range(2)]
        w_now = sb("w_now", [128, TT, E])
        term = [sb(f"term{p}", [128, TT, C]) for p in range(2)]; mixed = [sb(f"mixed{p}", [128, TT, C]) for p in range(2)]
        tanh_m, out_now = sb("tanh_m", [128, TT, C]), sb("out_now", [128, TT, C])

        ps_x = [ctx.enter_context(nc.psum_tensor(f"ps_h{p}", [128, T], FP32)) for p in range(4)]
        ps_o = [ctx.enter_context(nc.psum_tensor(f"ps_o{p}", [128, TT, C], FP32)) for p in range(2)]
        w_loaded = sem("e_loaded")
        now_copied, turned, copied, scored, routed = sem("now_copied"), sem("x_turned"), sem("x_copied"), sem("scored"), sem("routed")
        top_ready, gap_ready, exp_ready, mix_step = sem("top_ready"), sem("gap_ready"), sem("gap_exp"), sem("mix_step")
        top_passed = sem("top_passed")
        h_scores, h_ready, o_ready, o_taken = sem("h_scores"), sem("h_ready2"), sem("o_ready"), sem("o_taken")
        now_ready, term_ready, mixed_ready, tanh_ready, gated, out_ready, stored = (
            sem(n) for n in ("now_ready", "term_ready", "mixed_ready", "mix_tanh", "mix_gated", "out_ready", "out_stored"))
        block = ctx.enter_context(nc.Block())

        def wait(eng, s, v):
            if not isinstance(v, int) or v > 0:
                eng.wait_ge(s, v)

        def tiles(b):
            return slice(TT * b, TT * b + TT) if isinstance(b, int) else bass.ds(TT * b, TT)

        def tile(b, t):
            return slice(TT * b + t, TT * b + t + 1) if isinstance(b, int) else bass.ds(TT * b + t, 1)

        @block.sync
        def _(sp):
            sp.dma_start(rw[:, :], dram["rwT"]).then_inc(w_loaded, 16)
            sp.dma_start(b1[:, :, :], dram["b1T"]).then_inc(w_loaded, 16)
            sp.dma_start(b2[:, :, :], dram["b2"].rearrange("(a e) c -> a e c", a=1).broadcast_to([128, E, C])).then_inc(w_loaded, 16)
            sp.dma_start(numbers[:, :], dram["numbers"]).then_inc(w_loaded, 16)
            sp.dma_start(w1[:, :, :], dram["w1T"]).then_inc(w_loaded, 16)
            sp.dma_start(w2[:, :, :, :], dram["w2T"]).then_inc(w_loaded, 16)
            out = dram["out"].rearrange("b (t p) c -> p b t c", p=128)
            sp.wait_ge(out_ready, 1)
            sp.dma_start(out[:, 0, :, :], out_now[:, :, :]).then_inc(stored, 16)
            with sp.Fori(1, B) as b:
                sp.wait_ge(out_ready, b + 1)
                sp.dma_start(out[:, bass.ds(b, 1), :, :].rearrange("p a t c -> p (a t) c"), out_now[:, :, :]).then_inc(stored, 16)
            sp.wait_ge(stored, 16 * B)

        @block.tensor
        def _(pe):
            pe.wait_ge(w_loaded, 96)

            def route(b, p):
                pe.wait_ge(now_copied, b + 1)
                wait(pe, copied, b - 1)
                for t in range(TT):
                    last = pe.transpose(ps_x[p][:, 128 * t:128 * t + 128], xn_now[p][:, t, :], res.ident[:, :])
                last.then_inc(turned, 1)
                pe.wait_ge(copied, b + 1)
                wait(pe, routed, b - 1)
                for t in range(TT):
                    last = pe.matmul(ps_o[p][:, t, 0:E], xnT_now[p][:, 128 * t:128 * t + 128], rw[:, :], start=True, stop=True)
                last.then_inc(scored, 1)

            route(0, 0)
            route(1, 1)
            with pe.Fori(1, B // 2) as n:
                route(2 * n, 0)
                route(2 * n + 1, 1)

            def first_layer(n, e, b):
                for f in range(FE):
                    wait(pe, h_ready, 4 * n + f - 3)
                    pe.matmul(ps_x[f][:, :], w1[:, e, 128 * f:128 * f + 128], xnT[:, slice(0, T) if isinstance(b, int) else bass.ds(T * b, T)], start=True, stop=True).then_inc(h_scores, 1)

            def second_layer(n, e):
                wait(pe, o_taken, n - 1)
                pe.wait_ge(h_ready, 4 * n + 4)
                for t in range(TT):
                    for f in range(FE):
                        last = pe.matmul(ps_o[e % 2][:, t, :], hidden[e % 2][:, f, 128 * t:128 * t + 128], w2[:, e, f, :],
                                         start=(f == 0), stop=(f == FE - 1))
                last.then_inc(o_ready, 1)

            pe.wait_ge(routed, B)
            def one(b):
                for e in range(E):
                    first_layer(E * b + e, e, b)
                    if e:
                        second_layer(E * b + e - 1, e - 1)
                second_layer(E * b + E - 1, E - 1)

            one(0)
            with pe.Fori(1, B) as b:
                one(b)

        @block.scalar
        def _(act):
            def turn(b, p):
                act.wait_ge(turned, b + 1)
                act.activation(xnT_now[p][:, :], ps_x[p][:, :], ACT.Copy)
                act.activation(xnT[:, slice(T * b, T * b + T) if isinstance(b, int) else bass.ds(T * b, T)], ps_x[p][:, :], ACT.Copy).then_inc(copied, 1)

            turn(0, 0)
            turn(1, 1)
            with act.Fori(1, B // 2) as n:
                turn(2 * n, 0)
                turn(2 * n + 1, 1)
            act.wait_ge(gap_ready, 1)
            act.activation(gap[:, :], gap[:, :], ACT.Exp).then_inc(exp_ready, 1)

            def one(b):
                for e in range(E):
                    n = E * b + e
                    wait(act, o_ready, n - 1)
                    for f in range(FE):
                        act.wait_ge(h_scores, 4 * n + f + 1)
                        act.activation(hidden[e % 2][:, f, :], ps_x[f][:, :], ACT.Gelu, bias=b1[:, e, f:f + 1]).then_inc(h_ready, 1)
                act.wait_ge(mixed_ready, b + 1)
                act.activation(tanh_m[:, :, :], mixed[0][:, :, :], ACT.Tanh, scale=0.5).then_inc(tanh_ready, 1)

            one(0)
            with act.Fori(1, B) as b:
                one(b)

        @block.vector
        def _(dve):
            def fetch(b, p):
                wait(dve, turned, b - 1)
                dve.tensor_copy(xn_now[p][:, :, :], res.xn[:, tiles(b), :]).then_inc(now_copied, 1)

            def route(b, p):
                dve.wait_ge(scored, b + 1)
                dve.tensor_copy(logits[:, :, :], ps_o[p][:, :, 0:E]).then_inc(top_ready, 1)
                dve.wait_ge(top_ready, 3 * b + 1)
                apart(dve, top_passed)
                for t in range(TT):
                    last = dve.max(top_now[:, t, :], logits[:, t, :])
                last.then_inc(top_ready, 1)
                dve.wait_ge(top_ready, 3 * b + 2)
                apart(dve, top_passed)
                for t in range(TT):
                    last = dve.max_index(top_at_now[:, t, :], top_now[:, t, :], logits[:, t, :])
                last.then_inc(top_ready, 1)
                dve.wait_ge(top_ready, 3 * b + 3)
                dve.tensor_copy(top[:, tiles(b), :], top_now[:, :, 0:2])
                dve.tensor_copy(chosen[:, tiles(b), :], top_at_now[:, :, 0:2]).then_inc(routed, 1)

            dve.wait_ge(w_loaded, 96)
            fetch(0, 0)
            fetch(1, 1)
            with dve.Fori(1, B // 2) as n:
                for p in range(2):
                    route(2 * n - 2 + p, p)
                    fetch(2 * n + p, p)
            route(B - 2, 0)
            route(B - 1, 1)
            dve.wait_ge(routed, B)
            dve.tensor_tensor(gap[:, :], top[:, :, 1], top[:, :, 0], ALU.subtract).then_inc(gap_ready, 1)
            dve.wait_ge(exp_ready, 1)
            dve.tensor_scalar(w_first[:, :], gap[:, :], 1.0, None, ALU.add).then_inc(mix_step, 1)
            dve.wait_ge(mix_step, 1)
            dve.reciprocal(w_first[:, :], w_first[:, :]).then_inc(mix_step, 1)
            dve.wait_ge(mix_step, 2)
            dve.tensor_tensor(w_second[:, :], gap[:, :], w_first[:, :], ALU.mult)
            wide = [128, NT, E]
            for k, dst in ((0, weight), (1, second)):
                last = dve.tensor_tensor(dst[:, :, :], numbers[:, None, :].broadcast_to(wide), chosen[:, :, k:k + 1].broadcast_to(wide), ALU.is_equal)
            last.then_inc(mix_step, 1)
            dve.wait_ge(mix_step, 3)
            for dst, w in ((weight, w_first), (second, w_second)):
                last = dve.tensor_tensor(dst[:, :, :], dst[:, :, :], w[:, :, None].broadcast_to(wide), ALU.mult)
            last.then_inc(mix_step, 1)
            dve.wait_ge(mix_step, 4)
            dve.tensor_tensor(weight[:, :, :], weight[:, :, :], second[:, :, :], ALU.add).then_inc(mix_step, 1)
            dve.wait_ge(mix_step, 5)
            def one(b):
                dve.tensor_copy(w_now[:, :, :], weight[:, tiles(b), :]).then_inc(now_ready, 1)
                dve.wait_ge(now_ready, b + 1)
                for e in range(E):
                    n = E * b + e
                    dve.wait_ge(o_ready, n + 1)
                    dve.tensor_tensor(term[e % 2][:, :, :], ps_o[e % 2][:, :, :], b2[:, e:e + 1, :].broadcast_to([128, TT, C]), ALU.add).then_inc(o_taken, 1)
                    dve.wait_ge(o_taken, n + 1)
                    if e:
                        dve.wait_ge(term_ready, (E - 1) * b + e)
                    for t in range(TT):
                        into, add = mixed[(e + 1) % 2][:, t, :], mixed[e % 2][:, t, :]
                        if e == 0:
                            last = dve.tensor_scalar(into, term[e % 2][:, t, :], w_now[:, t, e:e + 1], None, ALU.mult)
                        else:
                            last = dve.scalar_tensor_tensor(into, term[e % 2][:, t, :], w_now[:, t, e:e + 1], add, ALU.mult, ALU.add)
                    last.then_inc(term_ready if e < E - 1 else mixed_ready, 1)
                dve.wait_ge(tanh_ready, b + 1)
                dve.scalar_tensor_tensor(tanh_m[:, :, :], tanh_m[:, :, :], 1.0, mixed[0][:, :, :], ALU.add, ALU.mult).then_inc(gated, 1)
                dve.wait_ge(gated, 2 * b + 1)
                dve.tensor_tensor(tanh_m[:, :, :], tanh_m[:, :, :], s_all[:, tiles(b), :], ALU.mult).then_inc(gated, 1)
                dve.wait_ge(gated, 2 * b + 2)
                wait(dve, stored, 16 * b)
                dve.scalar_tensor_tensor(out_now[:, :, :], tanh_m[:, :, :], 0.5, res.x[:, tiles(b), :], ALU.mult, ALU.add).then_inc(out_ready, 1)

            one(0)
            with dve.Fori(1, B) as b:
                one(b)


def laid_out(inputs):
    def t(a, *axes):
        return np.ascontiguousarray(np.transpose(a, axes or None))

    return {
        "x": inputs["L0_attn_x"],
        "wqT": t(inputs["L0_attn_Wq"]), "wkT": t(inputs["L0_attn_Wk"]), "wvT": t(inputs["L0_attn_Wv"]),
        "wpT": t(inputs["L0_attn_Wp"]),
        "bq": inputs["L0_attn_bq"], "bk": inputs["L0_attn_bk"], "bv": inputs["L0_attn_bv"], "bp": inputs["L0_attn_bp"],
        "level": np.reshape(inputs["L0_attn_resolve_level"], (1,)),
        "wgT": t(inputs["L0_ffn_w_gate"]), "wuT": t(inputs["L0_ffn_w_up"]), "wdT": t(inputs["L0_ffn_w_down"]),
        "abT": t(inputs["L1_attn_ab"]), "h0": inputs["L1_attn_h_0"],
        "rwT": t(inputs["L1_ffn_router_w"]),
        "b1T": t(np.reshape(inputs["L1_ffn_b1"], (E, FE, 128)), 2, 0, 1), "b2": inputs["L1_ffn_b2"],
        "w1T": t(inputs["L1_ffn_w1"], 2, 0, 1),
        "w2T": t(np.reshape(inputs["L1_ffn_w2"], (E, C, FE, 128)), 3, 0, 2, 1),
    }


def build(nc, dram):
    fwd, inv, nyq = transform_tables()
    constants = {
        "mask": head_mask(), "ident": np.eye(128, dtype=np.float32), "value_frame": value_frame(),
        "fwd": fwd, "inv": inv, "nyq": nyq,
        "numbers": np.tile(np.arange(E, dtype=np.float32), (128, 1)),
    }
    for name, value in constants.items():
        dram[name] = nc.inline_tensor(value, f"const_{name}").ap()
    dram["k_pad"] = nc.dram_tensor("k_pad_scratch", [C, KPAD + T], FP32).ap()
    with ExitStack() as ctx:
        res = Resident(nc, ctx)
        layer0(nc, res, dram)
        s_all = ctx.enter_context(nc.sbuf_tensor("s_all", [128, B * TT, C], FP32))
        make_filters(nc, dram)
        convolve(nc, res, dram, s_all)
        experts(nc, res, dram, s_all)


def kernel(**inputs):
    import concourse.bacc as _bacc
    from concourse.bass_utils import run_bass_kernel_spmd as _run

    nc = _bacc.Bacc("TRN2", target_bir_lowering=False, num_devices=1)
    arrays, dram = {}, {}
    for name, value in laid_out({k: np.asarray(v) for k, v in inputs.items()}).items():
        value = np.ascontiguousarray(value)
        arrays[f"in_{name}_dram"] = value
        dram[name] = nc.dram_tensor(f"in_{name}_dram", value.shape, mybir.dt.from_np(value.dtype), kind="ExternalInput").ap()
    dram["out"] = nc.dram_tensor("out_0_dram", (B, T, C), FP32, kind="ExternalOutput").ap()
    build(nc, dram)
    return _run(nc, [arrays], core_ids=[0]).results[0]["out_0_dram"]
```

```python
import numpy as np
import concourse.bass as bass
from concourse import mybir
from contextlib import ExitStack

FP32 = mybir.dt.float32
FP32R = mybir.dt.float32r
INT32 = mybir.dt.int32
ALU = mybir.AluOpType
ACT = mybir.ActivationFunctionType
AX = mybir.AxisListType

B, T, C = 16, 512, 128
TT = T // 128
EPS = 1e-5

H, HD = 16, 8
HG = 4
NG = H // HG
GR = HG * HD
PARTS = 3
MROW = PARTS * GR
KROWS = MROW + 2 * HG
VW = 32
FFN = 384
FC = FFN // 128
STEPS = NG * TT
AHEAD = 6


class Resident:

    def __init__(self, nc, ctx):
        self.x = ctx.enter_context(nc.sbuf_tensor("x_all", [128, B * TT, C], FP32))
        self.xn = ctx.enter_context(nc.sbuf_tensor("xn_all", [128, B * TT, C], FP32))
        self.ident = ctx.enter_context(nc.sbuf_tensor("ident", [128, 128], FP32))


def head_mask():
    m = np.zeros((128, HG), np.float32)
    for i in range(HG):
        for part in range(PARTS):
            m[GR * part + HD * i:GR * part + HD * (i + 1), i] = 1
        m[MROW + i, i] = m[MROW + HG + i, i] = 1
    return m


def apart(eng, passed):
    eng.sem_inc(passed, 1)


def value_frame():
    f = np.zeros((128, H, VW), np.float32)
    f[:, :, HD:2 * HD] = 1
    return f


def layer0(nc, res, dram):
    with ExitStack() as ctx:
        def sb(name, shape, dt=FP32):
            return ctx.enter_context(nc.sbuf_tensor(name, shape, dt))

        def sem(name):
            return ctx.enter_context(nc.semaphore(name))

        wq, wk, wv, wp = (sb(n, [C, C]) for n in ("wq", "wk", "wv", "wp"))
        bq, bk, bv, level, qscale = (sb(n, [C, 1]) for n in ("bq", "bk", "bv", "level", "qscale"))
        bv_wide = sb("bv_wide", [C, 128])
        bp_row = sb("bp_row", [128, C])
        wg_int, wu_int = sb("wg_int", [C, FFN], INT32), sb("wu_int", [C, FFN], INT32)
        wd_int = sb("wd_int", [128, FC, C], INT32)
        wg, wu, wd = sb("wg", [C, FFN]), sb("wu", [C, FFN]), sb("wd", [128, FC, C])
        mask = sb("mask", [128, HG])

        stats, moments = sb("stats", [128, TT, 6]), sb("moments", [128, TT, 2])
        var_eps, rstd, minus_half = sb("var_eps", [128, TT]), sb("rstd", [128, TT]), sb("minus_half", [128, TT])
        xn = sb("xn", [128, TT, C])
        xnT = sb("xnT", [C, T])

        q_hi = [sb(f"q_hi{p}", [128, T], FP32R) for p in range(2)]
        q_lo = [sb(f"q_lo{p}", [128, T], FP32R) for p in range(2)]
        k_hi = [sb(f"k_hi{p}", [128, T], FP32R) for p in range(2)]
        k_lo = [sb(f"k_lo{p}", [128, T], FP32R) for p in range(2)]
        q_op = [sb(f"q_op{g}", [128, T], FP32R) for g in range(NG)]
        k_op = [sb(f"k_op{p}", [128, T]) for p in range(2)]
        k_head = [[sb(f"k_head{g}_{i}", [128, T], FP32R) for i in range(HG)] for g in range(NG)]
        v_aug = [sb(f"v_aug{p}", [128, TT, H, VW]) for p in range(2)]
        row_max = [sb(f"row_max{p}", [128, TT, HG]) for p in range(2)]
        max_hi = sb("max_hi", [128, TT, HG], FP32R)
        max_parts = sb("max_parts", [128, TT, 2 * HG])
        probs = [sb(f"probs{p}", [128, HG, T]) for p in range(2)]

        y_raw, y_rows, den, yT = (sb(n, [128, T]) for n in ("y_raw", "y_rows", "den", "yT"))
        tanh_g, silu_g = sb("tanh_g", [128, T]), sb("silu_g", [128, T])
        hT = sb("hT", [128, FC, T])
        tanh_z = sb("tanh_z", [128, TT, C])
        gate = [sb(f"gate{p}", [128, TT, C]) for p in range(2)]
        s_out = sb("s_out", [128, TT, C])

        def ps(name, shape):
            return ctx.enter_context(nc.psum_tensor(name, shape, FP32))

        ps_exp = [ps(f"ps_exp{j}", [128, 2, T]) for j in range(2)]
        ps_max = [ps(f"ps_max{j}", [128, T]) for j in range(2)]
        ps_y = ps("ps_y", [128, T])
        ps_side = ps("ps_side", [128, T])
        side_by_token = ps_side[:, :].rearrange("p (t c) -> p t c", t=TT)

        x_loaded, loaded, weights_ready, consts_ready = sem("x_loaded"), sem("loaded"), sem("weights_ready"), sem("consts_ready")
        scale_ready, norm_step, var_ready, rstd_ready = sem("scale_ready"), sem("norm_step"), sem("var_ready"), sem("rstd_ready")
        stats_passed, k_passed = sem("stats_passed"), sem("k_passed")
        xn_ready, xn_out_ready = sem("xn_ready"), sem("xn_out_ready")
        side_ready, side_free = sem("side_ready"), sem("side_free")
        hi_ready, tanh_ready = sem("hi_ready"), sem("tanh_ready")
        q_loaded = [sem(f"q_loaded{g}") for g in range(NG)]
        k_loaded = [sem(f"k_loaded{p}") for p in range(2)]
        k_masked = sem("k_masked")
        max_scores, max_done, max_hi_ready, max_parts_ready = sem("max_scores"), sem("max_done"), sem("max_hi_ready"), sem("max_parts_ready")
        exp_scores, exp_done, pv_done = sem("exp_scores"), sem("exp_done"), sem("pv_done")
        y_evacuated, y_moved, den_inverted, yT_ready = sem("y_evacuated"), sem("y_moved"), sem("den_inverted"), sem("yT_ready")
        gated, x1_ready = sem("gated"), sem("x1_ready")

        def wait(eng, s, v):
            if not isinstance(v, int) or v > 0:
                eng.wait_ge(s, v)

        def norm_in(b):
            if isinstance(b, int):
                return 2 if b == 0 else 2 * b + 1 if b + 2 < B else None
            return 2 * b + 1

        def norm_out(b):
            if isinstance(b, int) and b + 2 >= B:
                return B - 1 + b
            return 2 * b + 2

        def is_last(b):
            return isinstance(b, int) and b == B - 1

        def pairs(b, s, j):
            return 2 * STEPS * b + 2 * s + j + 1

        def max_tiles(b, s, t):
            return TT * (STEPS * b + s + AHEAD) + t + 1

        SIDE = ["xnT", "q", "max", "k", "v", "g0", "max", "u0", "proj", "g1", "max", "u1", "g2", "u2", "max", "down"]
        HEAD_SIDE = ["bias", "xnT", "q", "k", "v", "g0", "u0", "g1", "u1", "g2", "u2", "down", "max"]

        def has_side(b, s):
            if isinstance(b, int) and b == 0 and SIDE[s] == "proj":
                return False
            return not is_last(b) or SIDE[s] == "proj" or (SIDE[s] == "max" and s != STEPS - 2)

        def side(b, s):
            if isinstance(b, int) and b == 0:
                return len(HEAD_SIDE) + sum(has_side(0, t) for t in range(s))
            first = len(HEAD_SIDE) + STEPS * b - 1
            return first + (sum(has_side(b, t) for t in range(s)) if is_last(b) else s)

        def max_head(b, s):
            n = s + AHEAD
            return n >= STEPS, n % STEPS // HG, n % HG

        def has_max(b, s):
            return not (is_last(b) and max_head(b, s)[0])

        def bodies(one):
            one(0, 0)
            with one.engine.Fori(0, (B - 4) // 2) as n:
                one(2 * n + 1, 1)
                one(2 * n + 2, 0)
            for b in range(B - 3, B):
                one(b, b % 2)

        def tiles(b):
            return slice(TT * b, TT * b + TT) if isinstance(b, int) else bass.ds(TT * b, TT)

        def tile(b, t):
            return slice(TT * b + t, TT * b + t + 1) if isinstance(b, int) else bass.ds(TT * b + t, 1)

        LOADS = 16 * (8 + 1 + 3 + 2 + 2 * TT)
        block = ctx.enter_context(nc.Block())

        @block.sync
        def _(sp):
            x_src = dram["x"].rearrange("b (t p) c -> p (b t) c", p=128)
            sp.dma_start(res.x[:, 0:2 * TT, :], x_src[:, 0:2 * TT, :]).then_inc(x_loaded, 16)
            for dst, src in ((wq, "wqT"), (wk, "wkT"), (wv, "wvT"), (wp, "wpT"), (wg_int, "wgT"), (wu_int, "wuT"),
                             (mask, "mask"), (res.ident, "ident")):
                sp.dma_start(dst[:, :], dram[src]).then_inc(loaded, 16)
            sp.dma_start(wd_int[:, :, :], dram["wdT"].rearrange("(f p) c -> p f c", p=128)).then_inc(loaded, 16)
            for dst, src in ((bq, "bq"), (bk, "bk"), (bv, "bv")):
                sp.dma_start(dst[:, :], dram[src].rearrange("(c a) -> c a", a=1)).then_inc(loaded, 16)
            sp.dma_start(bp_row[:, :], dram["bp"].rearrange("(a c) -> a c", a=1).broadcast_to([128, C])).then_inc(loaded, 16)
            sp.dma_start(level[:, :], dram["level"].rearrange("(a c) -> a c", a=1).broadcast_to([128, 1])).then_inc(loaded, 16)
            for p in range(2):
                for t in range(TT):
                    sp.dma_start(v_aug[p][:, t, :, :], dram["value_frame"]).then_inc(loaded, 16)
            sp.wait_ge(x_loaded, 16)
            sp.dma_start(res.x[:, 2 * TT:, :], x_src[:, 2 * TT:, :]).then_inc(x_loaded, 16)

            def load_operands(b, par, g):
                rows = slice(GR * g, GR * g + GR)
                for part, src in enumerate((q_hi, q_lo, q_hi)):
                    sp.dma_start(q_op[g][GR * part:GR * part + GR, :].bitcast(FP32), src[par][rows, :].bitcast(FP32)).then_inc(q_loaded[g], 16)
                wait(sp, k_masked, HG * (NG * b + g - 1))
                for part, src in enumerate((k_hi, k_hi, k_lo)):
                    sp.dma_start(k_op[g % 2][GR * part:GR * part + GR, :], src[par][rows, :].bitcast(FP32)).then_inc(k_loaded[g % 2], 16)

            def move_y(b, g):
                sp.wait_ge(y_evacuated, NG * b + g + 1)
                if g == 0:
                    wait(sp, yT_ready, TT * b)
                for i in range(HG):
                    rows = slice(GR * g + HD * i, GR * g + HD * i + HD)
                    sp.dma_start(y_rows[rows, :], y_raw[VW * i:VW * i + HD, :]).then_inc(y_moved, 16)
                    sp.dma_start(den[rows, :], y_raw[VW * i + HD:VW * i + 2 * HD, :]).then_inc(y_moved, 16)

            sp.wait_ge(consts_ready, 1)
            sp.wait_ge(side_free, HEAD_SIDE.index("k") + 1)
            for g in range(NG):
                load_operands(0, 0, g)

            def one(b, par):
                for g in range(NG):
                    if not is_last(b):
                        sp.wait_ge(exp_scores, pairs(b, TT * g + TT - 1, 1))
                        if g == 0:
                            sp.wait_ge(side_free, side(b, SIDE.index("k")) + 1)
                        load_operands(b + 1, 1 - par, g)
                    move_y(b, g)

            one.engine = sp
            bodies(one)

        @block.gpsimd
        def _(pool):
            for p in range(2):
                pool.memset(k_op[p][:, :], -1.0)
            pool.memset(minus_half[:, :], -0.5).then_inc(consts_ready, 1)

            def mask_heads(b, g):
                pool.wait_ge(k_loaded[g % 2], PARTS * 16 * (NG // 2 * b + g // 2 + 1))
                apart(pool, k_passed)
                for i in range(HG):
                    pool.tensor_scalar(k_head[g][i][0:KROWS, :], k_op[g % 2][0:KROWS, :], mask[0:KROWS, i:i + 1], 1.0,
                                       ALU.mult, ALU.mult).then_inc(k_masked, 1)

            def norm_rstd(n):
                pool.wait_ge(var_ready, n + 1)
                pool.tensor_tensor(rstd[:, :], var_eps[:, :], minus_half[:, :], ALU.pow).then_inc(rstd_ready, 1)

            def gate_out(b, par, projected):
                pool.wait_ge(side_free, projected)
                pool.tensor_tensor(s_out[:, :, :], s_out[:, :, :], gate[par][:, :, :], ALU.mult).then_inc(gated, 1)
                pool.wait_ge(gated, b + 1)
                pool.tensor_tensor(res.x[:, tiles(b), :], s_out[:, :, :], res.x[:, tiles(b), :], ALU.add).then_inc(x1_ready, 1)

            pool.wait_ge(consts_ready, 1)
            norm_rstd(0)
            norm_rstd(1)
            pool.wait_ge(loaded, LOADS)
            for g in range(NG):
                mask_heads(0, g)

            def one(b, par):
                first = isinstance(b, int) and b == 0
                if norm_in(b) is not None:
                    norm_rstd(norm_in(b))
                if not is_last(b):
                    mask_heads(b + 1, 0)
                if not first:
                    gate_out(b - 1, 1 - par, side(b, SIDE.index("proj")) + 1)
                    norm_rstd(norm_out(b))
                if not is_last(b):
                    for g in range(1, NG):
                        mask_heads(b + 1, g)

            one.engine = pool
            bodies(one)
            gate_out(B - 1, (B - 1) % 2, side(B - 1, STEPS) + 1)
            norm_rstd(2 * B - 1)

        @block.vector
        def _(dve):
            def norm_stats(n, b):
                for t in range(TT):
                    last = dve.bn_stats(stats[:, t, :], res.x[:, tile(b, t), :])
                last.then_inc(norm_step, 1)
                dve.wait_ge(norm_step, 2 * n + 1)
                apart(dve, stats_passed)
                for t in range(TT):
                    last = dve.bn_aggr(moments[:, t, :], stats[:, t, :])
                last.then_inc(norm_step, 1)
                dve.wait_ge(norm_step, 2 * n + 2)
                dve.tensor_scalar(var_eps[:, :], moments[:, :, 1], EPS, None, ALU.add).then_inc(var_ready, 1)

            def norm_apply(n, b, dst, ready):
                dve.wait_ge(rstd_ready, n + 1)
                for t in range(TT):
                    last = dve.tensor_scalar(dst(t), res.x[:, tile(b, t), :], moments[:, t, 0:1], rstd[:, t:t + 1],
                                             ALU.subtract, ALU.mult)
                last.then_inc(ready, 1)

            def norm_input(n, b):
                norm_apply(n, b, lambda t: xn[:, t:t + 1, :], xn_ready)

            def norm_output(n, b):
                norm_apply(n, b, lambda t: res.xn[:, tile(b, t), :], xn_out_ready)

            def maximum(t, bank, count, group, i):
                dve.wait_ge(max_scores, count)
                dve.tensor_reduce(row_max[group % 2][:, t, i:i + 1], ps_max[bank][:, :], AX.X, ALU.max).then_inc(max_done, 1)

            def maxima_parts(n, group, tiles_done, rows_made):
                dve.wait_ge(max_done, tiles_done)
                wait(dve, side_ready, rows_made)
                dve.tensor_copy(max_hi[:, :, :], row_max[group % 2][:, :, :]).then_inc(max_hi_ready, 1)
                dve.wait_ge(max_hi_ready, n + 1)
                dve.tensor_copy(max_parts[:, :, 0:HG], max_hi[:, :, :].bitcast(FP32))
                dve.tensor_tensor(max_parts[:, :, HG:], row_max[group % 2][:, :, :], max_hi[:, :, :].bitcast(FP32),
                                  ALU.subtract).then_inc(max_parts_ready, 1)

            def from_side(what, b, par, n):
                if what in ("q", "k"):
                    lo, hi, bias = (q_lo, q_hi, bq) if what == "q" else (k_lo, k_hi, bk)
                    dve.wait_ge(hi_ready, 2 * b + (1 if what == "q" else 2))
                    dve.scalar_tensor_tensor(lo[par][:, :], ps_side[:, :], bias[:, 0:1], hi[par][:, :].bitcast(FP32),
                                             ALU.add, ALU.subtract).then_inc(side_free, 1)
                elif what[0] == "g":
                    dve.wait_ge(tanh_ready, 4 * b + int(what[1]) + 1)
                    dve.scalar_tensor_tensor(silu_g[:, :], tanh_g[:, :], 1.0, ps_side[:, :], ALU.add, ALU.mult).then_inc(side_free, 1)
                elif what[0] == "u":
                    dve.wait_ge(side_ready, n + 1)
                    dve.wait_ge(side_free, n)
                    dve.tensor_tensor(hT[:, int(what[1]), :], silu_g[:, :], ps_side[:, :], ALU.mult).then_inc(side_free, 1)
                elif what == "down":
                    dve.wait_ge(tanh_ready, 4 * b + 4)
                    dve.scalar_tensor_tensor(gate[par][:, :, :], tanh_z[:, :, :], 1.0, side_by_token, ALU.add, ALU.mult).then_inc(side_free, 1)
                elif what == "proj":
                    dve.wait_ge(side_ready, n + 1)
                    dve.tensor_tensor(s_out[:, :, :], side_by_token, bp_row[:, None, :].broadcast_to([128, TT, C]), ALU.add)\
                       .then_inc(side_free, 1)

            def normalise_y(b, t):
                at = slice(128 * t, 128 * t + 128)
                if t == 0:
                    dve.wait_ge(y_moved, 2 * H * 16 * (b + 1))
                dve.reciprocal(den[:, at], den[:, at]).then_inc(den_inverted, 1)
                dve.wait_ge(den_inverted, TT * b + t + 1)
                dve.tensor_tensor(yT[:, at], y_rows[:, at], den[:, at], ALU.mult).then_inc(yT_ready, 1)

            dve.wait_ge(x_loaded, 16)
            norm_stats(0, 0)
            norm_input(0, 0)
            dve.wait_ge(loaded, LOADS)
            s8 = float(np.float32(1.0) / np.sqrt(np.float32(HD)))
            unit = float(np.float32(1.0 / 127.0))
            dve.tensor_scalar(qscale[:, :], level[:, :], 0.5 * s8, 0.5 * s8, ALU.mult, ALU.add).then_inc(scale_ready, 1)
            dve.wait_ge(scale_ready, 1)
            dve.tensor_scalar(wq[:, :], wq[:, :], qscale[:, 0:1], None, ALU.mult)
            dve.tensor_scalar(bq[:, :], bq[:, :], qscale[:, 0:1], None, ALU.mult)
            dve.tensor_scalar(wg[:, :], wg_int[:, :], unit, None, ALU.mult)
            dve.tensor_scalar(wu[:, :], wu_int[:, :], unit, None, ALU.mult)
            dve.tensor_scalar(wd[:, :, :], wd_int[:, :, :], unit, 0.5, ALU.mult, ALU.mult)
            dve.tensor_scalar(wp[:, :], wp[:, :], 0.5, None, ALU.mult)
            dve.tensor_scalar(bp_row[:, :], bp_row[:, :], 0.5, None, ALU.mult)
            dve.tensor_copy(bv_wide[:, :], bv[:, 0:1].broadcast_to([C, 128])).then_inc(weights_ready, 1)
            dve.wait_ge(weights_ready, 1)
            dve.wait_ge(side_ready, 1)
            dve.tensor_tensor(bp_row[:, :], ps_side[:, 0:C], bp_row[:, :], ALU.add).then_inc(side_free, 1)
            dve.wait_ge(side_free, 1)
            from_side("q", 0, 0, 2)
            from_side("k", 0, 0, 3)
            norm_stats(1, 1)
            dve.wait_ge(side_ready, 2)
            norm_input(1, 1)
            for n in range(AHEAD):
                for t in range(TT):
                    maximum(t, t % 2, TT * n + t + 1, n // HG, n % HG)
                from_side(HEAD_SIDE[5 + n], 0, 0, 5 + n)
            from_side("down", 0, 0, 11)
            maxima_parts(0, 0, TT * HG, 0)

            def one(b, par):
                first = isinstance(b, int) and b == 0
                for s in range(STEPS):
                    def tile_max(t):
                        if has_max(b, s):
                            _, group, i = max_head(b, s)
                            maximum(t, t % 2, max_tiles(b, s, t), group, i)

                    if s % HG == 2 and has_side(b, s):
                        g = s // HG
                        before = side(b, s - HG) + 1 if g else side(b, 0) - (0 if first else 1)
                        maxima_parts(NG * b + g + 1, g + 1, TT * (STEPS * b + TT * (g + 1) + HG), before)
                    tile_max(0)
                    if s == 0 and not first:
                        from_side("down", b, par, side(b, 0) - 1)
                    elif s > 0 and has_side(b, s - 1) and SIDE[s - 1] != "down":
                        prev = SIDE[s - 1]
                        if prev == "proj":
                            from_side(prev, b - 1, 1 - par, side(b, s - 1))
                        else:
                            from_side(prev, b + 1, 1 - par, side(b, s - 1))
                    tile_max(1)
                    if s == 7 and norm_in(b) is not None:
                        norm_stats(norm_in(b), b + 2)
                    if s == 9 and norm_in(b) is not None:
                        norm_input(norm_in(b), b + 2)
                    tile_max(2)
                    if s == 12 and not first:
                        dve.wait_ge(x1_ready, b)
                        norm_stats(norm_out(b), b - 1)
                    if s == 14 and not first:
                        norm_output(norm_out(b), b - 1)
                    tile_max(3)
                    if 2 <= s < 2 + TT and not first:
                        normalise_y(b - 1, s - 2)

            dve.wait_ge(x_loaded, 32)
            one.engine = dve
            bodies(one)
            for t in range(TT):
                normalise_y(B - 1, t)
            from_side("proj", B - 1, (B - 1) % 2, side(B - 1, STEPS))
            dve.wait_ge(x1_ready, B)
            norm_stats(2 * B - 1, B - 1)
            norm_output(2 * B - 1, B - 1)
            dve.wait_ge(xn_out_ready, B)

        @block.scalar
        def _(act):
            def from_side(what, b, par, n, group=None):
                if what in ("bias", "proj") or what[0] == "u":
                    return
                act.wait_ge(side_ready, n + 1)
                if what == "xnT":
                    act.activation(xnT[:, :], ps_side[:, :], ACT.Copy).then_inc(side_free, 1)
                elif what in ("q", "k"):
                    hi, bias = (q_hi, bq) if what == "q" else (k_hi, bk)
                    wait(act, q_loaded[NG - 1], PARTS * 16 * (b - 1))
                    wait(act, k_loaded[1], PARTS * 16 * NG // 2 * (b - 1))
                    act.activation(hi[par][:, :], ps_side[:, :], ACT.Identity, bias=bias[:, 0:1]).then_inc(hi_ready, 1)
                elif what == "v":
                    act.activation(v_aug[par][:, :, :, 0:HD], ps_side[:, :].rearrange("p (t h d) -> p t h d", t=TT, h=H),
                                   ACT.Copy).then_inc(side_free, 1)
                elif what[0] == "g":
                    act.activation(tanh_g[:, :], ps_side[:, :], ACT.Tanh, scale=0.5).then_inc(tanh_ready, 1)
                elif what == "down":
                    act.activation(tanh_z[:, :, :], side_by_token, ACT.Tanh, scale=0.5).then_inc(tanh_ready, 1)
                elif what == "max":
                    act.activation(q_op[group][MROW:KROWS, :], ps_side[MROW:KROWS, :], ACT.Copy).then_inc(side_free, 1)

            act.wait_ge(weights_ready, 1)
            for n, what in enumerate(HEAD_SIDE):
                from_side(what, 0, 0, n, 0)

            def exponentials(b, s, j):
                act.wait_ge(exp_scores, pairs(b, s, j))
                wait(act, pv_done, STEPS * b + s - 1)
                act.activation(probs[s % 2][:, 2 * j:2 * j + 2, :], ps_exp[j][:, :, :], ACT.Exp).then_inc(exp_done, 1)

            def evacuate_y(b, g):
                act.wait_ge(pv_done, STEPS * b + TT * g + TT)
                wait(act, y_moved, 2 * HG * 16 * (NG * b + g))
                act.activation(y_raw[:, :], ps_y[:, :], ACT.Copy).then_inc(y_evacuated, 1)

            def one(b, par):
                first = isinstance(b, int) and b == 0
                for s in range(STEPS):
                    exponentials(b, s, 0)
                    if s == 0 and not first:
                        from_side("down", b, par, side(b, 0) - 1)
                    elif s > 0 and has_side(b, s - 1) and SIDE[s - 1] != "down":
                        from_side(SIDE[s - 1], b + 1, 1 - par, side(b, s - 1), (s // HG + 1) % NG)
                    exponentials(b, s, 1)
                    if s % TT == 0:
                        if s:
                            evacuate_y(b, s // TT - 1)
                        elif not first:
                            evacuate_y(b - 1, NG - 1)

            one.engine = act
            bodies(one)
            evacuate_y(B - 1, NG - 1)

        @block.tensor
        def _(pe):
            def wide(out, lhsT, rhs):
                return pe.matmul(out, lhsT, rhs, start=True, stop=True)

            def to_side(what, b, par, n, group=0):
                wait(pe, side_free, n)
                if what == "bias":
                    pe.wait_ge(weights_ready, 1)
                    last = wide(ps_side[:, 0:C], bv_wide[:, :], wp[:, :])
                elif what == "xnT":
                    pe.wait_ge(xn_ready, b + 1)
                    for t in range(TT):
                        last = pe.transpose(side_by_token[:, t, :], xn[:, t, :], res.ident[:, :])
                elif what in ("q", "k"):
                    last = wide(ps_side[:, :], (wq if what == "q" else wk)[:, :], xnT[:, :])
                elif what == "v":
                    for t in range(TT):
                        last = wide(side_by_token[:, t, :], xnT[:, 128 * t:128 * t + 128], wv[:, :])
                elif what[0] in "gu":
                    f = int(what[1])
                    last = wide(ps_side[:, :], (wg if what[0] == "g" else wu)[:, 128 * f:128 * f + 128], xnT[:, :])
                elif what == "down":
                    for t in range(TT):
                        for f in range(FC):
                            last = pe.matmul(side_by_token[:, t, :], hT[:, f, 128 * t:128 * t + 128], wd[:, f, :],
                                             start=(f == 0), stop=(f == FC - 1))
                elif what == "proj":
                    pe.wait_ge(yT_ready, TT * (b + 1))
                    for t in range(TT):
                        last = wide(side_by_token[:, t, :], yT[:, 128 * t:128 * t + 128], wp[:, :])
                elif what == "max":
                    pe.wait_ge(max_parts_ready, group + 1)
                    for t in range(TT):
                        last = wide(ps_side[MROW:KROWS, 128 * t:128 * t + 128], max_parts[:, t, :], res.ident[:, :])
                last.then_inc(side_ready, 1)

            def score_for_max(group, i, t, count):
                wait(pe, max_done, count - 2)
                wide(ps_max[t % 2][:, :], q_op[group][0:MROW, 128 * t:128 * t + 128], k_head[group][i][0:MROW, :])\
                    .then_inc(max_scores, 1)

            def operands(b, group, i):
                pe.wait_ge(q_loaded[group], PARTS * 16 * (b + 1))
                pe.wait_ge(k_masked, HG * (NG * b + group) + i + 1)

            def score_for_exp(b, s, j):
                g, t = s // TT, s % TT
                wait(pe, exp_done, pairs(b, s, j) - 2)
                for i in (2 * j, 2 * j + 1):
                    last = wide(ps_exp[j][:, i % 2, :], k_head[g][i][0:KROWS, 128 * t:128 * t + 128], q_op[g][0:KROWS, :])
                last.then_inc(exp_scores, 1)

            def weigh_values(b, par, s):
                g, t = s // TT, s % TT
                if t == 0:
                    wait(pe, y_evacuated, NG * b + g)
                for i in range(HG):
                    if i % 2 == 0:
                        pe.wait_ge(exp_done, pairs(b, s, i // 2))
                    last = pe.matmul(ps_y[VW * i:VW * i + VW, :], v_aug[par][:, t, HG * g + i, :], probs[s % 2][:, i, :],
                                     start=(t == 0), stop=(t == TT - 1))
                last.then_inc(pv_done, 1)

            pe.wait_ge(loaded, LOADS)
            for n in range(5):
                to_side(HEAD_SIDE[n], 0, 0, n)
            for n in range(AHEAD):
                operands(0, n // HG, n % HG)
                for t in range(TT):
                    score_for_max(n // HG, n % HG, t, TT * n + t + 1)
                to_side(HEAD_SIDE[5 + n], 0, 0, 5 + n)
            to_side("down", 0, 0, 11)
            to_side("max", 0, 0, 12)

            def one(b, par):
                first = isinstance(b, int) and b == 0
                for s in range(STEPS):
                    def tile_max(t):
                        if has_max(b, s):
                            following, group, i = max_head(b, s)
                            if t == 0:
                                operands(b + 1 if following else b, group, i)
                            score_for_max(group, i, t, max_tiles(b, s, t))

                    if s % TT == 0:
                        at = side(b, s - 2) if s else side(b, 0) - (1 if first else 2)
                        pe.wait_ge(side_free, at + 1)
                    score_for_exp(b, s, 0)
                    tile_max(0)
                    if s:
                        weigh_values(b, par, s - 1)
                    elif not first:
                        weigh_values(b - 1, 1 - par, STEPS - 1)
                    tile_max(1)
                    score_for_exp(b, s, 1)
                    tile_max(2)
                    if has_side(b, s):
                        what = SIDE[s]
                        if what == "proj":
                            to_side(what, b - 1, 1 - par, side(b, s))
                        elif what == "max":
                            to_side(what, b, par, side(b, s), NG * b + s // HG + 1)
                        else:
                            to_side(what, b + 1, 1 - par, side(b, s))
                    tile_max(3)

            one.engine = pe
            bodies(one)
            weigh_values(B - 1, (B - 1) % 2, STEPS - 1)
            to_side("proj", B - 1, (B - 1) % 2, side(B - 1, STEPS))



BF16 = mybir.dt.bfloat16

L = 1024
TAPS = 64
FT = L // 2 // 128
E, F = 8, 512
FE = F // 128
KPAD = 128
CG = 4


def transform_tables():
    f = np.arange(L // 2 + 1)
    j = np.arange(1, TAPS + 1)[:, None]
    fwd = np.stack([np.cos(2 * np.pi * j * f / L), -np.sin(2 * np.pi * j * f / L)], 1)
    t = T - 1 - np.arange(T)
    w = np.where(np.arange(L // 2) == 0, 1.0, 2.0)[:, None] / L
    ang = 2 * np.pi * ((np.arange(L // 2)[:, None] * t) % L) / L
    inv = np.stack([w * np.cos(ang), -w * np.sin(ang)], 0).reshape(2, FT, 128, T).transpose(2, 0, 1, 3)
    nyq = ((-1.0) ** t / L)[None, :]
    return fwd.astype(np.float32), np.ascontiguousarray(inv).astype(np.float32), nyq.astype(np.float32)


N_TOK = B * T
UNIT = 256
REGION = N_TOK + UNIT
ROW = C + 4
MAX_UNITS = 2 * N_TOK // UNIT + E
SORTED = E * REGION + MAX_UNITS * UNIT
Y_ROWS = 2 * N_TOK + E * UNIT


def place_tables():
    p = np.arange(128)[:, None]
    fill = np.arange(E * UNIT // 128)[None, :]
    parts = (np.tile(np.arange(E), (128, 1)), np.tile(np.arange(E) * REGION, (128, 1)), 128 * np.arange(B * TT)[None, :] + p,
             2 * N_TOK + 128 * fill + p)
    return np.concatenate(parts, 1).astype(np.float32)


def earlier():
    return np.stack([np.triu(np.ones((128, 128)), 1), np.ones((128, 128))], 1).astype(np.float32)


class ExpertWeights:

    def __init__(self, nc, ctx):
        self.w1 = ctx.enter_context(nc.sbuf_tensor("w1", [C, E, F], FP32))
        self.w2 = ctx.enter_context(nc.sbuf_tensor("w2", [128, E, FE, C], FP32))
        self.b1 = ctx.enter_context(nc.sbuf_tensor("b1", [128, E, FE], FP32))
        self.b2 = ctx.enter_context(nc.sbuf_tensor("b2", [128, E, C], FP32))
        self.loaded = ctx.enter_context(nc.semaphore("weights_loaded"))
        self.LOADS = 16 * 4

    def load(self, sp, dram):
        sp.dma_start(self.w1[:, :, :], dram["w1T"]).then_inc(self.loaded, 16)
        sp.dma_start(self.w2[:, :, :, :], dram["w2T"]).then_inc(self.loaded, 16)
        sp.dma_start(self.b1[:, :, :], dram["b1T"]).then_inc(self.loaded, 16)
        sp.dma_start(self.b2[:, :, :], dram["b2"].rearrange("(a e) c -> a e c", a=1).broadcast_to([128, E, C])).then_inc(self.loaded, 16)


def route_and_convolve(nc, res, dram, s_all, weights):
    with ExitStack() as ctx:
        def sb(name, shape, dt=FP32):
            return ctx.enter_context(nc.sbuf_tensor(name, shape, dt))

        def ps(name, shape):
            return ctx.enter_context(nc.psum_tensor(name, shape, FP32))

        def sem(name):
            return ctx.enter_context(nc.semaphore(name))

        taps = sb("taps", [TAPS, 2 * C])
        fwd = sb("fwd", [TAPS, 2, L // 2 + 1])
        room = s_all[:, :, :].rearrange("p t c -> p (t c)")
        inv = room[:, 0:2 * FT * T].rearrange("p (i f t) -> p i f t", i=2, f=FT)
        nyq_row = sb("nyq_row", [1, T])
        h0 = sb("h0", [C, 1])
        room = room[:, 2 * FT * T:]
        spec = room[:, 0:4 * FT * C].rearrange("p (f r s c) -> p f r s c", f=FT, r=2, s=2)
        nyq = sb("nyq", [1, 2, C])
        norm = sb("norm", [128, FT, C])
        prod = [room[:, (4 + n) * FT * C:(5 + n) * FT * C].rearrange("p (f c) -> p f c", f=FT) for n in range(4)]
        ratio = sb("ratio", [128, 2, FT, C]); nyq_ratio = sb("nyq_ratio", [1, C])
        k_pad = sb("k_pad", [C, KPAD + T])
        loaded, transformed, spec_copied, div_step, divided = (sem(n) for n in ("f_loaded", "transformed", "spec_copied", "div_step", "divided"))
        inverted, k_ready, k_stored = sem("inverted"), sem("k_ready"), sem("k_stored")
        ps_nyq = ps("ps_nyq", [128, T])
        ps_k = ps_nyq

        NQ = C // CG
        toep = [sb(f"toep{p}", [128, CG, T]) for p in range(2)]
        inputs = [sb(f"conv_in{p}", [128, TT // 2, CG, 2, B]) for p in range(2)]
        by_time = [sb(f"by_time{p}", [128, T]) for p in range(2)]
        ps_conv = ps("ps_conv", [128, 4, 512])
        ps_t = [ps_conv[:, p, :] for p in range(2)]
        ps_b = [ps_conv[:, 2 + p, :].rearrange("p (t c b) -> p t c b", t=TT, c=CG) for p in range(2)]
        ps_spec = ps_conv[:, :, :].rearrange("p f (r s) -> p f r s", r=2)
        toep_loaded = [sem(f"toep_loaded{p}") for p in range(2)]
        evens_out, picked_in, convolved, time_copied, time_turned, spread = (
            sem(n) for n in ("evens_out", "picked", "convolved", "by_time_copied", "turned", "spread"))

        units = sb("units", [128, E + 1], INT32)
        fill_starts = sb("fill_starts", [128, E], INT32)
        units_ready, ends = sem("units_ready"), {}
        FILL = E * UNIT // 128
        rw = sb("rw", [C, E])
        tables = sb("tables", [128, 2 * E + B * TT + FILL])
        before_f, before = sb("before_f", [128, 2, 128]), sb("before", [128, 2, 128], BF16)
        numbers, regions = tables[:, 0:E], tables[:, E:2 * E]
        token_numbers = tables[:, 2 * E:2 * E + B * TT]
        fill_numbers = tables[:, 2 * E + B * TT:]
        rows = [[sb(f"rows{k}_{p}", [128, TT, ROW]) for p in range(2)] for k in range(2)]
        xn_now = [sb(f"xn_now{p}", [128, TT, C]) for p in range(2)]
        xnT_now = [sb(f"xnT_now{p}", [128, T]) for p in range(2)]
        logits = sb("logits", [128, TT, E])
        top, top_at = sb("top", [128, TT, 8]), sb("top_at", [128, TT, 8], mybir.dt.uint32)
        choice = sb("choice", [128, TT, 2])
        gap = [sb(f"gap{p}", [128, TT, 1]) for p in range(2)]
        gap_sum = sb("gap_sum", [128, TT, 1])
        hot = [sb(f"hot{k}", [128, TT, E]) for k in range(2)]
        hot_both = sb("hot_both", [128, TT, E], BF16)
        taken = [sb(f"taken{p}", [128, E]) for p in range(2)]
        rank = sb("rank", [128, TT, E])
        picked = [sb(f"picked{k}", [128, TT, E]) for k in range(2)]
        place_f = [sb(f"place_f{k}", [128, TT]) for k in range(2)]
        place = [[sb(f"place{k}_{p}", [128, TT], mybir.dt.uint32) for p in range(2)] for k in range(2)]
        fill_rows = sb("fill_rows", [128, FILL, ROW])
        count_f, count = sb("count_f", [128, E]), sb("count", [128, E], INT32)
        sums = [sb(f"sums{p}", [128, E], INT32) for p in range(2)]
        ps_x, ps_s = ps("ps_x", [128, T]), ps("ps_s", [128, TT, E])
        ps_rank = ps("ps_rank", [128, TT + 1, E])
        r_loaded, cleared, rows_ready, x_turned, x_copied, scored = (sem(n) for n in ("r_loaded", "rows_cleared", "rows_ready", "x_turned", "x_copied", "scored"))
        step, gap_ready, gap_exp, hot_ready, ranked, placed = (sem(n) for n in ("route_step", "gap_ready", "gap_exp", "hot_ready", "ranked", "placed"))
        fill_placed, fill_step, fill_stored = sem("fill_placed"), sem("fill_step"), sem("fill_stored")
        now_ready, act_passed = sem("now_ready"), sem("act_passed")
        scattered = [sem(f"scattered{p}") for p in range(2)]
        max_passed, pool_passed = sem("max_passed"), sem("pool_passed")
        STEPS_R = 10
        SCATTERS = 2 * TT
        block = ctx.enter_context(nc.Block())

        def wait(eng, s, v):
            if not isinstance(v, int) or v > 0:
                eng.wait_ge(s, v)

        def tiles(b):
            return slice(TT * b, TT * b + TT) if isinstance(b, int) else bass.ds(TT * b, TT)

        def at(q):
            return slice(CG * q, CG * q + CG) if isinstance(q, int) else bass.ds(CG * q, CG)

        def fill(eng, experts):
            eng.wait_ge(fill_placed, 1)
            for e in experts:
                start = eng.value_load(fill_starts[0:1, e:e + 1], min_val=e * REGION, max_val=e * REGION + N_TOK)
                eng.dma_start(dram["sorted"][bass.ds(start, UNIT), :].rearrange("(j p) c -> p j c", p=128), fill_rows[:, 2 * e:2 * e + 2, :])\
                   .then_inc(fill_stored, 16)

        def load_ends(eng):
            eng.wait_ge(units_ready, 1)
            ends[eng] = [eng.value_load(units[0:1, e:e + 1], min_val=e, max_val=MAX_UNITS) for e in range(E + 1)]

        def bodies(eng, one):
            with eng.Fori(1, B // 2 - 1) as n:
                one(2 * n, 0)
                one(2 * n + 1, 1)
            one(B - 2, 0)
            one(B - 1, 1)

        @block.sync
        def _(sp):
            sp.dma_start(rw[:, :], dram["rwT"]).then_inc(r_loaded, 16)
            sp.dma_start(tables[:, :], dram["place_tables"]).then_inc(r_loaded, 16)
            sp.dma_start(before_f[:, :, :], dram["earlier"]).then_inc(r_loaded, 16)
            sp.dma_start(taps[:, :], dram["abT"]).then_inc(loaded, 16)
            sp.dma_start(fwd[:, :, :], dram["fwd"]).then_inc(loaded, 16)
            sp.dma_start(nyq_row[:, :], dram["nyq"]).then_inc(loaded, 16)
            sp.dma_start(h0[:, :], dram["h0"].rearrange("(c a) -> c a", a=1)).then_inc(loaded, 16)
            sp.dma_start(inv[:, :, :, :], dram["inv"]).then_inc(loaded, 16)
            sp.wait_ge(k_ready, 1)
            sp.dma_start(dram["k_pad"], k_pad[:, :]).then_inc(k_stored, 16)
            sp.wait_ge(k_stored, 16)

            def one(q, p):
                wait(sp, convolved, q - 1)
                src = bass.AP(dram["k_pad"].tensor, CG * (KPAD + T) * q, [[1, 128], [KPAD + T, CG], [1, T]])
                sp.dma_start(toep[p][:, :, :], src).then_inc(toep_loaded[p], 16)

            one(0, 0)
            one(1, 1)
            weights.load(sp, dram)
            with sp.Fori(1, NQ // 2) as n:
                one(2 * n, 0)
                one(2 * n + 1, 1)
            fill(sp, range(E // 2))
            load_ends(sp)
            sp.wait_ge(fill_stored, 16 * E)

        @block.scalar
        def _(act):
            act.wait_ge(cleared, 1)

            def fetch_now(b, p):
                wait(act, x_turned, b - 1)
                apart(act, act_passed)
                act.activation(xn_now[p][:, :, :], res.xn[:, tiles(b), :], ACT.Copy).then_inc(now_ready, 1)

            def fetch_rows(b, p):
                if not isinstance(b, int) or b >= 2:
                    act.wait_ge(scattered[p], 8 * SCATTERS * (b - p))
                    apart(act, act_passed)
                for k in range(2):
                    last = act.activation(rows[k][p][:, :, 0:C], res.xn[:, tiles(b), :], ACT.Copy)
                last.then_inc(rows_ready, 1)

            def copy_x(b, p):
                act.wait_ge(x_turned, b + 1)
                act.activation(xnT_now[p][:, :], ps_x[:, :], ACT.Copy).then_inc(x_copied, 1)

            def exp(b, p):
                act.wait_ge(gap_ready, b + 1)
                act.activation(gap[p][:, :, :], gap[p][:, :, :], ACT.Exp).then_inc(gap_exp, 1)

            def reverse(q, p):
                act.wait_ge(convolved, q + 1)
                wait(act, time_turned, q - 1)
                act.activation(by_time[p][:, :], ps_t[p][:, ::-1], ACT.Copy).then_inc(time_copied, 1)

            for b in range(2):
                fetch_now(b, b)
                copy_x(b, b)
                exp(b, b)
                fetch_rows(b, b)
                if b == 0:
                    act.wait_ge(transformed, 1)
                    act.activation(spec[:, :, :, :, :].rearrange("p f r s c -> p (f r s c)"),
                                   ps_spec[:, :, :, :].rearrange("p f r s -> p (f r s)"), ACT.Copy)
                    act.activation(nyq[:, :, :].rearrange("p s c -> p (s c)"), ps_nyq[0:1, 0:2 * C], ACT.Copy).then_inc(spec_copied, 1)
            for q in range(4):
                reverse(q, q % 2)

            def one(b, par):
                fetch_now(b, par)
                copy_x(b, par)
                reverse(2 * b, 0)
                exp(b, par)
                reverse(2 * b + 1, 1)
                fetch_rows(b, par)

            bodies(act, one)
            fill(act, range(E // 2, E))
            load_ends(act)

        @block.tensor
        def _(pe):
            def turn_x(b, p):
                pe.wait_ge(now_ready, b + 1)
                wait(pe, x_copied, b)
                for t in range(TT):
                    last = pe.transpose(ps_x[:, 128 * t:128 * t + 128], xn_now[p][:, t, :], res.ident[:, :])
                last.then_inc(x_turned, 1)

            def score(b, p):
                pe.wait_ge(x_copied, b + 1)
                wait(pe, hot_ready, b)
                for t in range(TT):
                    last = pe.matmul(ps_s[:, t, :], xnT_now[p][:, 128 * t:128 * t + 128], rw[:, :], start=True, stop=True)
                last.then_inc(scored, 1)

            def rank_tokens(b):
                pe.wait_ge(hot_ready, b + 1)
                for t in range(TT):
                    pe.matmul(ps_rank[:, t, :], before[:, 0, :], hot_both[:, t, :], start=True, stop=(t == 0))
                    for u in range(t):
                        pe.matmul(ps_rank[:, t, :], before[:, 1, :], hot_both[:, u, :], start=False, stop=(u == t - 1))
                for t in range(TT):
                    last = pe.matmul(ps_rank[:, TT, :], before[:, 1, :], hot_both[:, t, :], start=(t == 0), stop=(t == TT - 1))
                last.then_inc(ranked, 1)

            def product(q, p):
                pe.wait_ge(picked_in, q + 1)
                pe.wait_ge(toep_loaded[p], 16 * (q // 2 + 1) if isinstance(q, int) else 8 * (q - p) + 16)
                wait(pe, time_copied, q - 1)
                for u in range(TT // 2):
                    for i in range(CG):
                        last = pe.matmul(ps_t[p][32 * i:32 * i + 32, 0:T - 256 * u], inputs[p][:, u, i, :, :].rearrange("p h b -> p (h b)"),
                                         toep[p][:, i, 256 * u:], start=(u == 0), stop=(u == TT // 2 - 1))
                last.then_inc(convolved, 1)

            def turn(q, p):
                pe.wait_ge(time_copied, q + 1)
                wait(pe, spread, q - 1)
                for t in range(TT):
                    last = pe.transpose(ps_b[p][:, t, :, :].rearrange("p c b -> p (c b)"), by_time[p][:, 128 * t:128 * t + 128], res.ident[:, :])
                last.then_inc(time_turned, 1)

            pe.wait_ge(r_loaded, 48)
            turn_x(0, 0)
            score(0, 0)
            pe.wait_ge(loaded, 80)
            for f in range(FT):
                for part in range(2):
                    pe.matmul(ps_spec[:, f, part, :], fwd[:, part, 128 * f:128 * f + 128], taps[:, :], start=True, stop=True)
            pe.matmul(ps_nyq[0:1, 0:2 * C], fwd[:, 0, L // 2:L // 2 + 1], taps[:, :], start=True, stop=True).then_inc(transformed, 1)
            rank_tokens(0)
            turn_x(1, 1)
            score(1, 1)
            pe.wait_ge(divided, 1)
            for f in range(FT):
                for part in range(2):
                    pe.matmul(ps_k[:, :], ratio[:, part, f, :], inv[:, part, f, :], start=(f == 0 and part == 0), stop=False)
            pe.matmul(ps_k[:, :], nyq_ratio[0:1, :], nyq_row[0:1, :], start=False, stop=True).then_inc(inverted, 1)
            rank_tokens(1)
            for q in range(4):
                product(q, q % 2)
            turn(0, 0)
            turn(1, 1)

            def one(b, par):
                product(2 * b, 0)
                turn_x(b, par)
                product(2 * b + 1, 1)
                score(b, par)
                turn(2 * b - 2, 0)
                turn(2 * b - 1, 1)
                rank_tokens(b)

            bodies(pe, one)
            turn(NQ - 2, 0)
            turn(NQ - 1, 1)
            load_ends(pe)

        @block.vector
        def _(dve):
            xn = res.xn[:, :, :].rearrange("p (b t) c -> p t b c", b=B)
            s_out = s_all[:, :, :].rearrange("p (b t) c -> p t b c", b=B)

            def pick(q, p):
                wait(dve, convolved, q - 1)
                for t in range(TT):
                    last = dve.tensor_copy(inputs[p][:, t // 2, :, t % 2, :].rearrange("p c b -> p b c"), xn[:, t, :, at(q)])
                last.then_inc(picked_in, 1)

            def out(q, p):
                dve.wait_ge(time_turned, q + 1)
                for t in range(TT):
                    last = dve.tensor_copy(s_out[:, t, :, at(q)], ps_b[p][:, t, :, 0:B].rearrange("p c b -> p b c"))
                last.then_inc(evens_out, 1)
                dve.wait_ge(evens_out, q + 1)
                for t in range(1, TT):
                    last = dve.tensor_tensor(s_out[:, t, :, at(q)], ps_b[p][:, t - 1, :, B:].rearrange("p c b -> p b c"), s_out[:, t, :, at(q)], ALU.add)
                last.then_inc(spread, 1)

            for k in range(2):
                for p in range(2):
                    last = dve.memset(rows[k][p][:, :, C:], 0.0)
            last.then_inc(cleared, 1)
            dve.memset(fill_rows[:, :, :], 0.0).then_inc(fill_step, 1)
            dve.wait_ge(r_loaded, 48)
            dve.wait_ge(fill_step, 1)
            dve.tensor_copy(before[:, :, :], before_f[:, :, :])
            dve.tensor_copy(fill_rows[:, :, C], fill_numbers)
            dve.tensor_copy(taken[0][:, :], regions).then_inc(fill_step, 1)
            dve.wait_ge(fill_step, 2)
            wide = [128, TT, E]

            def step_done(ins, b, n):
                ins.then_inc(step, 1)
                dve.wait_ge(step, STEPS_R * b + n)

            def choose(b, p):
                dve.wait_ge(scored, b + 1)
                step_done(dve.tensor_copy(logits[:, :, :], ps_s[:, :, :]), b, 1)
                apart(dve, max_passed)
                for t in range(TT):
                    last = dve.max(top[:, t, :], logits[:, t, :])
                step_done(last, b, 2)
                apart(dve, max_passed)
                for t in range(TT):
                    last = dve.max_index(top_at[:, t, :], top[:, t, :], logits[:, t, :])
                step_done(last, b, 3)
                dve.tensor_tensor(gap[p][:, :, :], top[:, :, 1:2], top[:, :, 0:1], ALU.subtract).then_inc(gap_ready, 1)
                step_done(dve.tensor_copy(choice[:, :, :], top_at[:, :, 0:2]), b, 4)
                for k in range(2):
                    last = dve.tensor_tensor(hot[k][:, :, :], numbers[:, None, :].broadcast_to(wide), choice[:, :, k:k + 1].broadcast_to(wide), ALU.is_equal)
                step_done(last, b, 5)
                dve.tensor_tensor(hot_both[:, :, :], hot[0][:, :, :], hot[1][:, :, :], ALU.add).then_inc(hot_ready, 1)

            def place_tokens(b, p):
                if not isinstance(b, int) or b >= 2:
                    dve.wait_ge(scattered[p], 8 * SCATTERS * (b - p))
                for k in range(2):
                    dve.tensor_scalar(rows[k][p][:, :, C], token_numbers[:, tiles(b)], float(k * N_TOK), None, ALU.add)
                dve.wait_ge(gap_exp, b + 1)
                step_done(dve.tensor_scalar(gap_sum[:, :, :], gap[p][:, :, :], 1.0, None, ALU.add), b, 6)
                step_done(dve.reciprocal(rows[0][p][:, :, C + 1:C + 2], gap_sum[:, :, :]), b, 7)
                dve.tensor_tensor(rows[1][p][:, :, C + 1:C + 2], gap[p][:, :, :], rows[0][p][:, :, C + 1:C + 2], ALU.mult)
                dve.wait_ge(ranked, b + 1)
                dve.tensor_tensor(taken[1 - p][:, :], ps_rank[:, TT, :], taken[p][:, :], ALU.add)
                step_done(dve.tensor_tensor(rank[:, :, :], ps_rank[:, 0:TT, :], taken[p][:, None, :].broadcast_to(wide), ALU.add), b, 8)
                for k in range(2):
                    last = dve.tensor_tensor(picked[k][:, :, :], hot[k][:, :, :], rank[:, :, :], ALU.mult)
                step_done(last, b, 9)
                for k in range(2):
                    last = dve.tensor_reduce(place_f[k][:, :], picked[k][:, :, :], AX.X, ALU.add)
                step_done(last, b, 10)
                for k in range(2):
                    last = dve.tensor_copy(place[k][p][:, :], place_f[k][:, :])
                last.then_inc(placed, 1)

            choose(0, 0)
            place_tokens(0, 0)
            divisions = [0]

            def div_done(ins):
                ins.then_inc(div_step, 1)
                divisions[0] += 1
                dve.wait_ge(div_step, divisions[0])

            ar, br, ai, bi = spec[:, :, 0, 0, :], spec[:, :, 0, 1, :], spec[:, :, 1, 0, :], spec[:, :, 1, 1, :]
            p = [x[:, :, :] for x in prod]
            dve.memset(k_pad[:, T:], 0.0)
            dve.wait_ge(spec_copied, 1)
            dve.tensor_scalar(nyq[:, 0, :], nyq[:, 0, :], 1.0, None, ALU.add)
            div_done(dve.tensor_scalar(ar, ar, 1.0, None, ALU.add))
            dve.reciprocal(nyq[:, 0, :], nyq[:, 0, :])
            dve.tensor_tensor(p[0], ar, ar, ALU.mult)
            div_done(dve.tensor_tensor(p[1], ai, ai, ALU.mult))
            dve.tensor_tensor(nyq_ratio[:, :], nyq[:, 0, :], nyq[:, 1, :], ALU.mult)
            div_done(dve.tensor_tensor(norm[:, :, :], p[0], p[1], ALU.add))
            dve.tensor_tensor(p[0], br, ar, ALU.mult)
            dve.tensor_tensor(p[1], bi, ai, ALU.mult)
            dve.tensor_tensor(p[2], bi, ar, ALU.mult)
            dve.tensor_tensor(p[3], br, ai, ALU.mult)
            div_done(dve.reciprocal(norm[:, :, :], norm[:, :, :]))
            dve.tensor_tensor(p[0], p[0], p[1], ALU.add)
            div_done(dve.tensor_tensor(p[2], p[2], p[3], ALU.subtract))
            dve.tensor_tensor(ratio[:, 0, :, :], p[0], norm[:, :, :], ALU.mult)
            dve.tensor_tensor(ratio[:, 1, :, :], p[2], norm[:, :, :], ALU.mult).then_inc(divided, 1)
            choose(1, 1)
            dve.wait_ge(inverted, 1)
            dve.tensor_tensor(k_pad[:, T - 1:T], ps_k[:, T - 1:T], h0[:, :], ALU.add)
            dve.tensor_copy(k_pad[:, 0:T - 1], ps_k[:, 0:T - 1]).then_inc(k_ready, 1)
            place_tokens(1, 1)
            for q in range(6):
                pick(q, q % 2)

            def one(b, par):
                out(2 * b - 4, 0)
                out(2 * b - 3, 1)
                choose(b, par)
                if not (isinstance(b, int) and b == B - 1):
                    pick(2 * b + 2, 0)
                    pick(2 * b + 3, 1)
                place_tokens(b, par)

            bodies(dve, one)
            def done(ins, n):
                ins.then_inc(fill_step, 1)
                dve.wait_ge(fill_step, n)

            dve.wait_ge(placed, B)
            dve.tensor_tensor(count_f[:, :], taken[0][:, :], regions, ALU.subtract).then_inc(fill_step, 1)
            dve.tensor_copy(fill_starts[:, :], taken[0][:, :]).then_inc(fill_placed, 1)
            dve.wait_ge(fill_step, 3)
            done(dve.tensor_scalar(count_f[:, :], count_f[:, :], 1.0, float(UNIT - 1), ALU.max, ALU.add), 4)
            done(dve.tensor_copy(count[:, :], count_f[:, :]), 5)
            done(dve.tensor_scalar(sums[0][:, :], count[:, :], UNIT.bit_length() - 1, None, ALU.logical_shift_right), 6)
            for i, shift in enumerate((1, 2, 4)):
                old, new = sums[i % 2], sums[(i + 1) % 2]
                dve.tensor_copy(new[:, 0:shift], old[:, 0:shift])
                done(dve.tensor_tensor(new[:, shift:], old[:, shift:], old[:, 0:E - shift], ALU.add), 7 + i)
            dve.memset(units[:, 0:1], 0)
            dve.tensor_copy(units[:, 1:], sums[1][:, :]).then_inc(units_ready, 1)
            for q in range(NQ - 4, NQ):
                out(q, q % 2)
            load_ends(dve)

        @block.gpsimd
        def _(pool):
            def scatter(b, p):
                pool.wait_ge(rows_ready, b + 1)
                pool.wait_ge(placed, b + 1)
                apart(pool, pool_passed)
                for k in range(2):
                    for t in range(TT):
                        pool.indirect_dma_start(dram["sorted"], bass.IndirectOffsetOnAxis(place[k][p][:, t:t + 1], 0), rows[k][p][:, t, :], None)\
                            .then_inc(scattered[p], 16)

            scatter(0, 0)
            scatter(1, 1)
            with pool.Fori(1, B // 2) as n:
                scatter(2 * n, 0)
                scatter(2 * n + 1, 1)
            for p in range(2):
                pool.wait_ge(scattered[p], 16 * SCATTERS * B // 2)
            load_ends(pool)

        return ends


def experts(nc, res, dram, ends, weights):
    with ExitStack() as ctx:
        def sb(name, shape, dt=FP32):
            return ctx.enter_context(nc.sbuf_tensor(name, shape, dt))

        def sem(name):
            return ctx.enter_context(nc.semaphore(name))

        w1, w2, b1, b2 = weights.w1, weights.w2, weights.b1, weights.b2
        rows = [sb(f"unit_rows{i}", [128, ROW]) for i in range(2)]
        xT = sb("unit_xT", [C, UNIT])
        tails = sb("tails", [128, 2 * MAX_UNITS + 2, 2])
        hidden = sb("hidden", [128, FE, UNIT])
        biased = [sb(f"biased{i}", [128, C]) for i in range(2)]
        result = [sb(f"result{i}", [128, C]) for i in range(2)]
        goes_to = [sb(f"goes_to{i}", [128, 1], mybir.dt.uint32) for i in range(2)]
        ps_x = ctx.enter_context(nc.psum_tensor("ps_unit_x", [128, UNIT], FP32))
        ps_h = [ctx.enter_context(nc.psum_tensor(f"ps_h{f}", [128, 512], FP32)) for f in range(FE)]
        ps_o = [ctx.enter_context(nc.psum_tensor(f"ps_o{i}", [128, 512], FP32)) for i in range(2)]
        x_loaded, turned, copied = sem("unit_loaded"), sem("unit_turned"), sem("unit_copied")
        h_scores, h_ready = sem("h_scores"), sem("h_ready2")
        o_ready, biased_ready, result_ready = ([sem(f"{n}{i}") for i in range(2)] for n in ("o_ready", "biased_ready", "result_ready"))
        stored = [sem(f"y_stored{i}") for i in range(2)]
        pool_passed = sem("pool_passed2")
        block = ctx.enter_context(nc.Block())

        def over_units(eng, one):
            first = ends[eng]
            for e in range(E):
                with eng.Fori(first[e], first[e + 1]) as n:
                    one(e, n)
            return first[E]


        @block.sync
        def _(sp):
            def load(row):
                for i in range(2):
                    at = slice(row + 128 * i, row + 128 * i + 128) if isinstance(row, int) else bass.ds(row + 128 * i, 128)
                    sp.dma_start(rows[i][:, :], dram["sorted"][at, :]).then_inc(x_loaded, 16)

            first = ends[sp]
            for e in range(E):
                with sp.Fori(0, first[e + 1] - first[e]) as i:
                    sp.wait_ge(copied, first[e] + i + 1)
                    load(i * UNIT + e * REGION)
            sp.wait_ge(copied, first[E] + 1)
            load(0)

        @block.tensor
        def _(pe):
            def turn(n):
                pe.wait_ge(x_loaded, 2 * 16 * (n + 1))
                for i in range(2):
                    last = pe.transpose(ps_x[:, 128 * i:128 * i + 128], rows[i][:, 0:C], res.ident[:, :])
                last.then_inc(turned, 1)

            def one(e, n):
                pe.wait_ge(copied, n + 2)
                for f in range(FE):
                    pe.wait_ge(h_ready, FE * n + f + 1)
                    pe.matmul(ps_h[f][:, 0:UNIT], w1[:, e, 128 * f:128 * f + 128], xT[:, :], start=True, stop=True).then_inc(h_scores, 1)
                turn(n + 1)
                for i in range(2):
                    pe.wait_ge(biased_ready[i], n + 1)
                    for f in range(FE):
                        if i == 0:
                            pe.wait_ge(h_ready, FE * (n + 1) + f + 1)
                        last = pe.matmul(ps_o[i][:, 0:C], hidden[:, f, 128 * i:128 * i + 128], w2[:, e, f, :],
                                         start=(f == 0), stop=(f == FE - 1))
                    last.then_inc(o_ready[i], 1)

            turn(0)
            pe.wait_ge(weights.loaded, weights.LOADS)
            over_units(pe, one)

        @block.scalar
        def _(act):
            act.sem_inc(h_ready, FE)
            act.wait_ge(weights.loaded, weights.LOADS)

            def one(e, n):
                for f in range(FE):
                    act.wait_ge(h_scores, FE * n + f + 1)
                    act.activation(hidden[:, f, :], ps_h[f][:, 0:UNIT], ACT.Gelu, bias=b1[:, e, f:f + 1]).then_inc(h_ready, 1)

            over_units(act, one)

        @block.vector
        def _(dve):
            dve.sem_inc(copied, 1)
            for i in range(2):
                dve.sem_inc(biased_ready[i], 1)
            dve.wait_ge(weights.loaded, weights.LOADS)

            def keep(n):
                dve.wait_ge(turned, n + 1)
                dve.tensor_copy(xT[:, :], ps_x[:, :])
                for i in range(2):
                    at = slice(i, i + 1) if isinstance(n, int) else bass.ds(2 * n + i, 1)
                    last = dve.tensor_copy(tails[:, at, :].rearrange("p a c -> p (a c)"), rows[i][:, C:C + 2])
                last.then_inc(copied, 1)

            def one(e, n):
                keep(n + 1)
                for i in range(2):
                    dve.wait_ge(o_ready[i], n + 1)
                    dve.tensor_tensor(biased[i][:, :], ps_o[i][:, 0:C], b2[:, e, :], ALU.add).then_inc(biased_ready[i], 1)
                    dve.wait_ge(stored[i], 16 * (n + 1))
                    dve.tensor_copy(goes_to[i][:, :], tails[:, bass.ds(2 * n + i, 1), 0:1].rearrange("p a c -> p (a c)"))
                    dve.wait_ge(biased_ready[i], n + 2)
                    dve.tensor_scalar(result[i][:, :], biased[i][:, :], tails[:, bass.ds(2 * n + i, 1), 1:2].rearrange("p a c -> p (a c)"), None, ALU.mult)\
                       .then_inc(result_ready[i], 1)

            keep(0)
            over_units(dve, one)

        @block.gpsimd
        def _(pool):
            for i in range(2):
                pool.dma_start(result[i][:, :], dram["ident"]).then_inc(stored[i], 16)

            def one(e, n):
                for i in range(2):
                    pool.wait_ge(result_ready[i], n + 1)
                    apart(pool, pool_passed)
                    pool.indirect_dma_start(dram["y"], bass.IndirectOffsetOnAxis(goes_to[i][:, 0:1], 0), result[i][:, :], None)\
                        .then_inc(stored[i], 16)

            total = over_units(pool, one)
            for i in range(2):
                pool.wait_ge(stored[i], 16 * total + 16)


def combine(nc, res, dram, s_all):
    with ExitStack() as ctx:
        def sb(name, shape, dt=FP32):
            return ctx.enter_context(nc.sbuf_tensor(name, shape, dt))

        def sem(name):
            return ctx.enter_context(nc.semaphore(name))

        y = [[sb(f"y{k}_{p}", [128, TT, C]) for p in range(2)] for k in range(2)]
        mixed = [sb(f"mixed{p}", [128, TT, C]) for p in range(2)]
        gate, s_gated = ([sb(f"{n}{p}", [128, TT, C]) for p in range(2)] for n in ("tanh_m", "s_gated"))
        out_now = [sb(f"out_now{p}", [128, TT, C]) for p in range(2)]
        mixed_ready, tanh_ready, gate_ready, s_ready, out_ready = (sem(n) for n in ("mixed_ready", "mix_tanh", "mix_gate", "s_gated_ready", "out_ready"))
        y_loaded = [sem(f"y_loaded{p}") for p in range(2)]
        stored = [sem(f"out_stored{p}") for p in range(2)]
        block = ctx.enter_context(nc.Block())

        def tiles(b):
            return slice(TT * b, TT * b + TT) if isinstance(b, int) else bass.ds(TT * b, TT)

        def bodies(eng, one):
            one(0, 0)
            one(1, 1)
            with eng.Fori(1, B // 2) as n:
                one(2 * n, 0)
                one(2 * n + 1, 1)

        @block.sync
        def _(sp):
            y_rows = dram["y"].rearrange("(t p) c -> p t c", p=128)

            def one(b, p):
                if not isinstance(b, int):
                    sp.wait_ge(mixed_ready, b - 1)
                for k in range(2):
                    at = slice(TT * b + k * B * TT, TT * b + k * B * TT + TT) if isinstance(b, int) else bass.ds(TT * b + k * B * TT, TT)
                    sp.dma_start(y[k][p][:, :, :], y_rows[:, at, :]).then_inc(y_loaded[p], 16)

            bodies(sp, one)

        @block.scalar
        def _(act):
            out = dram["out"].rearrange("b (t p) c -> p (b t) c", p=128)

            def tanh(b, p):
                act.wait_ge(mixed_ready, b + 1)
                act.activation(gate[p][:, :, :], mixed[p][:, :, :], ACT.Tanh, scale=0.5).then_inc(tanh_ready, 1)

            def store(b, p):
                act.wait_ge(out_ready, b + 1)
                act.dma_start(out[:, tiles(b), :], out_now[p][:, :, :]).then_inc(stored[p], 16)

            tanh(0, 0)
            tanh(1, 1)
            store(0, 0)
            with act.Fori(1, B // 2) as n:
                tanh(2 * n, 0)
                store(2 * n - 1, 1)
                tanh(2 * n + 1, 1)
                store(2 * n, 0)
            store(B - 1, 1)
            for p in range(2):
                act.wait_ge(stored[p], 16 * B // 2)

        @block.vector
        def _(dve):
            def mix(b, p):
                dve.wait_ge(y_loaded[p], 16 * (b - p) + 32)
                if not isinstance(b, int) or b >= 2:
                    dve.wait_ge(gate_ready, b - 1)
                dve.tensor_tensor(mixed[p][:, :, :], y[0][p][:, :, :], y[1][p][:, :, :], ALU.add).then_inc(mixed_ready, 1)

            def gate_s(b, p):
                dve.wait_ge(tanh_ready, b + 1)
                dve.scalar_tensor_tensor(gate[p][:, :, :], gate[p][:, :, :], 1.0, mixed[p][:, :, :], ALU.add, ALU.mult).then_inc(gate_ready, 1)
                dve.wait_ge(gate_ready, b + 1)
                dve.tensor_tensor(s_gated[p][:, :, :], gate[p][:, :, :], s_all[:, tiles(b), :], ALU.mult).then_inc(s_ready, 1)
                dve.wait_ge(s_ready, b + 1)
                if not isinstance(b, int) or b >= 2:
                    dve.wait_ge(stored[p], 8 * (b - p))
                dve.scalar_tensor_tensor(out_now[p][:, :, :], s_gated[p][:, :, :], 0.5, res.x[:, tiles(b), :], ALU.mult, ALU.add).then_inc(out_ready, 1)

            mix(0, 0)
            mix(1, 1)
            gate_s(0, 0)
            mix(2, 0)
            gate_s(1, 1)
            mix(3, 1)
            gate_s(2, 0)
            with dve.Fori(2, B // 2) as n:
                mix(2 * n, 0)
                gate_s(2 * n - 1, 1)
                mix(2 * n + 1, 1)
                gate_s(2 * n, 0)
            gate_s(B - 1, 1)


def laid_out(inputs):
    def t(a, *axes):
        return np.ascontiguousarray(np.transpose(a, axes or None))

    return {
        "x": inputs["L0_attn_x"],
        "wqT": t(inputs["L0_attn_Wq"]), "wkT": t(inputs["L0_attn_Wk"]), "wvT": t(inputs["L0_attn_Wv"]),
        "wpT": t(inputs["L0_attn_Wp"]),
        "bq": inputs["L0_attn_bq"], "bk": inputs["L0_attn_bk"], "bv": inputs["L0_attn_bv"], "bp": inputs["L0_attn_bp"],
        "level": np.reshape(inputs["L0_attn_resolve_level"], (1,)),
        "wgT": t(inputs["L0_ffn_w_gate"]), "wuT": t(inputs["L0_ffn_w_up"]), "wdT": t(inputs["L0_ffn_w_down"]),
        "abT": t(inputs["L1_attn_ab"]), "h0": inputs["L1_attn_h_0"],
        "rwT": t(inputs["L1_ffn_router_w"]),
        "b1T": t(np.reshape(inputs["L1_ffn_b1"], (E, FE, 128)), 2, 0, 1), "b2": inputs["L1_ffn_b2"],
        "w1T": t(inputs["L1_ffn_w1"], 2, 0, 1),
        "w2T": t(np.reshape(inputs["L1_ffn_w2"], (E, C, FE, 128)), 3, 0, 2, 1),
    }


def build(nc, dram):
    fwd, inv, nyq = transform_tables()
    constants = {
        "mask": head_mask(), "ident": np.eye(128, dtype=np.float32), "value_frame": value_frame(),
        "fwd": fwd, "inv": inv, "nyq": nyq,
        "place_tables": place_tables(), "earlier": earlier(),
    }
    for name, value in constants.items():
        dram[name] = nc.inline_tensor(value, f"const_{name}").ap()
    dram["k_pad"] = nc.dram_tensor("k_pad_scratch", [C, KPAD + T], FP32).ap()
    dram["sorted"] = nc.dram_tensor("sorted_scratch", [SORTED, ROW], FP32).ap()
    dram["y"] = nc.dram_tensor("y_scratch", [Y_ROWS, C], FP32).ap()
    with ExitStack() as ctx:
        res = Resident(nc, ctx)
        layer0(nc, res, dram)
        s_all = ctx.enter_context(nc.sbuf_tensor("s_all", [128, B * TT, C], FP32))
        weights = ExpertWeights(nc, ctx)
        ends = route_and_convolve(nc, res, dram, s_all, weights)
        experts(nc, res, dram, ends, weights)
        combine(nc, res, dram, s_all)


def kernel(**inputs):
    import concourse.bacc as _bacc
    from concourse.bass_utils import run_bass_kernel_spmd as _run

    nc = _bacc.Bacc("TRN2", target_bir_lowering=False, num_devices=1)
    arrays, dram = {}, {}
    for name, value in laid_out({k: np.asarray(v) for k, v in inputs.items()}).items():
        value = np.ascontiguousarray(value)
        arrays[f"in_{name}_dram"] = value
        dram[name] = nc.dram_tensor(f"in_{name}_dram", value.shape, mybir.dt.from_np(value.dtype), kind="ExternalInput").ap()
    dram["out"] = nc.dram_tensor("out_0_dram", (B, T, C), FP32, kind="ExternalOutput").ap()
    build(nc, dram)
    return _run(nc, [arrays], core_ids=[0]).results[0]["out_0_dram"]
```

```python
import numpy as np
import concourse.bass as bass
from concourse import mybir
from contextlib import ExitStack

FP32 = mybir.dt.float32
FP32R = mybir.dt.float32r
INT32 = mybir.dt.int32
ALU = mybir.AluOpType
ACT = mybir.ActivationFunctionType
AX = mybir.AxisListType

B, T, C = 16, 512, 128
TT = T // 128
EPS = 1e-5

H, HD = 16, 8
HG = 4
NG = H // HG
GR = HG * HD
PARTS = 3
MROW = PARTS * GR
KROWS = MROW + 2 * HG
VW = 32
FFN = 384
FC = FFN // 128
STEPS = NG * TT
AHEAD = 6


class Resident:

    def __init__(self, nc, ctx):
        self.x = ctx.enter_context(nc.sbuf_tensor("x_all", [128, B * TT, C], FP32))
        self.xn = ctx.enter_context(nc.sbuf_tensor("xn_all", [128, B * TT, C], FP32))
        self.ident = ctx.enter_context(nc.sbuf_tensor("ident", [128, 128], FP32))


def head_mask():
    m = np.zeros((128, HG), np.float32)
    for i in range(HG):
        for part in range(PARTS):
            m[GR * part + HD * i:GR * part + HD * (i + 1), i] = 1
        m[MROW + i, i] = m[MROW + HG + i, i] = 1
    return m


def apart(eng, passed):
    eng.sem_inc(passed, 1)


def value_frame():
    f = np.zeros((128, H, VW), np.float32)
    f[:, :, HD:2 * HD] = 1
    return f


def layer0(nc, res, dram, load_early):
    with ExitStack() as ctx:
        def sb(name, shape, dt=FP32):
            return ctx.enter_context(nc.sbuf_tensor(name, shape, dt))

        def sem(name):
            return ctx.enter_context(nc.semaphore(name))

        wq, wk, wv, wp = (sb(n, [C, C]) for n in ("wq", "wk", "wv", "wp"))
        bq, bk, bv, level, qscale = (sb(n, [C, 1]) for n in ("bq", "bk", "bv", "level", "qscale"))
        bv_wide = sb("bv_wide", [C, 128])
        bp_row = sb("bp_row", [128, C])
        wg, wu, wd = sb("wg", [C, FFN]), sb("wu", [C, FFN]), sb("wd", [128, FC, C])
        mask = sb("mask", [128, HG])

        stats, moments = sb("stats", [128, TT, 6]), sb("moments", [128, TT, 2])
        var_eps, rstd, minus_half = sb("var_eps", [128, TT]), sb("rstd", [128, TT]), sb("minus_half", [128, TT])
        xn = sb("xn", [128, TT, C])
        xnT = sb("xnT", [C, T])

        q_hi = [sb(f"q_hi{p}", [128, T], FP32R) for p in range(2)]
        q_lo = [sb(f"q_lo{p}", [128, T], FP32R) for p in range(2)]
        k_hi = [sb(f"k_hi{p}", [128, T], FP32R) for p in range(2)]
        k_lo = [sb(f"k_lo{p}", [128, T], FP32R) for p in range(2)]
        q_op = [sb(f"q_op{g}", [128, T], FP32R) for g in range(NG)]
        k_op = [sb(f"k_op{p}", [128, T]) for p in range(2)]
        k_head = [[sb(f"k_head{g}_{i}", [128, T], FP32R) for i in range(HG)] for g in range(NG)]
        v_aug = [sb(f"v_aug{p}", [128, TT, H, VW]) for p in range(2)]
        row_max = [sb(f"row_max{p}", [128, TT, HG]) for p in range(2)]
        max_hi = sb("max_hi", [128, TT, HG], FP32R)
        max_parts = sb("max_parts", [128, TT, 2 * HG])
        probs = [sb(f"probs{p}", [128, HG, T]) for p in range(2)]
        wg_int, wu_int, wd_int = (probs[0][:, i, 0:FFN].bitcast(INT32) for i in range(3))

        y_raw, y_rows, inverse, yT = (sb(n, [128, T]) for n in ("y_raw", "y_rows", "inverse", "yT"))
        dens, inverses = sb("dens", [128, H * T // 128]), sb("inverses", [128, H * T // 128])
        tanh_g = sb("tanh_g", [128, T])
        silu_g, up = ([sb(f"{n}{p}", [128, T]) for p in range(2)] for n in ("silu_g", "up"))
        hT = sb("hT", [128, FC, T])
        tanh_z = sb("tanh_z", [128, TT, C])
        gate = [sb(f"gate{p}", [128, TT, C]) for p in range(2)]
        s_out = sb("s_out", [128, TT, C])

        def ps(name, shape):
            return ctx.enter_context(nc.psum_tensor(name, shape, FP32))

        ps_exp = [ps(f"ps_exp{j}", [128, 2, T]) for j in range(2)]
        ps_max = [ps(f"ps_max{j}", [128, T]) for j in range(2)]
        ps_y = ps("ps_y", [128, T])
        ps_side = ps("ps_side", [128, T])
        side_by_token = ps_side[:, :].rearrange("p (t c) -> p t c", t=TT)

        x_loaded, loaded, frames_loaded, weights_ready, consts_ready = sem("x_loaded"), sem("loaded"), sem("frames_loaded"), sem("weights_ready"), sem("consts_ready")
        scale_ready, norm_step, var_ready, rstd_ready = sem("scale_ready"), sem("norm_step"), sem("var_ready"), sem("rstd_ready")
        stats_passed, k_passed, sp_passed = sem("stats_passed"), sem("k_passed"), sem("sp_passed")
        xn_ready, xn_out_ready = sem("xn_ready"), sem("xn_out_ready")
        side_ready, side_free = sem("side_ready"), sem("side_free")
        hi_ready, tanh_ready = sem("hi_ready"), sem("tanh_ready")
        silu_ready, up_ready, h_ready = sem("silu_ready"), sem("up_ready"), sem("h_ready")
        q_loaded = [sem(f"q_loaded{g}") for g in range(NG)]
        k_loaded = [sem(f"k_loaded{p}") for p in range(2)]
        k_masked = sem("k_masked")
        max_scores, max_done, max_hi_ready, max_parts_ready = sem("max_scores"), sem("max_done"), sem("max_hi_ready"), sem("max_parts_ready")
        exp_scores, exp_done, pv_done = sem("exp_scores"), sem("exp_done"), sem("pv_done")
        y_evacuated, y_moved, den_inverted, yT_ready = sem("y_evacuated"), sem("y_moved"), sem("den_inverted"), sem("yT_ready")
        den_stored, den_gathered, inverse_stored, inverse_spread = (
            sem(n) for n in ("den_stored", "den_gathered", "inverse_stored", "inverse_spread"))
        gated, x1_ready = sem("gated"), sem("x1_ready")

        def wait(eng, s, v):
            if not isinstance(v, int) or v > 0:
                eng.wait_ge(s, v)

        def norm_in(b):
            if isinstance(b, int):
                return 2 if b == 0 else 2 * b + 1 if b + 2 < B else None
            return 2 * b + 1

        def norm_out(b):
            if isinstance(b, int) and b + 2 >= B:
                return B - 1 + b
            return 2 * b + 2

        def h_before(b, f):
            return FC * b + {0: 0, 1: 2 - FC, 2: 1}[f]

        def is_last(b):
            return isinstance(b, int) and b == B - 1

        def pairs(b, s, j):
            return 2 * STEPS * b + 2 * s + j + 1

        def max_tiles(b, s, t):
            return TT * (STEPS * b + s + AHEAD) + t + 1

        SIDE = ["xnT", "q", "max", "v", "k", "g0", "max", "u0", "proj", "g1", "max", "u1", "g2", "u2", "max", "down"]
        HEAD_SIDE = ["bias", "xnT", "q", "k", "v", "g0", "u0", "g1", "u1", "g2", "u2", "down", "max"]

        def has_side(b, s):
            if isinstance(b, int) and b == 0 and SIDE[s] == "proj":
                return False
            return not is_last(b) or SIDE[s] == "proj" or (SIDE[s] == "max" and s != STEPS - 2)

        def side(b, s):
            if isinstance(b, int) and b == 0:
                return len(HEAD_SIDE) + sum(has_side(0, t) for t in range(s))
            first = len(HEAD_SIDE) + STEPS * b - 1
            return first + (sum(has_side(b, t) for t in range(s)) if is_last(b) else s)

        def max_head(b, s):
            n = s + AHEAD
            return n >= STEPS, n % STEPS // HG, n % HG

        def has_max(b, s):
            return not (is_last(b) and max_head(b, s)[0])

        def bodies(one):
            one(0, 0)
            with one.engine.Fori(0, (B - 4) // 2) as n:
                one(2 * n + 1, 1)
                one(2 * n + 2, 0)
            for b in range(B - 3, B):
                one(b, b % 2)

        def tiles(b):
            return slice(TT * b, TT * b + TT) if isinstance(b, int) else bass.ds(TT * b, TT)

        def tile(b, t):
            return slice(TT * b + t, TT * b + t + 1) if isinstance(b, int) else bass.ds(TT * b + t, 1)

        LOADS = 16 * (8 + 1 + 3 + 2)
        block = ctx.enter_context(nc.Block())

        @block.sync
        def _(sp):
            x_src = dram["x"].rearrange("b (t p) c -> p (b t) c", p=128)
            sp.dma_start(res.x[:, 0:2 * TT, :], x_src[:, 0:2 * TT, :]).then_inc(x_loaded, 16)
            for dst, src in ((wq, "wqT"), (wk, "wkT"), (wv, "wvT"), (wp, "wpT"), (wg_int, "wgT"), (wu_int, "wuT"),
                             (mask, "mask"), (res.ident, "ident")):
                sp.dma_start(dst[:, :], dram[src]).then_inc(loaded, 16)
            sp.dma_start(wd_int.rearrange("p (f c) -> p f c", f=FC), dram["wdT"].rearrange("(f p) c -> p f c", p=128)).then_inc(loaded, 16)
            for dst, src in ((bq, "bq"), (bk, "bk"), (bv, "bv")):
                sp.dma_start(dst[:, :], dram[src].rearrange("(c a) -> c a", a=1)).then_inc(loaded, 16)
            sp.dma_start(bp_row[:, :], dram["bp"].rearrange("(a c) -> a c", a=1).broadcast_to([128, C])).then_inc(loaded, 16)
            sp.dma_start(level[:, :], dram["level"].rearrange("(a c) -> a c", a=1).broadcast_to([128, 1])).then_inc(loaded, 16)
            for p in range(2):
                for t in range(TT):
                    sp.dma_start(v_aug[p][:, t, :, :], dram["value_frame"]).then_inc(frames_loaded, 16)
            sp.wait_ge(x_loaded, 16)
            sp.dma_start(res.x[:, 2 * TT:, :], x_src[:, 2 * TT:, :]).then_inc(x_loaded, 16)
            load_early(sp)

            def load_operands(b, par, g):
                rows = slice(GR * g, GR * g + GR)
                for part, src in enumerate((q_hi, q_lo, q_hi)):
                    sp.dma_start(q_op[g][GR * part:GR * part + GR, :].bitcast(FP32), src[par][rows, :].bitcast(FP32)).then_inc(q_loaded[g], 16)
                wait(sp, k_masked, HG * (NG * b + g - 1))
                for part, src in enumerate((k_hi, k_hi, k_lo)):
                    sp.dma_start(k_op[g % 2][GR * part:GR * part + GR, :], src[par][rows, :].bitcast(FP32)).then_inc(k_loaded[g % 2], 16)

            def move_y(b, g):
                sp.wait_ge(y_evacuated, NG * b + g + 1)
                if g == 0:
                    wait(sp, yT_ready, b)
                sp.dma_start(dram["dens"][HG * g:HG * g + HG, :], y_raw[HD::VW, :]).then_inc(den_stored, 16)
                for i in range(HG):
                    rows = slice(GR * g + HD * i, GR * g + HD * i + HD)
                    sp.dma_start(y_rows[rows, :], y_raw[VW * i:VW * i + HD, :]).then_inc(y_moved, 16)

            def spread_inverses(b):
                sp.wait_ge(den_stored, NG * 16 * (b + 1))
                sp.dma_start(dens[:, :], dram["dens"].rearrange("h (k t) -> (h k) t", k=128 // H)).then_inc(den_gathered, 16)
                sp.wait_ge(den_inverted, b + 1)
                apart(sp, sp_passed)
                wait(sp, inverse_spread, HD * 16 * b)
                apart(sp, sp_passed)
                sp.dma_start(dram["inverses"].rearrange("h (k t) -> (h k) t", k=128 // H), inverses[:, :]).then_inc(inverse_stored, 16)
                sp.wait_ge(inverse_stored, 16 * (b + 1))
                apart(sp, sp_passed)
                wait(sp, yT_ready, b)
                apart(sp, sp_passed)
                for i in range(HD):
                    sp.dma_start(inverse[i::HD, :], dram["inverses"]).then_inc(inverse_spread, 16)

            sp.wait_ge(consts_ready, 1)
            sp.wait_ge(side_free, HEAD_SIDE.index("k") + 1)
            for g in range(NG):
                load_operands(0, 0, g)

            def one(b, par):
                if not (isinstance(b, int) and b == 0):
                    spread_inverses(b - 1)
                for g in range(NG):
                    if not is_last(b):
                        sp.wait_ge(exp_scores, pairs(b, TT * g + TT - 1, 1))
                        if g == 0:
                            apart(sp, sp_passed)
                            sp.wait_ge(side_free, side(b, SIDE.index("k")) + 1)
                        load_operands(b + 1, 1 - par, g)
                    move_y(b, g)

            one.engine = sp
            bodies(one)
            spread_inverses(B - 1)

        @block.gpsimd
        def _(pool):
            for p in range(2):
                pool.memset(k_op[p][:, :], -1.0)
            pool.memset(minus_half[:, :], -0.5).then_inc(consts_ready, 1)

            def mask_heads(b, g):
                pool.wait_ge(k_loaded[g % 2], PARTS * 16 * (NG // 2 * b + g // 2 + 1))
                apart(pool, k_passed)
                for i in range(HG):
                    pool.tensor_scalar(k_head[g][i][0:KROWS, :], k_op[g % 2][0:KROWS, :], mask[0:KROWS, i:i + 1], 1.0,
                                       ALU.mult, ALU.mult).then_inc(k_masked, 1)

            def norm_rstd(n):
                pool.wait_ge(var_ready, n + 1)
                pool.tensor_tensor(rstd[:, :], var_eps[:, :], minus_half[:, :], ALU.pow).then_inc(rstd_ready, 1)

            def hidden(b, f, ups):
                pool.wait_ge(side_free, ups)
                pool.tensor_tensor(hT[:, f, :], silu_g[f % 2][:, :], up[f % 2][:, :], ALU.mult).then_inc(h_ready, 1)

            def gate_out(b, par, projected):
                pool.wait_ge(side_free, projected)
                pool.tensor_tensor(s_out[:, :, :], s_out[:, :, :], gate[par][:, :, :], ALU.mult).then_inc(gated, 1)
                pool.wait_ge(gated, b + 1)
                pool.tensor_tensor(res.x[:, tiles(b), :], s_out[:, :, :], res.x[:, tiles(b), :], ALU.add).then_inc(x1_ready, 1)

            pool.wait_ge(consts_ready, 1)
            norm_rstd(0)
            norm_rstd(1)
            pool.wait_ge(loaded, LOADS)
            for g in range(NG):
                mask_heads(0, g)
            for f in range(FC):
                hidden(0, f, HEAD_SIDE.index(f"u{f}") + 1)

            def one(b, par):
                first = isinstance(b, int) and b == 0
                if norm_in(b) is not None:
                    norm_rstd(norm_in(b))
                if not is_last(b):
                    mask_heads(b + 1, 0)
                    hidden(b + 1, 0, side(b, SIDE.index("u0")) + 1)
                if not first:
                    gate_out(b - 1, 1 - par, side(b, SIDE.index("proj")) + 1)
                if not is_last(b):
                    mask_heads(b + 1, 1)
                    hidden(b + 1, 1, side(b, SIDE.index("u1")) + 1)
                if not first:
                    norm_rstd(norm_out(b))
                if not is_last(b):
                    hidden(b + 1, 2, side(b, SIDE.index("u2")) + 1)
                    mask_heads(b + 1, 2)
                    mask_heads(b + 1, 3)

            one.engine = pool
            bodies(one)
            gate_out(B - 1, (B - 1) % 2, side(B - 1, STEPS) + 1)
            norm_rstd(2 * B - 1)

        @block.vector
        def _(dve):
            def norm_stats(n, b):
                for t in range(TT):
                    last = dve.bn_stats(stats[:, t, :], res.x[:, tile(b, t), :])
                last.then_inc(norm_step, 1)
                dve.wait_ge(norm_step, 2 * n + 1)
                apart(dve, stats_passed)
                for t in range(TT):
                    last = dve.bn_aggr(moments[:, t, :], stats[:, t, :])
                last.then_inc(norm_step, 1)
                dve.wait_ge(norm_step, 2 * n + 2)
                dve.tensor_scalar(var_eps[:, :], moments[:, :, 1], EPS, None, ALU.add).then_inc(var_ready, 1)

            def norm_apply(n, b, dst, ready):
                dve.wait_ge(rstd_ready, n + 1)
                for t in range(TT):
                    last = dve.tensor_scalar(dst(t), res.x[:, tile(b, t), :], moments[:, t, 0:1], rstd[:, t:t + 1],
                                             ALU.subtract, ALU.mult)
                last.then_inc(ready, 1)

            def norm_input(n, b):
                norm_apply(n, b, lambda t: xn[:, t:t + 1, :], xn_ready)

            def norm_output(n, b):
                norm_apply(n, b, lambda t: res.xn[:, tile(b, t), :], xn_out_ready)

            def maximum(t, bank, count, group, i):
                dve.wait_ge(max_scores, count)
                dve.tensor_reduce(row_max[group % 2][:, t, i:i + 1], ps_max[bank][:, :], AX.X, ALU.max).then_inc(max_done, 1)

            def maxima_parts(n, group, tiles_done, rows_made):
                dve.wait_ge(max_done, tiles_done)
                wait(dve, side_ready, rows_made)
                dve.tensor_copy(max_hi[:, :, :], row_max[group % 2][:, :, :]).then_inc(max_hi_ready, 1)
                dve.wait_ge(max_hi_ready, n + 1)
                dve.tensor_copy(max_parts[:, :, 0:HG], max_hi[:, :, :].bitcast(FP32))
                dve.tensor_tensor(max_parts[:, :, HG:], row_max[group % 2][:, :, :], max_hi[:, :, :].bitcast(FP32),
                                  ALU.subtract).then_inc(max_parts_ready, 1)

            def from_side(what, b, par, n):
                if what in ("q", "k"):
                    lo, hi, bias = (q_lo, q_hi, bq) if what == "q" else (k_lo, k_hi, bk)
                    dve.wait_ge(hi_ready, 2 * b + (1 if what == "q" else 2))
                    dve.scalar_tensor_tensor(lo[par][:, :], ps_side[:, :], bias[:, 0:1], hi[par][:, :].bitcast(FP32),
                                             ALU.add, ALU.subtract).then_inc(side_free, 1)
                elif what[0] == "g":
                    dve.wait_ge(tanh_ready, 4 * b + int(what[1]) + 1)
                    wait(dve, h_ready, h_before(b, int(what[1])))
                    dve.scalar_tensor_tensor(silu_g[int(what[1]) % 2][:, :], tanh_g[:, :], 1.0, ps_side[:, :], ALU.add, ALU.mult).then_inc(side_free, 1)
                elif what == "down":
                    dve.wait_ge(tanh_ready, 4 * b + 4)
                    dve.scalar_tensor_tensor(gate[par][:, :, :], tanh_z[:, :, :], 1.0, side_by_token, ALU.add, ALU.mult).then_inc(side_free, 1)
                elif what == "proj":
                    dve.wait_ge(side_ready, n + 1)
                    dve.tensor_tensor(s_out[:, :, :], side_by_token, bp_row[:, None, :].broadcast_to([128, TT, C]), ALU.add)\
                       .then_inc(side_free, 1)

            def invert(b):
                dve.wait_ge(den_gathered, 16 * (b + 1))
                wait(dve, inverse_stored, 16 * b)
                dve.reciprocal(inverses[:, :], dens[:, :]).then_inc(den_inverted, 1)

            def normalise_y(b):
                dve.wait_ge(y_moved, H * 16 * (b + 1))
                dve.wait_ge(inverse_spread, HD * 16 * (b + 1))
                dve.tensor_tensor(yT[:, :], y_rows[:, :], inverse[:, :], ALU.mult).then_inc(yT_ready, 1)

            dve.wait_ge(x_loaded, 16)
            norm_stats(0, 0)
            norm_input(0, 0)
            dve.wait_ge(loaded, LOADS)
            s8 = float(np.float32(1.0) / np.sqrt(np.float32(HD)))
            unit = float(np.float32(1.0 / 127.0))
            dve.tensor_scalar(qscale[:, :], level[:, :], 0.5 * s8, 0.5 * s8, ALU.mult, ALU.add).then_inc(scale_ready, 1)
            dve.wait_ge(scale_ready, 1)
            dve.tensor_scalar(wq[:, :], wq[:, :], qscale[:, 0:1], None, ALU.mult)
            dve.tensor_scalar(bq[:, :], bq[:, :], qscale[:, 0:1], None, ALU.mult)
            dve.tensor_scalar(wg[:, :], wg_int[:, :], unit, None, ALU.mult)
            dve.tensor_scalar(wu[:, :], wu_int[:, :], unit, None, ALU.mult)
            dve.tensor_scalar(wd[:, :, :], wd_int.rearrange("p (f c) -> p f c", f=FC), unit, 0.5, ALU.mult, ALU.mult)
            dve.tensor_scalar(wp[:, :], wp[:, :], 0.5, None, ALU.mult)
            dve.tensor_scalar(bp_row[:, :], bp_row[:, :], 0.5, None, ALU.mult)
            dve.tensor_copy(bv_wide[:, :], bv[:, 0:1].broadcast_to([C, 128])).then_inc(weights_ready, 1)
            dve.wait_ge(weights_ready, 1)
            dve.wait_ge(side_ready, 1)
            dve.tensor_tensor(bp_row[:, :], ps_side[:, 0:C], bp_row[:, :], ALU.add).then_inc(side_free, 1)
            dve.wait_ge(side_free, 1)
            from_side("q", 0, 0, 2)
            from_side("k", 0, 0, 3)
            norm_stats(1, 1)
            dve.wait_ge(side_ready, 2)
            norm_input(1, 1)
            for n in range(AHEAD):
                for t in range(TT):
                    maximum(t, t % 2, TT * n + t + 1, n // HG, n % HG)
                from_side(HEAD_SIDE[5 + n], 0, 0, 5 + n)
            from_side("down", 0, 0, 11)
            maxima_parts(0, 0, TT * HG, 0)

            def one(b, par):
                first = isinstance(b, int) and b == 0
                for s in range(STEPS):
                    def tile_max(t):
                        if has_max(b, s):
                            _, group, i = max_head(b, s)
                            maximum(t, t % 2, max_tiles(b, s, t), group, i)

                    if s % HG == 2 and has_side(b, s):
                        g = s // HG
                        before = side(b, s - HG) + 1 if g else side(b, 0) - (0 if first else 1)
                        maxima_parts(NG * b + g + 1, g + 1, TT * (STEPS * b + TT * (g + 1) + HG), before)
                    tile_max(0)
                    if s == 0 and not first:
                        from_side("down", b, par, side(b, 0) - 1)
                    elif s > 0 and has_side(b, s - 1) and SIDE[s - 1] != "down":
                        prev = SIDE[s - 1]
                        if prev == "proj":
                            from_side(prev, b - 1, 1 - par, side(b, s - 1))
                        else:
                            from_side(prev, b + 1, 1 - par, side(b, s - 1))
                    tile_max(1)
                    if s == 7 and norm_in(b) is not None:
                        norm_stats(norm_in(b), b + 2)
                    if s == 9 and norm_in(b) is not None:
                        norm_input(norm_in(b), b + 2)
                    tile_max(2)
                    if s == 12 and not first:
                        dve.wait_ge(x1_ready, b)
                        norm_stats(norm_out(b), b - 1)
                    if s == 14 and not first:
                        norm_output(norm_out(b), b - 1)
                    tile_max(3)
                    if s == 2 and not first:
                        invert(b - 1)
                    if s == 6 and not first:
                        normalise_y(b - 1)

            dve.wait_ge(x_loaded, 32)
            one.engine = dve
            bodies(one)
            invert(B - 1)
            normalise_y(B - 1)
            from_side("proj", B - 1, (B - 1) % 2, side(B - 1, STEPS))
            dve.wait_ge(x1_ready, B)
            norm_stats(2 * B - 1, B - 1)
            norm_output(2 * B - 1, B - 1)
            dve.wait_ge(xn_out_ready, B)

        @block.scalar
        def _(act):
            def from_side(what, b, par, n, group=None):
                if what in ("bias", "proj"):
                    return
                act.wait_ge(side_ready, n + 1)
                if what == "xnT":
                    act.activation(xnT[:, :], ps_side[:, :], ACT.Copy).then_inc(side_free, 1)
                elif what in ("q", "k"):
                    hi, bias = (q_hi, bq) if what == "q" else (k_hi, bk)
                    wait(act, q_loaded[NG - 1], PARTS * 16 * (b - 1))
                    wait(act, k_loaded[1], PARTS * 16 * NG // 2 * (b - 1))
                    act.activation(hi[par][:, :], ps_side[:, :], ACT.Identity, bias=bias[:, 0:1]).then_inc(hi_ready, 1)
                elif what == "v":
                    if isinstance(b, int) and b == 0:
                        act.wait_ge(frames_loaded, 16 * 2 * TT)
                    act.activation(v_aug[par][:, :, :, 0:HD], ps_side[:, :].rearrange("p (t h d) -> p t h d", t=TT, h=H),
                                   ACT.Copy).then_inc(side_free, 1)
                elif what[0] == "u":
                    wait(act, h_ready, h_before(b, int(what[1])))
                    act.activation(up[int(what[1]) % 2][:, :], ps_side[:, :], ACT.Copy).then_inc(side_free, 1)
                elif what[0] == "g":
                    act.activation(tanh_g[:, :], ps_side[:, :], ACT.Tanh, scale=0.5).then_inc(tanh_ready, 1)
                elif what == "down":
                    act.activation(tanh_z[:, :, :], side_by_token, ACT.Tanh, scale=0.5).then_inc(tanh_ready, 1)
                elif what == "max":
                    act.activation(q_op[group][MROW:KROWS, :], ps_side[MROW:KROWS, :], ACT.Copy).then_inc(side_free, 1)

            act.wait_ge(weights_ready, 1)
            for n, what in enumerate(HEAD_SIDE):
                from_side(what, 0, 0, n, 0)

            def exponentials(b, s, j):
                act.wait_ge(exp_scores, pairs(b, s, j))
                wait(act, pv_done, STEPS * b + s - 1)
                act.activation(probs[s % 2][:, 2 * j:2 * j + 2, :], ps_exp[j][:, :, :], ACT.Exp).then_inc(exp_done, 1)

            def evacuate_y(b, g):
                act.wait_ge(pv_done, STEPS * b + TT * g + TT)
                wait(act, y_moved, HG * 16 * (NG * b + g))
                wait(act, den_stored, 16 * (NG * b + g))
                act.activation(y_raw[:, :], ps_y[:, :], ACT.Copy).then_inc(y_evacuated, 1)

            def one(b, par):
                first = isinstance(b, int) and b == 0
                for s in range(STEPS):
                    if s == 0 and not first:
                        from_side("down", b, par, side(b, 0) - 1)
                    elif s > 0 and has_side(b, s - 1) and SIDE[s - 1] != "down":
                        from_side(SIDE[s - 1], b + 1, 1 - par, side(b, s - 1), (s // HG + 1) % NG)
                    exponentials(b, s, 0)
                    exponentials(b, s, 1)
                    if s % TT == 0:
                        if s:
                            evacuate_y(b, s // TT - 1)
                        elif not first:
                            evacuate_y(b - 1, NG - 1)

            one.engine = act
            bodies(one)
            evacuate_y(B - 1, NG - 1)

        @block.tensor
        def _(pe):
            def wide(out, lhsT, rhs):
                return pe.matmul(out, lhsT, rhs, start=True, stop=True)

            def to_side(what, b, par, n, group=0):
                wait(pe, side_free, n)
                if what == "bias":
                    pe.wait_ge(weights_ready, 1)
                    last = wide(ps_side[:, 0:C], bv_wide[:, :], wp[:, :])
                elif what == "xnT":
                    pe.wait_ge(xn_ready, b + 1)
                    for t in range(TT):
                        last = pe.transpose(side_by_token[:, t, :], xn[:, t, :], res.ident[:, :])
                elif what in ("q", "k"):
                    last = wide(ps_side[:, :], (wq if what == "q" else wk)[:, :], xnT[:, :])
                elif what == "v":
                    for t in range(TT):
                        last = wide(side_by_token[:, t, :], xnT[:, 128 * t:128 * t + 128], wv[:, :])
                elif what[0] in "gu":
                    f = int(what[1])
                    last = wide(ps_side[:, :], (wg if what[0] == "g" else wu)[:, 128 * f:128 * f + 128], xnT[:, :])
                elif what == "down":
                    pe.wait_ge(h_ready, FC * (b + 1))
                    for t in range(TT):
                        for f in range(FC):
                            last = pe.matmul(side_by_token[:, t, :], hT[:, f, 128 * t:128 * t + 128], wd[:, f, :],
                                             start=(f == 0), stop=(f == FC - 1))
                elif what == "proj":
                    pe.wait_ge(yT_ready, b + 1)
                    for t in range(TT):
                        last = wide(side_by_token[:, t, :], yT[:, 128 * t:128 * t + 128], wp[:, :])
                elif what == "max":
                    pe.wait_ge(max_parts_ready, group + 1)
                    for t in range(TT):
                        last = wide(ps_side[MROW:KROWS, 128 * t:128 * t + 128], max_parts[:, t, :], res.ident[:, :])
                last.then_inc(side_ready, 1)

            def score_for_max(group, i, t, count):
                wait(pe, max_done, count - 2)
                wide(ps_max[t % 2][:, :], q_op[group][0:MROW, 128 * t:128 * t + 128], k_head[group][i][0:MROW, :])\
                    .then_inc(max_scores, 1)

            def operands(b, group, i):
                pe.wait_ge(q_loaded[group], PARTS * 16 * (b + 1))
                pe.wait_ge(k_masked, HG * (NG * b + group) + i + 1)

            def score_for_exp(b, s, j):
                g, t = s // TT, s % TT
                wait(pe, exp_done, pairs(b, s, j) - 2)
                for i in (2 * j, 2 * j + 1):
                    last = wide(ps_exp[j][:, i % 2, :], k_head[g][i][0:KROWS, 128 * t:128 * t + 128], q_op[g][0:KROWS, :])
                last.then_inc(exp_scores, 1)

            def weigh_values(b, par, s):
                g, t = s // TT, s % TT
                if t == 0:
                    wait(pe, y_evacuated, NG * b + g)
                for i in range(HG):
                    if i % 2 == 0:
                        pe.wait_ge(exp_done, pairs(b, s, i // 2))
                    last = pe.matmul(ps_y[VW * i:VW * i + VW, :], v_aug[par][:, t, HG * g + i, :], probs[s % 2][:, i, :],
                                     start=(t == 0), stop=(t == TT - 1))
                last.then_inc(pv_done, 1)

            pe.wait_ge(loaded, LOADS)
            for n in range(5):
                to_side(HEAD_SIDE[n], 0, 0, n)
            for n in range(AHEAD):
                operands(0, n // HG, n % HG)
                for t in range(TT):
                    score_for_max(n // HG, n % HG, t, TT * n + t + 1)
                to_side(HEAD_SIDE[5 + n], 0, 0, 5 + n)
            to_side("down", 0, 0, 11)
            to_side("max", 0, 0, 12)

            def one(b, par):
                first = isinstance(b, int) and b == 0
                for s in range(STEPS):
                    def tile_max(t):
                        if has_max(b, s):
                            following, group, i = max_head(b, s)
                            if t == 0:
                                operands(b + 1 if following else b, group, i)
                            score_for_max(group, i, t, max_tiles(b, s, t))

                    if s % TT == 0:
                        at = side(b, s - 2) if s else side(b, 0) - (1 if first else 2)
                        pe.wait_ge(side_free, at + 1)
                    score_for_exp(b, s, 0)
                    tile_max(0)
                    if s:
                        weigh_values(b, par, s - 1)
                    elif not first:
                        weigh_values(b - 1, 1 - par, STEPS - 1)
                    tile_max(1)
                    score_for_exp(b, s, 1)
                    tile_max(2)
                    if has_side(b, s):
                        what = SIDE[s]
                        if what == "proj":
                            to_side(what, b - 1, 1 - par, side(b, s))
                        elif what == "max":
                            to_side(what, b, par, side(b, s), NG * b + s // HG + 1)
                        else:
                            to_side(what, b + 1, 1 - par, side(b, s))
                    tile_max(3)

            one.engine = pe
            bodies(one)
            weigh_values(B - 1, (B - 1) % 2, STEPS - 1)
            to_side("proj", B - 1, (B - 1) % 2, side(B - 1, STEPS))



BF16 = mybir.dt.bfloat16

L = 1024
TAPS = 64
FT = L // 2 // 128
E, F = 8, 512
FE = F // 128
KPAD = 128
CG = 4


def transform_tables():
    f = np.arange(L // 2 + 1)
    j = np.arange(1, TAPS + 1)[:, None]
    fwd = np.stack([np.cos(2 * np.pi * j * f / L), -np.sin(2 * np.pi * j * f / L)], 1)
    t = T - 1 - np.arange(T)
    w = np.where(np.arange(L // 2) == 0, 1.0, 2.0)[:, None] / L
    ang = 2 * np.pi * ((np.arange(L // 2)[:, None] * t) % L) / L
    inv = np.stack([w * np.cos(ang), -w * np.sin(ang)], 0).reshape(2, FT, 128, T).transpose(2, 0, 1, 3)
    nyq = ((-1.0) ** t / L)[None, :]
    return fwd.astype(np.float32), np.ascontiguousarray(inv).astype(np.float32), nyq.astype(np.float32)


N_TOK = B * T
UNIT = 256
REGION = N_TOK + UNIT
ROW = C + 4
MAX_UNITS = 2 * N_TOK // UNIT + E
SORTED = E * REGION + MAX_UNITS * UNIT
Y_ROWS = 2 * N_TOK + E * UNIT


def place_tables():
    p = np.arange(128)[:, None]
    fill = np.arange(E * UNIT // 128)[None, :]
    token = T * (np.arange(B * TT) // TT)[None, :] + TT * p + (np.arange(B * TT) % TT)[None, :]
    parts = (np.tile(np.arange(E), (128, 1)), np.tile(np.arange(E) * REGION, (128, 1)), token,
             2 * N_TOK + 128 * fill + p)
    return np.concatenate(parts, 1).astype(np.float32)


def earlier():
    return np.stack([np.triu(np.ones((128, 128)), 1), np.ones((128, 128))], 1).astype(np.float32)


class RouteTables:

    def __init__(self, nc, ctx):
        def sb(name, shape):
            return ctx.enter_context(nc.sbuf_tensor(name, shape, FP32))

        self.taps = sb("taps", [TAPS, 2 * C])
        self.fwd = sb("fwd", [TAPS, 2, L // 2 + 1])
        self.h0 = sb("h0", [C, 1])
        self.rw = sb("rw", [C, E])
        self.tables = sb("tables", [128, 2 * E + B * TT + E * UNIT // 128])
        self.before = sb("before_f", [128, 2, 128])
        self.loaded = ctx.enter_context(nc.semaphore("tables_loaded"))
        self.LOADS = 16 * 6

    def load(self, sp, dram):
        for dst, src in ((self.taps, "abT"), (self.fwd, "fwd"), (self.rw, "rwT"),
                         (self.tables, "place_tables"), (self.before, "earlier")):
            sp.dma_start(dst[:, :] if len(dst.shape) == 2 else dst[:, :, :], dram[src]).then_inc(self.loaded, 16)
        sp.dma_start(self.h0[:, :], dram["h0"].rearrange("(c a) -> c a", a=1)).then_inc(self.loaded, 16)


class ExpertWeights:

    def __init__(self, nc, ctx):
        self.w1 = ctx.enter_context(nc.sbuf_tensor("w1", [C, E, F], FP32))
        self.w2 = ctx.enter_context(nc.sbuf_tensor("w2", [128, E, FE, C], FP32))
        self.b1 = ctx.enter_context(nc.sbuf_tensor("b1", [128, E, FE], FP32))
        self.b2 = ctx.enter_context(nc.sbuf_tensor("b2", [128, E, C], FP32))
        self.loaded = ctx.enter_context(nc.semaphore("weights_loaded"))
        self.LOADS = 16 * 4

    def load(self, sp, dram):
        sp.dma_start(self.w1[:, :, :], dram["w1T"]).then_inc(self.loaded, 16)
        sp.dma_start(self.w2[:, :, :, :], dram["w2T"]).then_inc(self.loaded, 16)
        sp.dma_start(self.b1[:, :, :], dram["b1T"]).then_inc(self.loaded, 16)
        sp.dma_start(self.b2[:, :, :], dram["b2"].rearrange("(a e) c -> a e c", a=1).broadcast_to([128, E, C])).then_inc(self.loaded, 16)


def route_and_convolve(nc, res, dram, s_all, early, weights):
    with ExitStack() as ctx:
        def sb(name, shape, dt=FP32):
            return ctx.enter_context(nc.sbuf_tensor(name, shape, dt))

        def ps(name, shape):
            return ctx.enter_context(nc.psum_tensor(name, shape, FP32))

        def sem(name):
            return ctx.enter_context(nc.semaphore(name))

        taps, fwd, h0 = early.taps, early.fwd, early.h0
        nyq_row = sb("nyq_row", [1, T])
        room = s_all[:, :, :].rearrange("p t c -> p (t c)")
        inv = room[:, 0:2 * FT * T].rearrange("p (i f t) -> p i f t", i=2, f=FT)
        room = room[:, 2 * FT * T:]
        spec = room[:, 0:4 * FT * C].rearrange("p (f r s c) -> p f r s c", f=FT, r=2, s=2)
        nyq = sb("nyq", [1, 2, C])
        norm = sb("norm", [128, FT, C])
        prod = [room[:, (4 + n) * FT * C:(5 + n) * FT * C].rearrange("p (f c) -> p f c", f=FT) for n in range(4)]
        ratio = sb("ratio", [128, 2, FT, C]); nyq_ratio = sb("nyq_ratio", [1, C])
        k_pad = sb("k_pad", [C, KPAD + T])
        inv_loaded, transformed, spec_copied, div_step, divided = (sem(n) for n in ("inv_loaded", "transformed", "spec_copied", "div_step", "divided"))
        inverted, k_ready, k_stored = sem("inverted"), sem("k_ready"), sem("k_stored")
        ps_nyq = ps("ps_nyq", [128, T])
        ps_k = ps_nyq

        NQ = C // CG
        toep = [sb(f"toep{p}", [128, CG, T]) for p in range(2)]
        inputs = [sb(f"conv_in{p}", [128, TT // 2, CG, 2, B]) for p in range(2)]
        by_time = [sb(f"by_time{p}", [128, T]) for p in range(2)]
        ps_conv = ps("ps_conv", [128, 4, 512])
        ps_t = [ps_conv[:, p, :] for p in range(2)]
        ps_b = [ps_conv[:, 2 + p, :].rearrange("p (t c b) -> p t c b", t=TT, c=CG) for p in range(2)]
        ps_spec = ps_conv[:, :, :].rearrange("p f (r s) -> p f r s", r=2)
        toep_loaded = [sem(f"toep_loaded{p}") for p in range(2)]
        evens_out, picked_in, convolved, time_copied, time_turned, spread = (
            sem(n) for n in ("evens_out", "picked", "convolved", "by_time_copied", "turned", "spread"))

        units = sb("units", [128, E + 1], INT32)
        fill_starts = sb("fill_starts", [128, E], INT32)
        units_ready, ends = sem("units_ready"), {}
        FILL = E * UNIT // 128
        rw, tables, before_f = early.rw, early.tables, early.before
        before = sb("before", [128, 2, 128], BF16)
        numbers, regions = tables[:, 0:E], tables[:, E:2 * E]
        token_numbers = tables[:, 2 * E:2 * E + B * TT]
        fill_numbers = tables[:, 2 * E + B * TT:]
        rows = [[sb(f"rows{k}_{p}", [128, TT, ROW]) for p in range(2)] for k in range(2)]
        xn_now = [sb(f"xn_now{p}", [128, TT, C]) for p in range(2)]
        xnT_now = [sb(f"xnT_now{p}", [128, T]) for p in range(2)]
        logits = sb("logits", [128, TT, E])
        top, top_at = sb("top", [128, TT, 8]), sb("top_at", [128, TT, 8], mybir.dt.uint32)
        choice = sb("choice", [128, TT, 2])
        gap = [sb(f"gap{p}", [128, TT, 1]) for p in range(2)]
        gap_sum = sb("gap_sum", [128, TT, 1])
        hot = [sb(f"hot{k}", [128, TT, E]) for k in range(2)]
        hot_both = sb("hot_both", [128, TT, E], BF16)
        taken = [sb(f"taken{p}", [128, E]) for p in range(2)]
        rank = sb("rank", [128, TT, E])
        picked = [sb(f"picked{k}", [128, TT, E]) for k in range(2)]
        place_f = [sb(f"place_f{k}", [128, TT]) for k in range(2)]
        place = [[sb(f"place{k}_{p}", [128, TT], mybir.dt.uint32) for p in range(2)] for k in range(2)]
        fill_rows = sb("fill_rows", [128, FILL, ROW])
        count_f, count = sb("count_f", [128, E]), sb("count", [128, E], INT32)
        sums = [sb(f"sums{p}", [128, E], INT32) for p in range(2)]
        ps_x, ps_s = ps("ps_x", [128, T]), ps("ps_s", [128, TT, E])
        ps_rank = ps("ps_rank", [128, TT + 1, E])
        cleared, rows_ready, x_turned, x_copied, scored = (sem(n) for n in ("rows_cleared", "rows_ready", "x_turned", "x_copied", "scored"))
        step, gap_ready, gap_exp, hot_ready, ranked, placed = (sem(n) for n in ("route_step", "gap_ready", "gap_exp", "hot_ready", "ranked", "placed"))
        fill_placed, fill_step, fill_stored = sem("fill_placed"), sem("fill_step"), sem("fill_stored")
        now_ready, act_passed = sem("now_ready"), sem("act_passed")
        scattered = [sem(f"scattered{p}") for p in range(2)]
        max_passed, pool_passed = sem("max_passed"), sem("pool_passed")
        STEPS_R = 10
        SCATTERS = 2 * TT
        block = ctx.enter_context(nc.Block())

        def wait(eng, s, v):
            if not isinstance(v, int) or v > 0:
                eng.wait_ge(s, v)

        def tiles(b):
            return slice(TT * b, TT * b + TT) if isinstance(b, int) else bass.ds(TT * b, TT)

        def at(q):
            return slice(CG * q, CG * q + CG) if isinstance(q, int) else bass.ds(CG * q, CG)

        ROUTED, PER = 6, 3
        assert 2 + PER * (B - ROUTED) == NQ

        def fill(eng, experts):
            eng.wait_ge(fill_placed, 1)
            for e in experts:
                start = eng.value_load(fill_starts[0:1, e:e + 1], min_val=e * REGION, max_val=e * REGION + N_TOK)
                eng.dma_start(dram["sorted"][bass.ds(start, UNIT), :].rearrange("(j p) c -> p j c", p=128), fill_rows[:, 2 * e:2 * e + 2, :])\
                   .then_inc(fill_stored, 16)

        def load_ends(eng):
            eng.wait_ge(units_ready, 1)
            ends[eng] = [eng.value_load(units[0:1, e:e + 1], min_val=e, max_val=MAX_UNITS) for e in range(E + 1)]

        def only_route(eng, one):
            with eng.Fori(1, ROUTED // 2) as n:
                one(2 * n, 0)
                one(2 * n + 1, 1)

        def bodies(eng, one):
            def at_b(b, par):
                one(b, PER * b + 2 - PER * ROUTED, par, par)

            at_b(ROUTED, 0)
            at_b(ROUTED + 1, 1)
            with eng.Fori(ROUTED // 2 + 1, B // 2 - 1) as n:
                at_b(2 * n, 0)
                at_b(2 * n + 1, 1)
            at_b(B - 2, 0)
            at_b(B - 1, 1)

        @block.sync
        def _(sp):
            sp.dma_start(inv[:, :, :, :], dram["inv"]).then_inc(inv_loaded, 16)
            sp.dma_start(nyq_row[:, :], dram["nyq"]).then_inc(inv_loaded, 16)
            sp.wait_ge(k_ready, 1)
            sp.dma_start(dram["k_pad"], k_pad[:, :]).then_inc(k_stored, 16)
            sp.wait_ge(k_stored, 16)

            def one(q, p):
                wait(sp, convolved, q - 1)
                src = bass.AP(dram["k_pad"].tensor, CG * (KPAD + T) * q, [[1, 128], [KPAD + T, CG], [1, T]])
                sp.dma_start(toep[p][:, :, :], src).then_inc(toep_loaded[p], 16)

            one(0, 0)
            one(1, 1)
            weights.load(sp, dram)
            with sp.Fori(1, NQ // 2) as n:
                one(2 * n, 0)
                one(2 * n + 1, 1)
            fill(sp, range(E // 2))
            load_ends(sp)
            sp.wait_ge(fill_stored, 16 * E)

        @block.scalar
        def _(act):
            act.wait_ge(cleared, 1)

            def fetch_now(b, p):
                wait(act, x_turned, b - 1)
                apart(act, act_passed)
                act.activation(xn_now[p][:, :, :], res.xn[:, tiles(b), :], ACT.Copy).then_inc(now_ready, 1)

            def fetch_rows(b, p):
                if not isinstance(b, int) or b >= 2:
                    act.wait_ge(scattered[p], 8 * SCATTERS * (b - p))
                    apart(act, act_passed)
                for k in range(2):
                    last = act.activation(rows[k][p][:, :, 0:C], res.xn[:, tiles(b), :], ACT.Copy)
                last.then_inc(rows_ready, 1)

            def copy_x(b, p):
                act.wait_ge(x_turned, b + 1)
                act.activation(xnT_now[p][:, :], ps_x[:, :], ACT.Copy).then_inc(x_copied, 1)

            def exp(b, p):
                act.wait_ge(gap_ready, b + 1)
                act.activation(gap[p][:, :, :], gap[p][:, :, :], ACT.Exp).then_inc(gap_exp, 1)

            def reverse(q, p):
                act.wait_ge(convolved, q + 1)
                wait(act, time_turned, q - 1)
                act.activation(by_time[p][:, :], ps_t[p][:, ::-1], ACT.Copy).then_inc(time_copied, 1)

            for b in range(2):
                fetch_now(b, b)
                copy_x(b, b)
                exp(b, b)
                fetch_rows(b, b)
                if b == 0:
                    act.wait_ge(transformed, 1)
                    act.activation(spec[:, :, :, :, :].rearrange("p f r s c -> p (f r s c)"),
                                   ps_spec[:, :, :, :].rearrange("p f r s -> p (f r s)"), ACT.Copy)
                    act.activation(nyq[:, :, :].rearrange("p s c -> p (s c)"), ps_nyq[0:1, 0:2 * C], ACT.Copy).then_inc(spec_copied, 1)
            def route(b, par):
                fetch_now(b, par)
                copy_x(b, par)
                exp(b, par)
                fetch_rows(b, par)

            only_route(act, route)
            reverse(0, 0)
            reverse(1, 1)

            def one(b, q, par, p):
                fetch_now(b, par)
                reverse(q, p)
                copy_x(b, par)
                reverse(q + 1, 1 - p)
                exp(b, par)
                reverse(q + 2, p)
                fetch_rows(b, par)

            bodies(act, one)
            fill(act, range(E // 2, E))
            load_ends(act)

        @block.tensor
        def _(pe):
            def turn_x(b, p):
                pe.wait_ge(now_ready, b + 1)
                wait(pe, x_copied, b)
                for t in range(TT):
                    last = pe.transpose(ps_x[:, 128 * t:128 * t + 128], xn_now[p][:, t, :], res.ident[:, :])
                last.then_inc(x_turned, 1)

            def score(b, p):
                pe.wait_ge(x_copied, b + 1)
                wait(pe, hot_ready, b)
                for t in range(TT):
                    last = pe.matmul(ps_s[:, t, :], xnT_now[p][:, 128 * t:128 * t + 128], rw[:, :], start=True, stop=True)
                last.then_inc(scored, 1)

            def rank_tokens(b):
                pe.wait_ge(hot_ready, b + 1)
                for t in range(TT):
                    pe.matmul(ps_rank[:, t, :], before[:, 0, :], hot_both[:, t, :], start=True, stop=(t == 0))
                    for u in range(t):
                        pe.matmul(ps_rank[:, t, :], before[:, 1, :], hot_both[:, u, :], start=False, stop=(u == t - 1))
                for t in range(TT):
                    last = pe.matmul(ps_rank[:, TT, :], before[:, 1, :], hot_both[:, t, :], start=(t == 0), stop=(t == TT - 1))
                last.then_inc(ranked, 1)

            def product(q, p):
                pe.wait_ge(picked_in, q + 1)
                pe.wait_ge(toep_loaded[p], 16 * (q // 2 + 1) if isinstance(q, int) else 8 * (q - p) + 16)
                wait(pe, time_copied, q - 1)
                for u in range(TT // 2):
                    for i in range(CG):
                        last = pe.matmul(ps_t[p][32 * i:32 * i + 32, 0:T - 256 * u], inputs[p][:, u, i, :, :].rearrange("p h b -> p (h b)"),
                                         toep[p][:, i, 256 * u:], start=(u == 0), stop=(u == TT // 2 - 1))
                last.then_inc(convolved, 1)

            def turn(q, p):
                pe.wait_ge(time_copied, q + 1)
                wait(pe, spread, q - 1)
                for t in range(TT):
                    last = pe.transpose(ps_b[p][:, t, :, :].rearrange("p c b -> p (c b)"), by_time[p][:, 128 * t:128 * t + 128], res.ident[:, :])
                last.then_inc(time_turned, 1)

            pe.wait_ge(early.loaded, early.LOADS)
            turn_x(0, 0)
            score(0, 0)
            for f in range(FT):
                for part in range(2):
                    pe.matmul(ps_spec[:, f, part, :], fwd[:, part, 128 * f:128 * f + 128], taps[:, :], start=True, stop=True)
            pe.matmul(ps_nyq[0:1, 0:2 * C], fwd[:, 0, L // 2:L // 2 + 1], taps[:, :], start=True, stop=True).then_inc(transformed, 1)
            rank_tokens(0)

            def route(b, par):
                turn_x(b, par)
                score(b, par)
                rank_tokens(b)

            route(1, 1)
            pe.wait_ge(inv_loaded, 32)
            pe.wait_ge(divided, 1)
            for f in range(FT):
                for part in range(2):
                    pe.matmul(ps_k[:, :], ratio[:, part, f, :], inv[:, part, f, :], start=(f == 0 and part == 0), stop=False)
            pe.matmul(ps_k[:, :], nyq_ratio[0:1, :], nyq_row[0:1, :], start=False, stop=True).then_inc(inverted, 1)
            only_route(pe, route)
            product(0, 0)
            product(1, 1)

            def one(b, q, par, p):
                product(q, p)
                turn(q - 2, p)
                turn_x(b, par)
                product(q + 1, 1 - p)
                turn(q - 1, 1 - p)
                score(b, par)
                product(q + 2, p)
                turn(q, p)
                rank_tokens(b)

            bodies(pe, one)
            turn(NQ - 2, 0)
            turn(NQ - 1, 1)
            load_ends(pe)

        @block.vector
        def _(dve):
            xn = res.xn[:, :, :].rearrange("p (b t) c -> p t b c", b=B)
            s_out = s_all[:, :, :].rearrange("p (b t) c -> p t b c", b=B)

            def pick(q, p):
                wait(dve, convolved, q - 1)
                for t in range(TT):
                    last = dve.tensor_copy(inputs[p][:, t // 2, :, t % 2, :].rearrange("p c b -> p b c"), xn[:, t, :, at(q)])
                last.then_inc(picked_in, 1)

            def out(q, p):
                dve.wait_ge(time_turned, q + 1)
                for t in range(TT):
                    last = dve.tensor_copy(s_out[:, t, :, at(q)], ps_b[p][:, t, :, 0:B].rearrange("p c b -> p b c"))
                last.then_inc(evens_out, 1)
                dve.wait_ge(evens_out, q + 1)
                for t in range(1, TT):
                    last = dve.tensor_tensor(s_out[:, t, :, at(q)], ps_b[p][:, t - 1, :, B:].rearrange("p c b -> p b c"), s_out[:, t, :, at(q)], ALU.add)
                last.then_inc(spread, 1)

            for k in range(2):
                for p in range(2):
                    last = dve.memset(rows[k][p][:, :, C:], 0.0)
            last.then_inc(cleared, 1)
            dve.memset(fill_rows[:, :, :], 0.0).then_inc(fill_step, 1)
            dve.wait_ge(early.loaded, early.LOADS)
            dve.wait_ge(fill_step, 1)
            dve.tensor_copy(before[:, :, :], before_f[:, :, :])
            dve.tensor_copy(fill_rows[:, :, C], fill_numbers)
            dve.tensor_copy(taken[0][:, :], regions).then_inc(fill_step, 1)
            dve.wait_ge(fill_step, 2)
            wide = [128, TT, E]

            def step_done(ins, b, n):
                ins.then_inc(step, 1)
                dve.wait_ge(step, STEPS_R * b + n)

            def choose(b, p):
                dve.wait_ge(scored, b + 1)
                step_done(dve.tensor_copy(logits[:, :, :], ps_s[:, :, :]), b, 1)
                apart(dve, max_passed)
                for t in range(TT):
                    last = dve.max(top[:, t, :], logits[:, t, :])
                step_done(last, b, 2)
                apart(dve, max_passed)
                for t in range(TT):
                    last = dve.max_index(top_at[:, t, :], top[:, t, :], logits[:, t, :])
                step_done(last, b, 3)
                dve.tensor_tensor(gap[p][:, :, :], top[:, :, 1:2], top[:, :, 0:1], ALU.subtract).then_inc(gap_ready, 1)
                step_done(dve.tensor_copy(choice[:, :, :], top_at[:, :, 0:2]), b, 4)
                for k in range(2):
                    last = dve.tensor_tensor(hot[k][:, :, :], numbers[:, None, :].broadcast_to(wide), choice[:, :, k:k + 1].broadcast_to(wide), ALU.is_equal)
                step_done(last, b, 5)
                dve.tensor_tensor(hot_both[:, :, :], hot[0][:, :, :], hot[1][:, :, :], ALU.add).then_inc(hot_ready, 1)

            def place_tokens(b, p):
                if not isinstance(b, int) or b >= 2:
                    dve.wait_ge(scattered[p], 8 * SCATTERS * (b - p))
                for k in range(2):
                    dve.tensor_scalar(rows[k][p][:, :, C], token_numbers[:, tiles(b)], float(k * N_TOK), None, ALU.add)
                dve.wait_ge(gap_exp, b + 1)
                step_done(dve.tensor_scalar(gap_sum[:, :, :], gap[p][:, :, :], 1.0, 2.0, ALU.add, ALU.mult), b, 6)
                step_done(dve.reciprocal(rows[0][p][:, :, C + 1:C + 2], gap_sum[:, :, :]), b, 7)
                dve.tensor_tensor(rows[1][p][:, :, C + 1:C + 2], gap[p][:, :, :], rows[0][p][:, :, C + 1:C + 2], ALU.mult)
                dve.wait_ge(ranked, b + 1)
                dve.tensor_tensor(taken[1 - p][:, :], ps_rank[:, TT, :], taken[p][:, :], ALU.add)
                step_done(dve.tensor_tensor(rank[:, :, :], ps_rank[:, 0:TT, :], taken[p][:, None, :].broadcast_to(wide), ALU.add), b, 8)
                for k in range(2):
                    last = dve.tensor_tensor(picked[k][:, :, :], hot[k][:, :, :], rank[:, :, :], ALU.mult)
                step_done(last, b, 9)
                for k in range(2):
                    last = dve.tensor_reduce(place_f[k][:, :], picked[k][:, :, :], AX.X, ALU.add)
                step_done(last, b, 10)
                for k in range(2):
                    last = dve.tensor_copy(place[k][p][:, :], place_f[k][:, :])
                last.then_inc(placed, 1)

            choose(0, 0)
            place_tokens(0, 0)
            divisions = [0]

            def div_done(ins):
                ins.then_inc(div_step, 1)
                divisions[0] += 1
                dve.wait_ge(div_step, divisions[0])

            ar, br, ai, bi = spec[:, :, 0, 0, :], spec[:, :, 0, 1, :], spec[:, :, 1, 0, :], spec[:, :, 1, 1, :]
            p = [x[:, :, :] for x in prod]
            dve.memset(k_pad[:, T:], 0.0)
            dve.wait_ge(spec_copied, 1)
            dve.tensor_scalar(nyq[:, 0, :], nyq[:, 0, :], 1.0, None, ALU.add)
            div_done(dve.tensor_scalar(ar, ar, 1.0, None, ALU.add))
            dve.reciprocal(nyq[:, 0, :], nyq[:, 0, :])
            dve.tensor_tensor(p[0], ar, ar, ALU.mult)
            div_done(dve.tensor_tensor(p[1], ai, ai, ALU.mult))
            dve.tensor_tensor(nyq_ratio[:, :], nyq[:, 0, :], nyq[:, 1, :], ALU.mult)
            div_done(dve.tensor_tensor(norm[:, :, :], p[0], p[1], ALU.add))
            dve.tensor_tensor(p[0], br, ar, ALU.mult)
            dve.tensor_tensor(p[1], bi, ai, ALU.mult)
            dve.tensor_tensor(p[2], bi, ar, ALU.mult)
            dve.tensor_tensor(p[3], br, ai, ALU.mult)
            div_done(dve.reciprocal(norm[:, :, :], norm[:, :, :]))
            dve.tensor_tensor(p[0], p[0], p[1], ALU.add)
            div_done(dve.tensor_tensor(p[2], p[2], p[3], ALU.subtract))
            dve.tensor_tensor(ratio[:, 0, :, :], p[0], norm[:, :, :], ALU.mult)
            dve.tensor_tensor(ratio[:, 1, :, :], p[2], norm[:, :, :], ALU.mult).then_inc(divided, 1)

            def route(b, par):
                choose(b, par)
                place_tokens(b, par)

            route(1, 1)
            dve.wait_ge(inverted, 1)
            dve.tensor_tensor(k_pad[:, T - 1:T], ps_k[:, T - 1:T], h0[:, :], ALU.add)
            dve.tensor_copy(k_pad[:, 0:T - 1], ps_k[:, 0:T - 1]).then_inc(k_ready, 1)
            only_route(dve, route)
            for q in range(4):
                pick(q, q % 2)

            def one(b, q, par, p):
                def pick_on(q, p):
                    if not isinstance(q, int) or q < NQ:
                        pick(q, p)

                pick_on(q + 2, p)
                out(q - 2, p)
                pick_on(q + 3, 1 - p)
                out(q - 1, 1 - p)
                choose(b, par)
                pick_on(q + 4, p)
                out(q, p)
                place_tokens(b, par)

            bodies(dve, one)
            def done(ins, n):
                ins.then_inc(fill_step, 1)
                dve.wait_ge(fill_step, n)

            dve.wait_ge(placed, B)
            dve.tensor_tensor(count_f[:, :], taken[0][:, :], regions, ALU.subtract).then_inc(fill_step, 1)
            dve.tensor_copy(fill_starts[:, :], taken[0][:, :]).then_inc(fill_placed, 1)
            dve.wait_ge(fill_step, 3)
            done(dve.tensor_scalar(count_f[:, :], count_f[:, :], 1.0, float(UNIT - 1), ALU.max, ALU.add), 4)
            done(dve.tensor_copy(count[:, :], count_f[:, :]), 5)
            done(dve.tensor_scalar(sums[0][:, :], count[:, :], UNIT.bit_length() - 1, None, ALU.logical_shift_right), 6)
            for i, shift in enumerate((1, 2, 4)):
                old, new = sums[i % 2], sums[(i + 1) % 2]
                dve.tensor_copy(new[:, 0:shift], old[:, 0:shift])
                done(dve.tensor_tensor(new[:, shift:], old[:, shift:], old[:, 0:E - shift], ALU.add), 7 + i)
            dve.memset(units[:, 0:1], 0)
            dve.tensor_copy(units[:, 1:], sums[1][:, :]).then_inc(units_ready, 1)
            out(NQ - 2, 0)
            out(NQ - 1, 1)
            load_ends(dve)

        @block.gpsimd
        def _(pool):
            def scatter(b, p):
                pool.wait_ge(rows_ready, b + 1)
                pool.wait_ge(placed, b + 1)
                apart(pool, pool_passed)
                for k in range(2):
                    for t in range(TT):
                        pool.indirect_dma_start(dram["sorted"], bass.IndirectOffsetOnAxis(place[k][p][:, t:t + 1], 0), rows[k][p][:, t, :], None)\
                            .then_inc(scattered[p], 16)

            scatter(0, 0)
            scatter(1, 1)
            with pool.Fori(1, B // 2) as n:
                scatter(2 * n, 0)
                scatter(2 * n + 1, 1)
            for p in range(2):
                pool.wait_ge(scattered[p], 16 * SCATTERS * B // 2)
            load_ends(pool)

        return ends


def experts(nc, res, dram, ends, weights):
    with ExitStack() as ctx:
        def sb(name, shape, dt=FP32):
            return ctx.enter_context(nc.sbuf_tensor(name, shape, dt))

        def sem(name):
            return ctx.enter_context(nc.semaphore(name))

        w1, w2, b1, b2 = weights.w1, weights.w2, weights.b1, weights.b2
        rows = [sb(f"unit_rows{i}", [128, ROW]) for i in range(2)]
        xT = sb("unit_xT", [C, UNIT])
        tails = sb("tails", [128, 2 * MAX_UNITS + 2, 2])
        hidden = sb("hidden", [128, FE, UNIT])
        biased = [sb(f"biased{i}", [128, C]) for i in range(2)]
        result = [sb(f"result{i}", [128, C]) for i in range(2)]
        goes_to = [sb(f"goes_to{i}", [128, 1], mybir.dt.uint32) for i in range(2)]
        ps_x = ctx.enter_context(nc.psum_tensor("ps_unit_x", [128, UNIT], FP32))
        ps_h = [ctx.enter_context(nc.psum_tensor(f"ps_h{f}", [128, 512], FP32)) for f in range(FE)]
        ps_o = [ctx.enter_context(nc.psum_tensor(f"ps_o{i}", [128, 512], FP32)) for i in range(2)]
        x_loaded, turned, copied = sem("unit_loaded"), sem("unit_turned"), sem("unit_copied")
        h_scores, h_ready = sem("h_scores"), sem("h_ready2")
        o_ready, biased_ready, result_ready = ([sem(f"{n}{i}") for i in range(2)] for n in ("o_ready", "biased_ready", "result_ready"))
        stored = [sem(f"y_stored{i}") for i in range(2)]
        pool_passed = sem("pool_passed2")
        block = ctx.enter_context(nc.Block())

        def over_units(eng, one):
            first = ends[eng]
            for e in range(E):
                with eng.Fori(first[e], first[e + 1]) as n:
                    one(e, n)
            return first[E]


        @block.sync
        def _(sp):
            def load(row):
                for i in range(2):
                    at = slice(row + 128 * i, row + 128 * i + 128) if isinstance(row, int) else bass.ds(row + 128 * i, 128)
                    sp.dma_start(rows[i][:, :], dram["sorted"][at, :]).then_inc(x_loaded, 16)

            first = ends[sp]
            for e in range(E):
                with sp.Fori(0, first[e + 1] - first[e]) as i:
                    sp.wait_ge(copied, first[e] + i + 1)
                    load(i * UNIT + e * REGION)
            sp.wait_ge(copied, first[E] + 1)
            load(0)

        @block.tensor
        def _(pe):
            def turn(n):
                pe.wait_ge(x_loaded, 2 * 16 * (n + 1))
                for i in range(2):
                    last = pe.transpose(ps_x[:, 128 * i:128 * i + 128], rows[i][:, 0:C], res.ident[:, :])
                last.then_inc(turned, 1)

            def one(e, n):
                pe.wait_ge(copied, n + 2)
                for f in range(FE):
                    pe.wait_ge(h_ready, FE * n + f + 1)
                    pe.matmul(ps_h[f][:, 0:UNIT], w1[:, e, 128 * f:128 * f + 128], xT[:, :], start=True, stop=True).then_inc(h_scores, 1)
                turn(n + 1)
                for i in range(2):
                    pe.wait_ge(biased_ready[i], n + 1)
                    for f in range(FE):
                        if i == 0:
                            pe.wait_ge(h_ready, FE * (n + 1) + f + 1)
                        last = pe.matmul(ps_o[i][:, 0:C], hidden[:, f, 128 * i:128 * i + 128], w2[:, e, f, :],
                                         start=(f == 0), stop=(f == FE - 1))
                    last.then_inc(o_ready[i], 1)

            turn(0)
            pe.wait_ge(weights.loaded, weights.LOADS)
            over_units(pe, one)

        @block.scalar
        def _(act):
            act.sem_inc(h_ready, FE)
            act.wait_ge(weights.loaded, weights.LOADS)

            def one(e, n):
                for f in range(FE):
                    act.wait_ge(h_scores, FE * n + f + 1)
                    act.activation(hidden[:, f, :], ps_h[f][:, 0:UNIT], ACT.Gelu, bias=b1[:, e, f:f + 1]).then_inc(h_ready, 1)

            over_units(act, one)

        @block.vector
        def _(dve):
            dve.sem_inc(copied, 1)
            for i in range(2):
                dve.sem_inc(biased_ready[i], 1)
            dve.wait_ge(weights.loaded, weights.LOADS)

            def keep(n):
                dve.wait_ge(turned, n + 1)
                dve.tensor_copy(xT[:, :], ps_x[:, :])
                for i in range(2):
                    at = slice(i, i + 1) if isinstance(n, int) else bass.ds(2 * n + i, 1)
                    last = dve.tensor_copy(tails[:, at, :].rearrange("p a c -> p (a c)"), rows[i][:, C:C + 2])
                last.then_inc(copied, 1)

            def one(e, n):
                keep(n + 1)
                for i in range(2):
                    dve.wait_ge(o_ready[i], n + 1)
                    dve.tensor_tensor(biased[i][:, :], ps_o[i][:, 0:C], b2[:, e, :], ALU.add).then_inc(biased_ready[i], 1)
                    dve.wait_ge(stored[i], 16 * (n + 1))
                    dve.tensor_copy(goes_to[i][:, :], tails[:, bass.ds(2 * n + i, 1), 0:1].rearrange("p a c -> p (a c)"))
                    dve.wait_ge(biased_ready[i], n + 2)
                    dve.tensor_scalar(result[i][:, :], biased[i][:, :], tails[:, bass.ds(2 * n + i, 1), 1:2].rearrange("p a c -> p (a c)"), None, ALU.mult)\
                       .then_inc(result_ready[i], 1)

            keep(0)
            over_units(dve, one)

        @block.gpsimd
        def _(pool):
            for i in range(2):
                pool.dma_start(result[i][:, :], dram["ident"]).then_inc(stored[i], 16)

            def one(e, n):
                for i in range(2):
                    pool.wait_ge(result_ready[i], n + 1)
                    apart(pool, pool_passed)
                    pool.indirect_dma_start(dram["y"], bass.IndirectOffsetOnAxis(goes_to[i][:, 0:1], 0), result[i][:, :], None)\
                        .then_inc(stored[i], 16)

            total = over_units(pool, one)
            for i in range(2):
                pool.wait_ge(stored[i], 16 * total + 16)


def combine(nc, res, dram, s_all):
    with ExitStack() as ctx:
        def sb(name, shape, dt=FP32):
            return ctx.enter_context(nc.sbuf_tensor(name, shape, dt))

        def sem(name):
            return ctx.enter_context(nc.semaphore(name))

        y = [[sb(f"y{k}_{p}", [128, TT, C]) for p in range(2)] for k in range(2)]
        mixed = [sb(f"mixed{p}", [128, TT, C]) for p in range(2)]
        gate, s_gated = ([sb(f"{n}{p}", [128, TT, C]) for p in range(2)] for n in ("tanh_m", "s_gated"))
        out_now = [sb(f"out_now{p}", [128, TT, C]) for p in range(2)]
        mixed_ready, tanh_ready, gate_ready, s_ready, out_ready = (sem(n) for n in ("mixed_ready", "mix_tanh", "mix_gate", "s_gated_ready", "out_ready"))
        pool_passed = sem("pool_passed3")
        y_loaded = [sem(f"y_loaded{p}") for p in range(2)]
        stored = [sem(f"out_stored{p}") for p in range(2)]
        block = ctx.enter_context(nc.Block())

        def tiles(b):
            return slice(TT * b, TT * b + TT) if isinstance(b, int) else bass.ds(TT * b, TT)

        def bodies(eng, one):
            one(0, 0)
            one(1, 1)
            with eng.Fori(1, B // 2) as n:
                one(2 * n, 0)
                one(2 * n + 1, 1)

        @block.sync
        def _(sp):
            y_rows = dram["y"].rearrange("(n p t) c -> p n (t c)", p=128, t=TT)

            def one(b, p):
                if not isinstance(b, int):
                    sp.wait_ge(mixed_ready, b - 1)
                for k in range(2):
                    at = slice(b + k * B, b + k * B + 1) if isinstance(b, int) else bass.ds(b + k * B, 1)
                    sp.dma_start(y[k][p][:, :, :].rearrange("p t c -> p (t c)"), y_rows[:, at, :].rearrange("p a c -> p (a c)")).then_inc(y_loaded[p], 16)

            bodies(sp, one)

        @block.scalar
        def _(act):
            out = dram["out"].rearrange("b (t p) c -> p (b t) c", p=128)

            def tanh(b, p):
                act.wait_ge(mixed_ready, b + 1)
                act.activation(gate[p][:, :, :], mixed[p][:, :, :], ACT.Tanh).then_inc(tanh_ready, 1)

            def store(b, p):
                act.wait_ge(out_ready, b + 1)
                act.dma_start(out[:, tiles(b), :], out_now[p][:, :, :]).then_inc(stored[p], 16)

            tanh(0, 0)
            tanh(1, 1)
            store(0, 0)
            with act.Fori(1, B // 2) as n:
                tanh(2 * n, 0)
                store(2 * n - 1, 1)
                tanh(2 * n + 1, 1)
                store(2 * n, 0)
            store(B - 1, 1)
            for p in range(2):
                act.wait_ge(stored[p], 16 * B // 2)

        @block.vector
        def _(dve):
            def mix(b, p):
                dve.wait_ge(y_loaded[p], 16 * (b - p) + 32)
                if not isinstance(b, int) or b >= 2:
                    dve.wait_ge(gate_ready, b - 1)
                dve.tensor_tensor(mixed[p][:, :, :], y[0][p][:, :, :], y[1][p][:, :, :], ALU.add).then_inc(mixed_ready, 1)

            def gate_s(b, p):
                dve.wait_ge(tanh_ready, b + 1)
                dve.scalar_tensor_tensor(gate[p][:, :, :], gate[p][:, :, :], 1.0, mixed[p][:, :, :], ALU.add, ALU.mult).then_inc(gate_ready, 1)
                dve.wait_ge(gate_ready, b + 1)
                if not isinstance(b, int) or b >= 2:
                    dve.wait_ge(out_ready, b - 1)
                dve.tensor_tensor(s_gated[p][:, :, :], gate[p][:, :, :], s_all[:, tiles(b), :], ALU.mult).then_inc(s_ready, 1)

            mix(0, 0)
            mix(1, 1)
            gate_s(0, 0)
            mix(2, 0)
            gate_s(1, 1)
            mix(3, 1)
            gate_s(2, 0)
            with dve.Fori(2, B // 2) as n:
                mix(2 * n, 0)
                gate_s(2 * n - 1, 1)
                mix(2 * n + 1, 1)
                gate_s(2 * n, 0)
            gate_s(B - 1, 1)

        @block.gpsimd
        def _(pool):
            def one(b, p):
                if not isinstance(b, int) or b >= 2:
                    pool.wait_ge(stored[p], 8 * (b - p))
                pool.wait_ge(s_ready, b + 1)
                apart(pool, pool_passed)
                pool.tensor_tensor(out_now[p][:, :, :], s_gated[p][:, :, :], res.x[:, tiles(b), :], ALU.add).then_inc(out_ready, 1)

            bodies(pool, one)


def laid_out(inputs):
    def t(a, *axes):
        return np.ascontiguousarray(np.transpose(a, axes or None))

    return {
        "x": inputs["L0_attn_x"],
        "wqT": t(inputs["L0_attn_Wq"]), "wkT": t(inputs["L0_attn_Wk"]), "wvT": t(inputs["L0_attn_Wv"]),
        "wpT": t(inputs["L0_attn_Wp"]),
        "bq": inputs["L0_attn_bq"], "bk": inputs["L0_attn_bk"], "bv": inputs["L0_attn_bv"], "bp": inputs["L0_attn_bp"],
        "level": np.reshape(inputs["L0_attn_resolve_level"], (1,)),
        "wgT": t(inputs["L0_ffn_w_gate"]), "wuT": t(inputs["L0_ffn_w_up"]), "wdT": t(inputs["L0_ffn_w_down"]),
        "abT": t(inputs["L1_attn_ab"]), "h0": inputs["L1_attn_h_0"],
        "rwT": t(inputs["L1_ffn_router_w"]),
        "b1T": t(np.reshape(inputs["L1_ffn_b1"], (E, FE, 128)), 2, 0, 1), "b2": inputs["L1_ffn_b2"],
        "w1T": t(inputs["L1_ffn_w1"], 2, 0, 1),
        "w2T": t(np.reshape(inputs["L1_ffn_w2"], (E, C, FE, 128)), 3, 0, 2, 1),
    }


def build(nc, dram):
    fwd, inv, nyq = transform_tables()
    constants = {
        "mask": head_mask(), "ident": np.eye(128, dtype=np.float32), "value_frame": value_frame(),
        "fwd": fwd, "inv": inv, "nyq": nyq,
        "place_tables": place_tables(), "earlier": earlier(),
    }
    for name, value in constants.items():
        dram[name] = nc.inline_tensor(value, f"const_{name}").ap()
    dram["k_pad"] = nc.dram_tensor("k_pad_scratch", [C, KPAD + T], FP32).ap()
    dram["dens"] = nc.dram_tensor("scratch_dens", [H, T], FP32).ap()
    dram["inverses"] = nc.dram_tensor("scratch_inverses", [H, T], FP32).ap()
    dram["sorted"] = nc.dram_tensor("sorted_scratch", [SORTED, ROW], FP32).ap()
    dram["y"] = nc.dram_tensor("y_scratch", [Y_ROWS, C], FP32).ap()
    with ExitStack() as ctx:
        res = Resident(nc, ctx)
        early = RouteTables(nc, ctx)
        layer0(nc, res, dram, lambda sp: early.load(sp, dram))
        s_all = ctx.enter_context(nc.sbuf_tensor("s_all", [128, B * TT, C], FP32))
        weights = ExpertWeights(nc, ctx)
        ends = route_and_convolve(nc, res, dram, s_all, early, weights)
        experts(nc, res, dram, ends, weights)
        combine(nc, res, dram, s_all)


def kernel(**inputs):
    import concourse.bacc as _bacc
    from concourse.bass_utils import run_bass_kernel_spmd as _run

    nc = _bacc.Bacc("TRN2", target_bir_lowering=False, num_devices=1)
    arrays, dram = {}, {}
    for name, value in laid_out({k: np.asarray(v) for k, v in inputs.items()}).items():
        value = np.ascontiguousarray(value)
        arrays[f"in_{name}_dram"] = value
        dram[name] = nc.dram_tensor(f"in_{name}_dram", value.shape, mybir.dt.from_np(value.dtype), kind="ExternalInput").ap()
    dram["out"] = nc.dram_tensor("out_0_dram", (B, T, C), FP32, kind="ExternalOutput").ap()
    build(nc, dram)
    return _run(nc, [arrays], core_ids=[0]).results[0]["out_0_dram"]
```
